# Optimizing a Trainium2 kernel written in Bass

```python
import numpy as np
import jax
import jax.numpy as jnp

def _softmax(x, axis=-1):
    return jax.nn.softmax(x, axis=axis)

def _gelu(x):
    return jax.nn.gelu(x, approximate=True)

def _silu(x):
    return jax.nn.silu(x)

def _sigmoid(x):
    return jax.nn.sigmoid(x)

def _layernorm(x, axis=-1, eps=1e-05):
    m = jnp.mean(x, axis=axis, keepdims=True)
    v = jnp.var(x, axis=axis, keepdims=True)
    return (x - m) / jnp.sqrt(v + eps)

def _scatter_add(tgt, idx, src, axis=0):
    return tgt.at[idx].add(src)

def _segment_sum(src, seg, n):
    return jax.ops.segment_sum(src, seg, n)
kernel_name = 'mk_adj_ffn_d2_adj_r2_2b304d'

def setup_inputs(seed: int=0):
    np.random.seed(seed)
    _w = jnp.asarray

    def _rec_inputs():
        import jax
        import jax.numpy as jnp
        _gk = jax.random.key(seed)
        x = -0.0005207 + 1.001 * jax.random.normal(jax.random.fold_in(_gk, 1), (8192, 128), jnp.float32)
        _a = jax.random.bernoulli(jax.random.fold_in(_gk, 2), 0.000488281, (8192, 8192))
        _a = jnp.logical_or(_a, jnp.swapaxes(_a, -1, -2))
        _a = jnp.logical_or(_a, jnp.eye(8192, dtype=bool))
        adj = _a.astype(jnp.int32)
        return (x, adj)
    x, adj = _rec_inputs()

    def _L0_gnn_setup():
        import jax, jax.numpy as jnp
        import numpy as np
        N = 4096
        D = 128
        NEG_SLOPE = 0.01
        MASK_VAL = -1000000000000.0
        key = jax.random.key(seed)
        k1, k2, k3, k4 = jax.random.split(key, 4)
        x = jax.random.normal(k1, (N, D), dtype=jnp.float32)
        adj = jax.random.randint(k2, (N, N), 0, 2, dtype=jnp.int32)
        W = jax.random.normal(k3, (D, D), dtype=jnp.float32) * (1.0 / np.sqrt(D))
        a = jax.random.normal(k4, (2 * D, 1), dtype=jnp.float32) * (1.0 / np.sqrt(2 * D))
        return {'x': x, 'adj': adj, 'W': W, 'a': a}
    _L0_gnn_all = _L0_gnn_setup()
    _L0_gnn_in = {k: v for k, v in _L0_gnn_all.items() if k in ('W', 'a')}
    del _L0_gnn_all

    def _L0_ffn_setup():
        import jax, jax.numpy as jnp
        import numpy as np
        B, N, D = (16, 2048, 128)
        NUM_EXPERTS, TOP_K, HEADS = (4, 2, 4)
        N_EDGES = 524288
        LN_EPS = 1e-05

        def _layernorm(x, g, b):
            mu = x.mean(-1, keepdims=True)
            var = ((x - mu) ** 2).mean(-1, keepdims=True)
            return (x - mu) * jax.lax.rsqrt(var + LN_EPS) * g + b

        def _forward(x, edge_index, W_gat, att_src, att_dst, b_gat, ln_gamma, ln_beta, W1, b1, W2, b2):
            Bc, Nc, Dc = x.shape
            M = Bc * Nc
            x_flat = x.reshape(M, Dc)
            h = (x_flat @ W_gat).reshape(M, HEADS, NUM_EXPERTS)
            loops = jnp.arange(M, dtype=edge_index.dtype)
            src = jnp.concatenate([edge_index[0], loops])
            dst = jnp.concatenate([edge_index[1], loops])
            a_src = (h * att_src).sum(-1)
            a_dst = (h * att_dst).sum(-1)
            e = jax.nn.leaky_relu(a_src[src] + a_dst[dst], negative_slope=0.2)
            e_max = jax.ops.segment_max(e, dst, num_segments=M)
            ee = jnp.exp(e - e_max[dst])
            denom = jax.ops.segment_sum(ee, dst, num_segments=M)
            alpha = ee / (denom[dst] + 1e-16)
            msg = h[src] * alpha[:, :, None]
            agg = jax.ops.segment_sum(msg, dst, num_segments=M).reshape(M, HEADS * NUM_EXPERTS) + b_gat
            scores = _layernorm(agg, ln_gamma, ln_beta).reshape(M, HEADS, NUM_EXPERTS).mean(1)
            scores = scores.reshape(Bc, Nc, NUM_EXPERTS)
            topk_s, topk_i = jax.lax.top_k(scores, TOP_K)
            w = jax.nn.softmax(topk_s, axis=-1)
            out = jnp.zeros_like(x)
            for ei in range(NUM_EXPERTS):
                g = jnp.where(topk_i == ei, w, 0.0).sum(-1)
                hh = jax.nn.gelu(x @ W1[ei] + b1[ei], approximate=False)
                out = out + g[..., None] * (hh @ W2[ei] + b2[ei])
            return out
        key = jax.random.key(seed)
        ks = jax.random.split(key, 8)
        s = 0.05
        return {'x': jax.random.normal(ks[0], (B, N, D), jnp.float32), 'W_gat': jax.random.normal(ks[1], (D, HEADS * NUM_EXPERTS), jnp.float32) * s, 'att_src': jax.random.normal(ks[2], (HEADS, NUM_EXPERTS), jnp.float32) * s, 'att_dst': jax.random.normal(ks[3], (HEADS, NUM_EXPERTS), jnp.float32) * s, 'b_gat': jnp.zeros((HEADS * NUM_EXPERTS,), jnp.float32), 'ln_gamma': jnp.ones((HEADS * NUM_EXPERTS,), jnp.float32), 'ln_beta': jnp.zeros((HEADS * NUM_EXPERTS,), jnp.float32), 'W1': jax.random.normal(ks[4], (NUM_EXPERTS, D, 2 * D), jnp.float32) * s, 'b1': jnp.zeros((NUM_EXPERTS, 2 * D), jnp.float32), 'W2': jax.random.normal(ks[5], (NUM_EXPERTS, 2 * D, D), jnp.float32) * s, 'b2': jnp.zeros((NUM_EXPERTS, D), jnp.float32), 'edge_index': jax.random.randint(ks[6], (2, N_EDGES), 0, B * N, jnp.int32)}
    _L0_ffn_all = _L0_ffn_setup()
    _L0_ffn_in = {k: v for k, v in _L0_ffn_all.items() if k in ('W_gat', 'att_src', 'att_dst', 'b_gat', 'ln_gamma', 'ln_beta', 'W1', 'b1', 'W2', 'b2', 'edge_index')}
    del _L0_ffn_all

    def _L1_gnn_setup():
        import jax, jax.numpy as jnp
        import numpy as np
        KEEP_RATIO = 0.5
        TEMP = 1.0
        NEG_BIG = -9000000000000000.0
        N_NODE = 4096
        FEA_DIM = 128
        HID_DIM = 128
        key = jax.random.key(seed)
        ks = jax.random.split(key, 7)
        features = jax.random.normal(ks[0], (N_NODE, FEA_DIM), dtype=jnp.float32)
        adj = jax.random.randint(ks[1], (N_NODE, N_NODE), 0, 2, dtype=jnp.int32)
        W1 = jax.random.normal(ks[2], (HID_DIM, FEA_DIM), dtype=jnp.float32) * 0.001
        b1 = jax.random.normal(ks[3], (HID_DIM,), dtype=jnp.float32) * 0.001
        W2 = jax.random.normal(ks[4], (HID_DIM, FEA_DIM), dtype=jnp.float32) * 0.001
        Ww = jax.random.normal(ks[5], (1, HID_DIM), dtype=jnp.float32) * 0.001
        bw = jax.random.normal(ks[6], (1,), dtype=jnp.float32) * 0.001
        return {'features': features, 'adj': adj, 'W1': W1, 'b1': b1, 'W2': W2, 'Ww': Ww, 'bw': bw}
    _L1_gnn_all = _L1_gnn_setup()
    _L1_gnn_in = {k: v for k, v in _L1_gnn_all.items() if k in ('W1', 'b1', 'W2', 'Ww', 'bw')}
    del _L1_gnn_all

    def _L1_ffn_setup():
        import jax, jax.numpy as jnp
        import numpy as np
        N_EXPERTS = 8
        TOP_K = 2
        key = jax.random.key(seed)
        ks = jax.random.split(key, 5)
        B, T, C, E, H = (8, 1024, 128, 8, 341)
        scale = 1.0 / np.sqrt(C)
        return {'x': jax.random.normal(ks[0], (B, T, C), dtype=jnp.float32), 'router_w': jax.random.normal(ks[1], (E, C), dtype=jnp.float32) * scale, 'w1': jax.random.normal(ks[2], (E, H, C), dtype=jnp.float32) * scale, 'w2': jax.random.normal(ks[3], (E, C, H), dtype=jnp.float32) * (1.0 / np.sqrt(H)), 'w3': jax.random.normal(ks[4], (E, H, C), dtype=jnp.float32) * scale}
    _L1_ffn_all = _L1_ffn_setup()
    _L1_ffn_in = {k: v for k, v in _L1_ffn_all.items() if k in ('router_w', 'w1', 'w2', 'w3')}
    del _L1_ffn_all
    return {'x': x, 'adj': adj, 'L0_gnn_W': _L0_gnn_in['W'], 'L0_gnn_a': _L0_gnn_in['a'], 'L0_ffn_W_gat': _L0_ffn_in['W_gat'], 'L0_ffn_att_src': _L0_ffn_in['att_src'], 'L0_ffn_att_dst': _L0_ffn_in['att_dst'], 'L0_ffn_b_gat': _L0_ffn_in['b_gat'], 'L0_ffn_ln_gamma': _L0_ffn_in['ln_gamma'], 'L0_ffn_ln_beta': _L0_ffn_in['ln_beta'], 'L0_ffn_W1': _L0_ffn_in['W1'], 'L0_ffn_b1': _L0_ffn_in['b1'], 'L0_ffn_W2': _L0_ffn_in['W2'], 'L0_ffn_b2': _L0_ffn_in['b2'], 'L0_ffn_edge_index': _L0_ffn_in['edge_index'], 'L1_gnn_W1': _L1_gnn_in['W1'], 'L1_gnn_b1': _L1_gnn_in['b1'], 'L1_gnn_W2': _L1_gnn_in['W2'], 'L1_gnn_Ww': _L1_gnn_in['Ww'], 'L1_gnn_bw': _L1_gnn_in['bw'], 'L1_ffn_router_w': _L1_ffn_in['router_w'], 'L1_ffn_w1': _L1_ffn_in['w1'], 'L1_ffn_w2': _L1_ffn_in['w2'], 'L1_ffn_w3': _L1_ffn_in['w3']}

def reference(x, adj, L0_gnn_W, L0_gnn_a, L0_ffn_W_gat, L0_ffn_att_src, L0_ffn_att_dst, L0_ffn_b_gat, L0_ffn_ln_gamma, L0_ffn_ln_beta, L0_ffn_W1, L0_ffn_b1, L0_ffn_W2, L0_ffn_b2, L0_ffn_edge_index, L1_gnn_W1, L1_gnn_b1, L1_gnn_W2, L1_gnn_Ww, L1_gnn_bw, L1_ffn_router_w, L1_ffn_w1, L1_ffn_w2, L1_ffn_w3):
    import jax
    import jax.numpy as jnp

    def _L0_gnn_ref(x, adj, W, a):
        import jax, jax.numpy as jnp
        import numpy as np
        N = 4096
        D = 128
        NEG_SLOPE = 0.01
        MASK_VAL = -1000000000000.0
        h = x @ W
        e_src = h @ a[:D, 0]
        e_dst = h @ a[D:, 0]
        e = e_src[:, None] + e_dst[None, :]
        e = jnp.where(e > 0, e, NEG_SLOPE * e)
        att_logits = jnp.where(adj > 0, e, MASK_VAL)
        attention = jax.nn.softmax(att_logits, axis=1)
        h_prime = attention @ h
        return jax.nn.elu(h_prime)

    def _L0_ffn_ref(x, W_gat, att_src, att_dst, b_gat, ln_gamma, ln_beta, W1, b1, W2, b2, edge_index):
        import jax, jax.numpy as jnp
        import numpy as np
        B, N, D = (16, 2048, 128)
        NUM_EXPERTS, TOP_K, HEADS = (4, 2, 4)
        N_EDGES = 524288
        LN_EPS = 1e-05

        def _layernorm(x, g, b):
            mu = x.mean(-1, keepdims=True)
            var = ((x - mu) ** 2).mean(-1, keepdims=True)
            return (x - mu) * jax.lax.rsqrt(var + LN_EPS) * g + b

        def _forward(x, edge_index, W_gat, att_src, att_dst, b_gat, ln_gamma, ln_beta, W1, b1, W2, b2):
            Bc, Nc, Dc = x.shape
            M = Bc * Nc
            x_flat = x.reshape(M, Dc)
            h = (x_flat @ W_gat).reshape(M, HEADS, NUM_EXPERTS)
            loops = jnp.arange(M, dtype=edge_index.dtype)
            src = jnp.concatenate([edge_index[0], loops])
            dst = jnp.concatenate([edge_index[1], loops])
            a_src = (h * att_src).sum(-1)
            a_dst = (h * att_dst).sum(-1)
            e = jax.nn.leaky_relu(a_src[src] + a_dst[dst], negative_slope=0.2)
            e_max = jax.ops.segment_max(e, dst, num_segments=M)
            ee = jnp.exp(e - e_max[dst])
            denom = jax.ops.segment_sum(ee, dst, num_segments=M)
            alpha = ee / (denom[dst] + 1e-16)
            msg = h[src] * alpha[:, :, None]
            agg = jax.ops.segment_sum(msg, dst, num_segments=M).reshape(M, HEADS * NUM_EXPERTS) + b_gat
            scores = _layernorm(agg, ln_gamma, ln_beta).reshape(M, HEADS, NUM_EXPERTS).mean(1)
            scores = scores.reshape(Bc, Nc, NUM_EXPERTS)
            topk_s, topk_i = jax.lax.top_k(scores, TOP_K)
            w = jax.nn.softmax(topk_s, axis=-1)
            out = jnp.zeros_like(x)
            for ei in range(NUM_EXPERTS):
                g = jnp.where(topk_i == ei, w, 0.0).sum(-1)
                hh = jax.nn.gelu(x @ W1[ei] + b1[ei], approximate=False)
                out = out + g[..., None] * (hh @ W2[ei] + b2[ei])
            return out
        return _forward(x, edge_index, W_gat, att_src, att_dst, b_gat, ln_gamma, ln_beta, W1, b1, W2, b2)

    def _L1_gnn_ref(features, adj, W1, b1, W2, Ww, bw):
        import jax, jax.numpy as jnp
        import numpy as np
        KEEP_RATIO = 0.5
        TEMP = 1.0
        NEG_BIG = -9000000000000000.0
        N_NODE = 4096
        FEA_DIM = 128
        HID_DIM = 128
        s1 = features @ W1.T + b1
        s2 = features @ W2.T
        w = Ww[0]
        u = s1 @ w + bw[0]
        v = s2 @ w
        raw_att = u[:, None] + v[None, :]
        att = jnp.where(adj > 0, raw_att, NEG_BIG) * TEMP
        att = jax.nn.softmax(att, axis=1)
        prop_fea = att @ features
        adj_num = jnp.sum(adj, axis=1)
        adj_mask = (adj_num > 0).astype(features.dtype)[:, None]
        prop_fea = adj_mask * prop_fea + (1.0 - adj_mask) * features
        out = (1.0 - KEEP_RATIO) * prop_fea + KEEP_RATIO * features
        return out

    def _L1_ffn_ref(x, router_w, w1, w2, w3):
        import jax, jax.numpy as jnp
        import numpy as np
        N_EXPERTS = 8
        TOP_K = 2
        B, T, C = x.shape
        flat = x.reshape(-1, C)
        logits = flat @ router_w.T
        probs = jax.nn.softmax(logits, axis=-1)
        topk_probs, topk_idx = jax.lax.top_k(probs, TOP_K)
        topk_probs = topk_probs / (jnp.sum(topk_probs, axis=-1, keepdims=True) + 1e-09)
        onehot = jax.nn.one_hot(topk_idx, N_EXPERTS, dtype=flat.dtype)
        gates = jnp.einsum('nk,nke->ne', topk_probs, onehot)
        h1 = jnp.einsum('nc,ehc->neh', flat, w1)
        h3 = jnp.einsum('nc,ehc->neh', flat, w3)
        h = jax.nn.silu(h1) * h3
        y = jnp.einsum('neh,ech->nec', h, w2)
        out = jnp.einsum('ne,nec->nc', gates, y)
        return out.reshape(B, T, C)
    x = x + _L0_gnn_ref(_layernorm(x, axis=-1), adj, L0_gnn_W, L0_gnn_a)
    x = x + _L0_ffn_ref(_layernorm(x, axis=-1)[None], L0_ffn_W_gat, L0_ffn_att_src, L0_ffn_att_dst, L0_ffn_b_gat, L0_ffn_ln_gamma, L0_ffn_ln_beta, L0_ffn_W1, L0_ffn_b1, L0_ffn_W2, L0_ffn_b2, L0_ffn_edge_index)[0]
    x = x + _L1_gnn_ref(_layernorm(x, axis=-1), adj, L1_gnn_W1, L1_gnn_b1, L1_gnn_W2, L1_gnn_Ww, L1_gnn_bw)
    x = x + _L1_ffn_ref(_layernorm(x, axis=-1)[None], L1_ffn_router_w, L1_ffn_w1, L1_ffn_w2, L1_ffn_w3)[0]
    return x

_drawn_inputs = setup_inputs


def setup_inputs(seed=0):
    import zlib

    import numpy as np

    out = dict(_drawn_inputs(seed))
    spreads = {'L0_ffn_b_gat': (0.0, 0.1),
     'L0_ffn_ln_gamma': (1.0, 0.2),
     'L0_ffn_ln_beta': (0.0, 0.362),
     'L0_ffn_b1': (0.0, 0.1),
     'L0_ffn_b2': (0.0, 0.1)}
    factors = {'L0_ffn_att_src': 5.641,
     'L0_ffn_att_dst': 7.859,
     'L1_gnn_W1': 64.0,
     'L1_gnn_b1': 64.0,
     'L1_gnn_W2': 64.0,
     'L1_gnn_Ww': 64.0}
    for name, (base, spread) in spreads.items():
        noise = np.random.default_rng([zlib.crc32(name.encode()), seed]).standard_normal(out[name].shape)
        drawn = base * np.exp(spread * noise) if base else spread * noise
        out[name] = jnp.asarray(drawn.astype(out[name].dtype))
    for name, factor in factors.items():
        out[name] = (out[name] * factor).astype(out[name].dtype)
    return out
```

```python
from contextlib import ExitStack

import concourse.bass as bass
from concourse import mybir

ALU = mybir.AluOpType
ACT = mybir.ActivationFunctionType
AX = mybir.AxisListType
F32 = mybir.dt.float32
BF16 = mybir.dt.bfloat16
I32 = mybir.dt.int32
U16 = mybir.dt.uint16

P = 128
BANK = 512
EPS = 1e-5
MASKED = 2.0 ** 40
LOW = 1e30
CW = 2048
CHUNKS = 4
UW = 1024
LEVEL = 60.0


class Chain:

    def __init__(self, eng, sem):
        self.eng, self.sem, self.n = eng, sem, 0

    def __call__(self, ins):
        self.n += 1
        ins.then_inc(self.sem, 1)
        self.eng.wait_ge(self.sem, self.n)


class Phase:

    def __init__(self, nc, tag):
        self.nc, self.tag, self.stack, self.taken = nc, tag, ExitStack(), []

    def __enter__(self):
        self.stack.__enter__()
        return self

    def __exit__(self, *e):
        if self.taken:
            self.nc.clear_and_free_semaphores(self.taken)
            self.nc.all_engine_barrier()
        return self.stack.__exit__(*e)

    def sbuf(self, name, shape, dtype=F32):
        return self.stack.enter_context(self.nc.sbuf_tensor(f"{self.tag}_{name}", shape, dtype))

    def psum(self, name, shape, dtype=F32):
        return self.stack.enter_context(self.nc.psum_tensor(f"{self.tag}_{name}", shape, dtype))

    def sem(self, name):
        sem = self.nc.alloc_semaphore(f"{self.tag}_{name}")
        self.taken.append(sem.num)
        return sem

    def sems(self, *names):
        return [self.sem(n) for n in names]


def norm_rows(nc, dve, step, X, Y, work, small, rsqrt_ready, sqrt_done, width):
    T = X.shape[1]
    mean, var, rstd = small[:, 0, :], small[:, 1, :], small[:, 2, :]
    step(nc.vector.tensor_reduce(mean, X[:], AX.X, ALU.add))
    step(nc.vector.tensor_scalar(mean, mean, 1.0 / width, None, ALU.mult))
    step(nc.vector.tensor_tensor(Y[:], X[:], mean.unsqueeze(2).to_broadcast([P, T, width]), ALU.subtract))
    step(nc.vector.tensor_tensor(work, Y[:], Y[:], ALU.mult))
    step(nc.vector.tensor_reduce(var, work, AX.X, ALU.add))
    step(nc.vector.tensor_scalar(var, var, 1.0 / width, EPS, ALU.mult, ALU.add))
    nc.vector.tensor_copy(rstd, var).then_inc(rsqrt_ready, 1)
    dve.wait_ge(sqrt_done, 1)
    step(nc.vector.reciprocal(rstd, var))
    step(nc.vector.tensor_tensor(Y[:], Y[:], rstd.unsqueeze(2).to_broadcast([P, T, width]), ALU.mult))


def make_identity(nc, ident):
    with Phase(nc, "id") as ph:
        zeroed, made = ph.sems("zeroed", "made")
        with nc.Block() as block:
            @block.gpsimd
            def _(pool):
                nc.gpsimd.memset(ident[:], 0.0).then_inc(zeroed, 1)
                pool.wait_ge(zeroed, 1)
                nc.gpsimd.affine_select(out=ident[:], in_=ident[:], compare_op=ALU.not_equal, fill=1.0, base=0,
                                        pattern=[[-1, P]], channel_multiplier=1).then_inc(made, 1)
                pool.wait_ge(made, 1)


def project_l0(nc, ident, x, W, a, H, drow, d01, scol):
    N, D = x.shape
    T = N // P
    G = T // 4
    with Phase(nc, "pj0") as ph:
        X = ph.sbuf("X", [P, T, D])
        XT = ph.sbuf("XT", [P, T, D])
        Wt = ph.sbuf("W", [P, D])
        WT = ph.sbuf("WT", [P, D])
        a2 = ph.sbuf("a2", [P, 2])
        wa = ph.sbuf("wa", [P, 2])
        wd = ph.sbuf("wd", [P, P])
        small = ph.sbuf("small", [P, 3, T])
        PS = ph.psum("ps", [P, 8, BANK])
        x_in, w_in, var_ok, sqrt_ok, dve_step, xn_ok, wt_ok, wt_out, wa_ok, wa_out = ph.sems(
            "x_in", "w_in", "var_ok", "sqrt_ok", "dve_step", "xn_ok", "wt_ok", "wt_out", "wa_ok", "wa_out")
        xt_ok, xt_out, h_ok, h_out, d_ok, d_out, s_ok, s_out = ph.sems(
            "xt_ok", "xt_out", "h_ok", "h_out", "d_ok", "d_out", "s_ok", "s_out")
        with nc.Block() as block:
            @block.sync
            def _(sp):
                sp.dma_start(Wt[:], W).then_inc(w_in, 16)
                for s in range(2):
                    sp.dma_start(a2[:, s:s + 1], a[s * D:(s + 1) * D, :]).then_inc(w_in, 16)
                xv = x.rearrange("(t p) d -> p t d", p=P)
                for q in range(4):
                    sp.dma_start(X[:, q * T // 4:(q + 1) * T // 4, :], xv[:, q * T // 4:(q + 1) * T // 4, :]).then_inc(x_in, 16)

            @block.vector
            def _(dve):
                step = Chain(dve, dve_step)
                dve.wait_ge(x_in, 64)
                norm_rows(nc, dve, step, X, X, H[:], small, var_ok, sqrt_ok, D)
                nc.vector.tensor_copy(small[:, 2, 0:1], small[:, 1, 0:1]).then_inc(xn_ok, 1)
                dve.wait_ge(wt_ok, 1)
                nc.vector.tensor_copy(WT[:], PS[:, 7, 0:D]).then_inc(wt_out, 1)
                dve.wait_ge(wa_ok, 1)
                step(nc.vector.tensor_copy(wa[:], PS[:, 7, 128:130]))
                nc.vector.tensor_copy(wd[:], wa[:, 1:2].to_broadcast([P, P])).then_inc(wa_out, 1)
                for g in range(G):
                    dve.wait_ge(xt_ok, g + 1)
                    nc.vector.tensor_copy(XT[:, 4 * g:4 * g + 4, :], PS[:, g % 2, :].rearrange("p (t d) -> p t d", t=4)).then_inc(xt_out, 1)
                    dve.wait_ge(h_ok, g + 1)
                    nc.vector.tensor_copy(H[:, 4 * g:4 * g + 4, :], PS[:, 2 + g % 2, :].rearrange("p (t d) -> p t d", t=4)).then_inc(h_out, 1)
                dve.wait_ge(s_ok, 1)
                nc.vector.tensor_copy(scol[:], PS[:, 6, 0:T]).then_inc(s_out, 1)

            @block.scalar
            def _(act):
                act.wait_ge(var_ok, 1)
                nc.scalar.activation(small[:, 1, :], small[:, 2, :], ACT.Sqrt).then_inc(sqrt_ok, 1)
                for g in range(G):
                    act.wait_ge(d_ok, g + 1)
                    nc.scalar.activation(drow[:, BANK * g:BANK * g + BANK], PS[:, 4 + g % 2, :], ACT.Copy).then_inc(d_out, 1)
                    nc.scalar.activation(d01[:, BANK * g:BANK * g + BANK], PS[:, 4 + g % 2, :], ACT.Copy, scale=0.01).then_inc(d_out, 1)

            @block.tensor
            def _(pe):
                pe.wait_ge(w_in, 48)
                nc.tensor.transpose(PS[:, 7, 0:D], Wt[:], ident[:]).then_inc(wt_ok, 1)
                pe.wait_ge(wt_out, 1)
                nc.tensor.matmul(PS[:, 7, 128:130], WT[:], a2[:], start=True, stop=True).then_inc(wa_ok, 1)
                pe.wait_ge(xn_ok, 1)
                pe.wait_ge(wa_out, 1)
                for g in range(G):
                    if g >= 2:
                        pe.wait_ge(xt_out, g - 1)
                    for k in range(4):
                        ins = nc.tensor.transpose(PS[:, g % 2, k * P:(k + 1) * P], X[:, 4 * g + k, :], ident[:])
                    ins.then_inc(xt_ok, 1)
                    if g >= 2:
                        pe.wait_ge(h_out, g - 1)
                        pe.wait_ge(d_out, 2 * (g - 1))
                    pe.wait_ge(xt_out, g + 1)
                    for k in range(4):
                        nc.tensor.matmul(PS[:, 6, 4 * g + k:4 * g + k + 1], XT[:, 4 * g + k, :], wa[:, 0:1], start=True, stop=True)
                        ins = nc.tensor.matmul(PS[:, 2 + g % 2, k * P:(k + 1) * P], XT[:, 4 * g + k, :], Wt[:], start=True, stop=True)
                    ins.then_inc(h_ok, 1)
                    ins = nc.tensor.matmul(PS[:, 4 + g % 2, :], wd[:], XT[:, 4 * g:4 * g + 4, :], start=True, stop=True)
                    ins.then_inc(d_ok, 1)
                    if g == G - 1:
                        nc.tensor.matmul(PS[:, 7, 256:257], XT[:, 0, :], wa[:, 0:1], start=True, stop=True).then_inc(s_ok, 1)


def project_edges(nc, ident, x, hp, X, W_gat, att_src, att_dst, XT, tab):
    N, D = x.shape
    T = N // P
    G = T // 4
    HE = W_gat.shape[1]
    NH, NE = att_src.shape
    with Phase(nc, "pj1") as ph:
        Y = ph.sbuf("Y", [P, T, D])
        E = ph.sbuf("E", [P, T, D])
        Wg = ph.sbuf("Wg", [P, HE])
        att = ph.sbuf("att", [P, 2, HE])
        rows = ph.sbuf("rows", [P, T, HE + 2 * NH])
        prod = ph.sbuf("prod", [P, T, HE])
        small = ph.sbuf("small", [P, 3, T])
        PS = ph.psum("ps", [P, 4, BANK])
        x_in, w_in, neg_ok, exp_ok, var_ok, sqrt_ok, dve_step, y_ok = ph.sems(
            "x_in", "w_in", "neg_ok", "exp_ok", "var_ok", "sqrt_ok", "dve_step", "y_ok")
        xt_ok, xt_out, h_ok, tab_ok, tab_out = ph.sems("xt_ok", "xt_out", "h_ok", "tab_ok", "tab_out")
        with nc.Block() as block:
            @block.sync
            def _(sp):
                sp.dma_start(X[:], x.rearrange("(t p) d -> p t d", p=P)).then_inc(x_in, 16)
                sp.dma_start(Y[:], hp.rearrange("(t p) d -> p t d", p=P)).then_inc(x_in, 16)
                sp.dma_start(Wg[:], W_gat).then_inc(w_in, 16)
                for k, v in enumerate((att_src, att_dst)):
                    sp.dma_start(att[:, k, :], v.rearrange("(o h) e -> o (h e)", o=1).to_broadcast([P, HE])).then_inc(w_in, 16)
                sp.wait_ge(tab_ok, 1)
                sp.dma_start(tab.rearrange("(t p) c -> p t c", p=P), rows[:]).then_inc(tab_out, 16)
                sp.wait_ge(tab_out, 16)

            @block.vector
            def _(dve):
                step = Chain(dve, dve_step)
                dve.wait_ge(x_in, 32)
                nc.vector.tensor_scalar(E[:], Y[:], 0.0, None, ALU.min).then_inc(neg_ok, 1)
                step(nc.vector.scalar_tensor_tensor(out=X[:], in0=Y[:], scalar=0.0, in1=X[:], op0=ALU.max, op1=ALU.add))
                dve.wait_ge(exp_ok, 1)
                step(nc.vector.scalar_tensor_tensor(out=X[:], in0=E[:], scalar=-1.0, in1=X[:], op0=ALU.add, op1=ALU.add))
                norm_rows(nc, dve, step, X, Y, E[:], small, var_ok, sqrt_ok, D)
                dve.sem_inc(y_ok, 1)
                for g in range(G):
                    if g % 2:
                        dve.wait_ge(xt_ok, g + 1)
                        nc.vector.tensor_copy(XT[:, 4 * g:4 * g + 4, :], PS[:, g % 2, :].rearrange("p (t d) -> p t d", t=4)).then_inc(xt_out, 1)
                dve.wait_ge(h_ok, 1)
                hrow = PS[:, 2:4, :].rearrange("p b c -> p (b c)")
                nc.vector.tensor_copy(rows[:, :, 0:HE], hrow.rearrange("p (t c) -> p t c", t=T))
                dve.wait_ge(w_in, 48)
                for k in range(2):
                    step(nc.vector.tensor_tensor(prod[:], hrow.rearrange("p (t c) -> p t c", t=T),
                                                 att[:, k, :].unsqueeze(1).to_broadcast([P, T, HE]), ALU.mult))
                    step(nc.vector.tensor_reduce(rows[:, :, HE + k * NH:HE + (k + 1) * NH],
                                                 prod[:].rearrange("p t (h e) -> p t h e", h=NH), AX.X, ALU.add))
                dve.sem_inc(tab_ok, 1)

            @block.scalar
            def _(act):
                act.wait_ge(neg_ok, 1)
                nc.scalar.activation(E[:], E[:], ACT.Exp).then_inc(exp_ok, 1)
                act.wait_ge(var_ok, 1)
                nc.scalar.activation(small[:, 1, :], small[:, 2, :], ACT.Sqrt).then_inc(sqrt_ok, 1)
                for g in range(0, G, 2):
                    act.wait_ge(xt_ok, g + 1)
                    nc.scalar.copy(XT[:, 4 * g:4 * g + 4, :], PS[:, g % 2, :].rearrange("p (t d) -> p t d", t=4)).then_inc(exp_ok, 1)

            @block.tensor
            def _(pe):
                pe.wait_ge(y_ok, 1)
                pe.wait_ge(w_in, 48)

                def turned(g):
                    if g % 2:
                        pe.wait_ge(xt_out, g // 2 + 1)
                    else:
                        pe.wait_ge(exp_ok, g // 2 + 2)

                def project(g):
                    for t in range(4 * g, 4 * g + 4):
                        o = t * HE
                        ins = nc.tensor.matmul(PS[:, 2 + o // BANK, o % BANK:o % BANK + HE], XT[:, t, :], Wg[:], start=True, stop=True)
                    return ins

                for g in range(G):
                    if g >= 2:
                        turned(g - 2)
                    for k in range(4):
                        ins = nc.tensor.transpose(PS[:, g % 2, k * P:(k + 1) * P], Y[:, 4 * g + k, :], ident[:])
                    ins.then_inc(xt_ok, 1)
                    if g:
                        turned(g - 1)
                        project(g - 1)
                turned(G - 1)
                project(G - 1).then_inc(h_ok, 1)


def split_rows(nc, step, pos, rows_per, inv_rows, neg_rows, gap, q_int, rest, flip, q_out, idx_out):
    step(nc.vector.tensor_scalar(q_int, pos, inv_rows, None, ALU.mult))
    step(nc.vector.scalar_tensor_tensor(out=rest, in0=q_int, scalar=neg_rows, in1=pos, op0=ALU.mult, op1=ALU.add))
    step(nc.vector.scalar_tensor_tensor(out=flip, in0=rest, scalar=0.0, in1=q_int, op0=ALU.is_lt, op1=ALU.subtract))
    step(nc.vector.scalar_tensor_tensor(out=q_out, in0=rest, scalar=rows_per, in1=flip, op0=ALU.is_ge, op1=ALU.subtract))
    return nc.vector.scalar_tensor_tensor(out=idx_out, in0=q_out, scalar=gap, in1=pos, op0=ALU.mult, op1=ALU.add)


def sort_edges(nc, ident, edge_index, N, rec, plan, self_idx, self_rec, ctl, endi, endq, cont):
    E = edge_index.shape[1]
    CE = E // P
    NF = N // P
    GC = 8
    LMAX = rec.shape[0] // P
    CHUNK = 128
    TRASH = 2 * N
    FAR = float(1 << 22)
    LOGF = NF.bit_length() - 1
    assert 1 << LOGF == NF and N % (P * NF) == 0
    with Phase(nc, "sort") as ph:
        dstF = ph.sbuf("dstF", [P, CE + GC])
        partB = ph.sbuf("partB", [P, CE + GC], BF16)
        offB = ph.sbuf("offB", [P, CE + GC], BF16)
        both = ph.sbuf("both", [P, CE + GC, 2], I32)
        iotaF = ph.sbuf("iotaF", [P, P], BF16)
        tri = ph.sbuf("tri", [P, P])
        before = ph.sbuf("before", [P, P])
        ones = ph.sbuf("ones", [P, P])
        Lc = ph.sbuf("Lc", [P, 4])
        cnt = ph.sbuf("cnt", [P, 1])
        start1 = ph.sbuf("start1", [P, NF])

        with Phase(nc, "pack") as pk:
            src = pk.sbuf("src", [P, CE], I32)
            V = [pk.sbuf(f"V{k}", [P, CE]) for k in range(2)]
            S = [pk.sbuf(f"S{k}", [P, CE], I32) for k in range(2)]
            M = pk.sbuf("M", [P, CE], I32)
            iota = pk.sbuf("iota", [P, CE])
            scr = pk.sbuf("scr", [P, 6])
            scri = pk.sbuf("scri", [P, 4], I32)
            PS = pk.psum("ps", [P, 2, BANK])
            e_in, made, z_ok, step_p, dve_step, cnt_ok, tot_ok, fill_ok, fill_out = pk.sems(
                "e_in", "made", "z_ok", "step_p", "dve_step", "cnt_ok", "tot_ok", "fill_ok", "fill_out")
            dst = M
            t1 = iota
            with nc.Block() as block:
                @block.sync
                def _(sp):
                    ev = edge_index.rearrange("k (p c) -> k p c", p=P)
                    sp.dma_start(src[:], ev[0]).then_inc(e_in, 16)
                    sp.dma_start(dst[:], ev[1]).then_inc(e_in, 16)
                    sp.wait_ge(fill_ok, 1)
                    rv = rec.rearrange("(p a t) c -> a p (t c)", p=P, a=4)
                    for q in range(4):
                        sp.dma_start(rv[q], both[:, 0:LMAX // 4, :]).then_inc(fill_out, 16)
                    sp.wait_ge(fill_out, 64)

                @block.gpsimd
                def _(pool):
                    c = [0]

                    def link(ins):
                        c[0] += 1
                        ins.then_inc(step_p, 1)
                        pool.wait_ge(step_p, c[0])

                    link(nc.gpsimd.iota(iotaF[:], pattern=[[1, P]], base=0, channel_multiplier=0,
                                        allow_small_or_imprecise_dtypes=True))
                    link(nc.gpsimd.memset(ones[:], 1.0))
                    for m, mult in ((tri, 1), (before, -1)):
                        link(nc.gpsimd.affine_select(out=m[:], in_=ones[:], compare_op=ALU.is_gt, fill=0.0, base=0,
                                                     pattern=[[mult, P]], channel_multiplier=-mult))
                    link(nc.gpsimd.iota(self_rec[:], pattern=[[1, NF], [0, 2]], base=0, channel_multiplier=NF))
                    nc.gpsimd.memset(ones[:], 1.0).then_inc(made, 1)
                    pool.wait_ge(z_ok, 1)
                    nc.gpsimd.iota(iota[:], pattern=[[1, CE]], base=0, channel_multiplier=0,
                                   allow_small_or_imprecise_dtypes=True).then_inc(made, 1)

                @block.vector
                def _(dve):
                    step = Chain(dve, dve_step)
                    half = [v[:].bitcast(U16).rearrange("p (c k) -> p c k", k=2) for v in V]
                    step(nc.vector.memset(both[:, 0:LMAX // 4, 0], N))
                    step(nc.vector.memset(both[:, 0:LMAX // 4, 1], 0))
                    dve.sem_inc(fill_ok, 1)
                    dve.wait_ge(e_in, 32)
                    step(nc.vector.tensor_scalar(t1[:], src[:], 0.0, float(N), ALU.is_lt, ALU.mult))
                    step(nc.vector.tensor_tensor(t1[:], t1[:], src[:], ALU.add))
                    step(nc.vector.tensor_scalar(half[0][:, :, 0], t1[:], 0.0, float(N - 1), ALU.max, ALU.min))
                    step(nc.vector.tensor_scalar(t1[:], dst[:], 0.0, float(N), ALU.is_lt, ALU.mult))
                    step(nc.vector.tensor_tensor(t1[:], t1[:], dst[:], ALU.add))
                    inv, run = V[1], dstF[:, 0:CE]
                    step(nc.vector.tensor_scalar(inv[:], t1[:], 0.0, None, ALU.is_ge))
                    step(nc.vector.scalar_tensor_tensor(out=inv[:], in0=t1[:], scalar=float(N - 1), in1=inv[:], op0=ALU.is_le, op1=ALU.mult))
                    step(nc.vector.tensor_scalar(t1[:], t1[:], 0.0, float(N - 1), ALU.max, ALU.min))
                    step(nc.vector.tensor_scalar(half[0][:, :, 1], t1[:], 16384.0, None, ALU.add))
                    step(nc.vector.tensor_scalar(t1[:], inv[:], -1.0, 1.0, ALU.mult, ALU.add))
                    step(nc.vector.tensor_tensor_scan(run, t1[:], t1[:], 0.0, ALU.add, ALU.max))
                    step(nc.vector.tensor_scalar(cnt[:], dstF[:, CE - 1:CE], -1.0, float(CE), ALU.mult, ALU.add))
                    dve.sem_inc(cnt_ok, 1)
                    step(nc.vector.tensor_tensor(S[0][:], run, inv[:], ALU.mult))
                    a = 0
                    for k in range(CE.bit_length() - 1):
                        far, b = 1 << k, 1 - a
                        step(nc.vector.tensor_scalar(M[:], S[a][:], far, None, ALU.bitwise_and))
                        step(nc.vector.scalar_tensor_tensor(out=S[b][:], in0=M[:], scalar=0.0, in1=S[a][:], op0=ALU.is_equal, op1=ALU.mult))
                        step(nc.vector.copy_predicated(S[b][:, 0:CE - far], M[:, far:CE], S[a][:, far:CE]))
                        step(nc.vector.tensor_copy(V[b][:], V[a][:]))
                        step(nc.vector.copy_predicated(V[b][:, 0:CE - far], M[:, far:CE], V[a][:, far:CE]))
                        a = b
                    dve.sem_inc(z_ok, 1)
                    dve.wait_ge(made, 2)
                    step(nc.vector.tensor_scalar(iota[:], iota[:], cnt[:], float(TRASH), ALU.is_ge, ALU.mult))
                    step(nc.vector.tensor_scalar(V[1 - a][:], half[a][:, :, 1], -16384.0, None, ALU.add))
                    step(nc.vector.tensor_tensor(dstF[:, 0:CE], V[1 - a][:], iota[:], ALU.max))
                    step(nc.vector.memset(dstF[:, CE:CE + GC], float(TRASH)))
                    step(nc.vector.tensor_copy(S[0][:], dstF[:, 0:CE]))
                    dve.wait_ge(fill_out, 64)
                    step(nc.vector.memset(both[:, CE:CE + GC, :], 0))
                    step(nc.vector.tensor_copy(both[:, 0:CE, 0], dstF[:, 0:CE]))
                    step(nc.vector.tensor_copy(both[:, 0:CE, 1], half[a][:, :, 0]))
                    step(nc.vector.tensor_scalar(M[:], S[0][:], LOGF, None, ALU.arith_shift_right))
                    step(nc.vector.tensor_copy(partB[:, 0:CE], M[:]))
                    step(nc.vector.memset(partB[:, CE:CE + GC], float(TRASH // NF)))
                    step(nc.vector.tensor_scalar(M[:], S[0][:], NF - 1, None, ALU.bitwise_and))
                    step(nc.vector.tensor_copy(offB[:, 0:CE], M[:]))
                    step(nc.vector.memset(offB[:, CE:CE + GC], 0.0))
                    dve.wait_ge(tot_ok, 1)
                    step(nc.vector.tensor_scalar(scr[:, 1:2], PS[:, 0, 0:1], float(N + P * CHUNK - 1), None, ALU.add))
                    step(nc.vector.tensor_copy(scri[:, 0:1], scr[:, 1:2]))
                    step(nc.vector.tensor_scalar(scri[:, 1:2], scri[:, 0:1], (P * CHUNK).bit_length() - 1, None, ALU.arith_shift_right))
                    step(nc.vector.tensor_scalar(Lc[:, 0:1], scri[:, 1:2], float(CHUNK), None, ALU.mult))
                    step(nc.vector.reciprocal(Lc[:, 1:2], Lc[:, 0:1]))
                    step(nc.vector.tensor_scalar(Lc[:, 2:3], Lc[:, 0:1], -1.0, None, ALU.mult))
                    step(nc.vector.tensor_scalar(Lc[:, 3:4], Lc[:, 0:1], -1.0, float(LMAX), ALU.mult, ALU.add))
                    step(nc.vector.tensor_copy(ctl[0:1, 1:2], scri[0:1, 1:2]))
                    step(nc.vector.tensor_scalar(ctl[0:1, 2:3], scri[0:1, 1:2], -1.0, float(LMAX // CHUNK), ALU.mult, ALU.add))
                    step(nc.vector.tensor_reduce(scr[0:1, 2:3], PS[0:1, 1, 0:P], AX.X, ALU.max))
                    step(nc.vector.tensor_scalar(scr[0:1, 3:4], scr[0:1, 2:3], 1.0, float(2 * GC - 1), ALU.max, ALU.add))
                    step(nc.vector.tensor_copy(scri[0:1, 2:3], scr[0:1, 3:4]))
                    step(nc.vector.tensor_scalar(ctl[0:1, 0:1], scri[0:1, 2:3], (2 * GC).bit_length() - 1, None, ALU.arith_shift_right))

                @block.tensor
                def _(pe):
                    pe.wait_ge(cnt_ok, 1)
                    pe.wait_ge(made, 1)
                    nc.tensor.matmul(PS[:, 0, 0:1], ones[:], cnt[:], start=True, stop=True)
                    nc.tensor.transpose(PS[0:1, 1, 0:P], cnt[:], ident[:]).then_inc(tot_ok, 1)

        with Phase(nc, "count") as pc:
            OF = [pc.sbuf(f"OF{k}", [P, GC, NF], BF16) for k in range(2)]
            OP = [pc.sbuf(f"OP{k}", [P, GC, P], BF16) for k in range(2)]
            w = pc.sbuf("w", [P, 8, NF])
            wi = pc.sbuf("wi", [P, NF], I32)
            tot = pc.sbuf("tot", [P, 2])
            zero = pc.sbuf("zero", [P, P], BF16)
            HIST = pc.psum("hist", [P, BANK])
            BASE = pc.psum("base", [P, BANK])
            hot, counted, hist_ok, tot_ok, base_ok, dve_step, zero_ok = pc.sems(
                "hot", "counted", "hist_ok", "tot_ok", "base_ok", "dve_step", "zero_ok")
            with nc.Block() as block:
                @block.vector
                def _(dve):
                    groups = dve.value_load(ctl[0:1, 0:1], min_val=1, max_val=CE // (2 * GC))
                    nc.vector.memset(zero[:], 0.0).then_inc(zero_ok, 1)
                    with dve.Fori(0, groups) as i:
                        for b in range(2):
                            dve.wait_ge(counted, 2 * i + b + 1)
                            cols = bass.ds((2 * i + b) * GC, GC)
                            one_hots(nc, OF[b], OP[b], iotaF, offB[:, cols], partB[:, cols], NF, GC)[1].then_inc(hot, 1)
                    dve.wait_ge(hist_ok, 1)
                    step = Chain(dve, dve_step)
                    c1, incl, start, last = w[:, 0, :], w[:, 1, :], w[:, 2, :], w[:, 3, :]
                    step(nc.vector.tensor_scalar(c1, HIST[:, 0:NF], 1.0, None, ALU.add))
                    step(nc.vector.tensor_reduce(tot[:, 0:1], c1, AX.X, ALU.add))
                    dve.sem_inc(tot_ok, 1)
                    dve.wait_ge(base_ok, 1)
                    step(nc.vector.tensor_copy(tot[:, 1:2], BASE[:, 0:1]))
                    step(nc.vector.tensor_tensor_scan(incl, c1, c1, tot[:, 1:2], ALU.add, ALU.max))
                    step(nc.vector.tensor_tensor(start, incl, c1, ALU.subtract))
                    step(nc.vector.tensor_scalar(start1[:], start, 1.0, None, ALU.add))
                    step(nc.vector.tensor_scalar(last, incl, -1.0, None, ALU.add))
                    step(split_rows(nc, step, start, Lc[:, 0:1], Lc[:, 1:2], Lc[:, 2:3], Lc[:, 3:4], wi[:], w[:, 4, :], w[:, 5, :], w[:, 6, :], self_idx[:]))
                    step(split_rows(nc, step, last, Lc[:, 0:1], Lc[:, 1:2], Lc[:, 2:3], Lc[:, 3:4], wi[:], w[:, 4, :], w[:, 5, :], w[:, 6, :], endi[:]))
                    step(nc.vector.tensor_copy(endq[:], w[:, 6, :]))
                    step(nc.vector.scalar_tensor_tensor(out=w[:, 7, :], in0=w[:, 6, :], scalar=Lc[:, 2:3], in1=start, op0=ALU.mult, op1=ALU.add))
                    step(nc.vector.tensor_scalar(cont[:], w[:, 7, :], 0.0, None, ALU.is_lt))

                @block.tensor
                def _(pe):
                    groups = pe.value_load(ctl[0:1, 0:1], min_val=1, max_val=CE // (2 * GC))
                    pe.wait_ge(zero_ok, 1)
                    nc.tensor.matmul(HIST[:, 0:NF], zero[:], zero[:, 0:NF], start=True, stop=False, skip_group_check=True).then_inc(counted, 2)
                    with pe.Fori(0, groups) as i:
                        for b in range(2):
                            pe.wait_ge(hot, 2 * i + b + 1)
                            for c in range(GC):
                                ins = nc.tensor.matmul(HIST[:, 0:NF], OP[b][:, c, :], OF[b][:, c, :], start=False, stop=False, skip_group_check=True)
                            ins.then_inc(counted, 1)
                    nc.tensor.matmul(HIST[:, 0:NF], zero[:], zero[:, 0:NF], start=False, stop=True, skip_group_check=True).then_inc(hist_ok, 1)
                    pe.wait_ge(tot_ok, 1)
                    nc.tensor.matmul(BASE[:, 0:1], tri[:], tot[:, 0:1], start=True, stop=True).then_inc(base_ok, 1)

        with Phase(nc, "place") as pp:
            OF = [pp.sbuf(f"OF{k}", [P, GC, NF], BF16) for k in range(2)]
            OP = [pp.sbuf(f"OP{k}", [P, GC, P], BF16) for k in range(2)]
            OPT = [pp.sbuf(f"OPT{k}", [P, GC, P]) for k in range(2)]
            HS = [pp.sbuf(f"HS{k}", [P, NF]) for k in range(2)]
            dcol = [pp.sbuf(f"dcol{k}", [P, GC]) for k in range(2)]
            recs = [pp.sbuf(f"recs{k}", [P, GC, 3], I32) for k in range(2)]
            hit = pp.sbuf("hit", [P, GC, P])
            pick = pp.sbuf("pick", [P, GC, NF])
            rank = pp.sbuf("rank", [P, 2, GC])
            sel = pp.sbuf("sel", [P, 2, GC])
            m = pp.sbuf("m", [P, 5, GC])
            mi = pp.sbuf("mi", [P, GC], I32)
            identB = pp.sbuf("identB", [P, P], BF16)
            TB = pp.psum("tb", [P, GC * P], BF16)
            DD = [pp.psum(f"dd{k}", [P, GC * P]) for k in range(2)]
            LK = [pp.psum(f"lk{k}", [P, GC, NF]) for k in range(2)]
            HR = pp.psum("hr", [P, BANK])
            hot, ttd, optd, ddd, hcopy, hupd, looked, placed, dve_step, id_ok = pp.sems(
                "hot", "ttd", "optd", "ddd", "hcopy", "hupd", "looked", "placed", "dve_step", "id_ok")
            plan_out = [pp.sem("plan_out0"), pp.sem("plan_out1")]
            passed, past_out = pp.sems("passed", "past_out")
            STEPS = 1 + GC + GC + 7
            with nc.Block() as block:
                @block.sync
                def _(sp):
                    groups = sp.value_load(ctl[0:1, 0:1], min_val=1, max_val=CE // (2 * GC))
                    with sp.Fori(0, groups) as i:
                        for b in range(2):
                            sp.wait_ge(placed, 2 * i + b + 1)
                            sp.sem_inc(passed, 1)
                            sp.dma_start(plan[:, bass.ds((2 * i + b) * GC, GC), :], recs[b][:]).then_inc(plan_out[b], 16)
                    sp.dma_start(plan[:, bass.ds(groups * (2 * GC), GC), :], recs[0][:]).then_inc(past_out, 16)
                    planned = sp.snap(groups * 16 + 1)
                    for b in range(2):
                        sp.wait_ge(plan_out[b], planned)
                        sp.sem_inc(passed, 1)
                    sp.wait_ge(past_out, 16)

                @block.vector
                def _(dve):
                    groups = dve.value_load(ctl[0:1, 0:1], min_val=1, max_val=CE // (2 * GC))
                    nc.vector.tensor_copy(identB[:], ident[:]).then_inc(id_ok, 1)
                    dve.sem_inc(dve_step, 1)
                    for b in range(2):
                        dve.sem_inc(plan_out[b], 1)

                    def build(g, b):
                        cols = bass.ds(g * GC, GC)
                        one_hots(nc, OF[b], OP[b], iotaF, offB[:, cols], partB[:, cols], NF, GC)
                        nc.vector.tensor_copy(dcol[b][:], dstF[:, cols]).then_inc(hot, 1)

                    def consume(step, g, i, b):
                        cols = bass.ds(g * GC, GC)
                        dve.wait_ge(plan_out[b], i * 16 + 1)
                        step(nc.vector.tensor_copy(recs[b][:, :, 0:2], both[:, cols, :]))
                        dve.wait_ge(ddd, g + 1)
                        for c in range(GC):
                            a = step(nc.vector.scalar_tensor_tensor(
                                out=hit[:, c, :], in0=DD[b][:, c * P:(c + 1) * P], scalar=dcol[b][:, c:c + 1], in1=before[:],
                                op0=ALU.is_equal, op1=ALU.mult, accum_out=rank[:, b, c:c + 1]))
                        dve.wait_ge(looked, (g + 1) * GC)
                        for c in range(GC):
                            a = step(nc.vector.tensor_tensor_reduce(pick[:, c, :], LK[b][:, c, :], OF[b][:, c, :], 1.0, 0.0,
                                                                    ALU.mult, ALU.add, sel[:, b, c:c + 1]))
                        step.eng.wait_ge(dve_step, a)
                        step.now(nc.vector.tensor_tensor(m[:, 0, :], sel[:, b, :], rank[:, b, :], ALU.add))
                        step.now(nc.vector.tensor_scalar(m[:, 1, :], dcol[b][:], float(N), FAR, ALU.is_ge, ALU.mult))
                        step.now(nc.vector.tensor_tensor(m[:, 0, :], m[:, 0, :], m[:, 1, :], ALU.add))
                        split_rows(nc, step.now, m[:, 0, :], Lc[:, 0:1], Lc[:, 1:2], Lc[:, 2:3], Lc[:, 3:4], mi[:],
                                   m[:, 2, :], m[:, 3, :], m[:, 4, :], recs[b][:, :, 2]).then_inc(placed, 1)

                    build(0, 0)
                    with dve.Fori(0, groups) as i:
                        step = LoopSteps(dve, dve_step, i * (2 * STEPS) + 1)
                        for b in range(2):
                            g = 2 * i + b
                            dve.wait_ge(hupd, g * GC + 1)
                            dve.wait_ge(dve_step, g * STEPS + 1)
                            build(g + 1, 1 - b)
                            consume(step, g, i, b)
                        assert step.n == 2 * STEPS, step.n

                @block.scalar
                def _(act):
                    groups = act.value_load(ctl[0:1, 0:1], min_val=1, max_val=CE // (2 * GC))
                    act.sem_inc(optd, 1)
                    with act.Fori(0, groups) as i:
                        for b in range(2):
                            g = 2 * i + b
                            act.wait_ge(ttd, g + 1)
                            nc.scalar.copy(OPT[b][:].rearrange("p c e -> p (c e)"), TB[:]).then_inc(optd, 1)
                            for c in range(GC):
                                act.wait_ge(hupd, g * GC + c + 1)
                                nc.scalar.copy(HS[c % 2][:], HR[:, 0:NF]).then_inc(hcopy, 1)

                @block.tensor
                def _(pe):
                    groups = pe.value_load(ctl[0:1, 0:1], min_val=1, max_val=CE // (2 * GC))
                    pe.wait_ge(id_ok, 1)
                    nc.tensor.matmul(HR[:, 0:NF], ident[:], start1[:], start=True, stop=False, skip_group_check=True).then_inc(hupd, 1)
                    with pe.Fori(0, groups) as i:
                        for b in range(2):
                            g = 2 * i + b
                            pe.wait_ge(hot, g + 1)
                            pe.wait_ge(optd, g + 1)
                            for c in range(GC):
                                ins = nc.tensor.transpose(TB[:, c * P:(c + 1) * P], OP[b][:, c, :], identB[:])
                            ins.then_inc(ttd, 1)
                            for c in range(GC):
                                ins = nc.tensor.matmul(DD[b][:, c * P:(c + 1) * P], dcol[b][:, c:c + 1].to_broadcast([P, P]),
                                                       ident[:], start=True, stop=True)
                            ins.then_inc(ddd, 1)
                            pe.wait_ge(optd, g + 2)
                            for c in range(GC):
                                pe.wait_ge(hcopy, g * GC + c + 1)
                                nc.tensor.matmul(HR[:, 0:NF], OP[b][:, c, :], OF[b][:, c, :], start=False, stop=False,
                                                 skip_group_check=True).then_inc(hupd, 1)
                                nc.tensor.matmul(LK[b][:, c, :], OPT[b][:, c, :], HS[c % 2][:], start=True, stop=True).then_inc(looked, 1)


def scatter_records(nc, pool, ph, rec, plan, self_idx, self_rec, ctl):
    NF = self_idx.shape[1]
    QC, NQ = 4, 4
    GROUP = QC * NQ
    LAST = rec.shape[0] - 1
    SELF = 16 * (NF // NQ)
    part = [ph.sbuf(f"plan{q}", [P, QC, 3], I32) for q in range(NQ)]
    part_in = [ph.sem(f"part_in{q}") for q in range(NQ)]
    scat = [ph.sem(f"scat{q}") for q in range(NQ)]
    passed = ph.sem("scat_passed")
    groups = pool.value_load(ctl[0:1, 0:1], min_val=1, max_val=(plan.shape[1] - GROUP) // GROUP)
    for f in range(NF):
        pool.indirect_dma_start(rec, bass.IndirectOffsetOnAxis(ap=self_idx[:, f:f + 1], axis=0),
                                self_rec[:, f, :], None).then_inc(scat[f % NQ], 16)
    for q in range(2):
        pool.dma_start(part[q][:], plan[:, q * QC:(q + 1) * QC, :]).then_inc(part_in[q], 16)
    with pool.Fori(0, groups) as i:
        for q in range(NQ):
            pool.wait_ge(part_in[q], i * 16 + 16)
            pool.sem_inc(passed, 1)
            for c in range(QC):
                pool.indirect_dma_start(rec, bass.IndirectOffsetOnAxis(ap=part[q][:, c, 2:3], axis=0),
                                        part[q][:, c, 0:2], None, bounds_check=LAST, oob_is_err=False).then_inc(scat[q], 16)
            n = (q + 2) % NQ
            pool.wait_ge(scat[n], i * (16 * QC) + (SELF if q < 2 else SELF + 16 * QC))
            pool.sem_inc(passed, 1)
            pool.dma_start(part[n][:], plan[:, bass.ds(i * GROUP + (q + 2) * QC, QC), :]).then_inc(part_in[n], 16)
    scattered = pool.snap(groups * (16 * QC) + SELF)
    loaded = pool.snap(groups * 16 + 16)
    for q in range(NQ):
        pool.wait_ge(scat[q], scattered)
        pool.sem_inc(passed, 1)
    for q in range(2):
        pool.wait_ge(part_in[q], loaded)
        pool.sem_inc(passed, 1)


def one_hots(nc, off_hot, part_hot, iota, off, part, NF, GC):
    return (nc.vector.tensor_tensor(off_hot[:], iota[:, 0:NF].unsqueeze(1).to_broadcast([P, GC, NF]),
                                    off.unsqueeze(2).to_broadcast([P, GC, NF]), ALU.is_equal),
            nc.vector.tensor_tensor(part_hot[:], iota[:].unsqueeze(1).to_broadcast([P, GC, P]),
                                    part.unsqueeze(2).to_broadcast([P, GC, P]), ALU.is_equal))


def top_two(nc, step, score, left, sel, best, free):
    NE = score.shape[2]
    T = score.shape[1]
    src = score
    for k in range(2):
        step(nc.vector.tensor_reduce(best[:, k, :], src, AX.X, ALU.max))
        step(nc.vector.tensor_tensor(sel[k], src, best[:, k, :].unsqueeze(2).to_broadcast([P, T, NE]), ALU.is_equal))
        step(nc.vector.memset(free, 1.0))
        for e in range(NE):
            step(nc.vector.tensor_tensor(sel[k][:, :, e], sel[k][:, :, e], free, ALU.mult))
            if e < NE - 1:
                step(nc.vector.tensor_tensor(free, free, sel[k][:, :, e], ALU.subtract))
        if k == 0:
            step(nc.vector.scalar_tensor_tensor(out=left, in0=sel[0], scalar=-LOW, in1=score, op0=ALU.mult, op1=ALU.add))
            src = left


def gate_nodes(nc, ident, rec, tab, runs, carry, ctl, endi, endq, cont, b_gat, ln_gamma, ln_beta, gates):
    N, TW = tab.shape
    NE = gates.shape[1]
    HE = b_gat.shape[0]
    NH = HE // NE
    NF = N // P
    S = NH + HE
    W = NH + S
    LMAX = rec.shape[0] // P
    CK = 64
    rv = rec.rearrange("(p t) c -> p t c", p=P)
    nv = runs.rearrange("(p t) c -> p t c", p=P)
    with Phase(nc, "gat") as ph:
        state = ph.sbuf("state", [P, W])
        lastd = ph.sbuf("lastd", [P, 1])
        with Phase(nc, "runs") as pr:
            RC = [pr.sbuf(f"RC{k}", [P, CK, 2], I32) for k in range(2)]
            GT = [pr.sbuf(f"GT{k}", [P, CK, TW]) for k in range(2)]
            RN = [pr.sbuf(f"RN{k}", [P, CK + 1, W]) for k in range(2)]
            HOLD = [pr.sbuf(f"HOLD{k}", [P, CK + 1, NH]) for k in range(2)]
            DF = [pr.sbuf(f"DF{k}", [P, CK + 1]) for k in range(2)]
            flag = pr.sbuf("flag", [P, 3, CK])
            own = pr.sbuf("own", [P, CK, NH])
            lg = pr.sbuf("lg", [P, CK, NH])
            ex = pr.sbuf("ex", [P, 2, CK, NH])
            wt = pr.sbuf("wt", [P, CK, HE])
            first = pr.sbuf("first", [P, 2], I32)
            firsti = pr.sbuf("firsti", [P, 1], I32)
            firstg = pr.sbuf("firstg", [P, 2, TW])
            zeros = pr.sbuf("zeros", [P, 2 * CK, W])
            first_in, firsti_ok, rc_read, dve_step, ex_ok, exp_ok, run_ok = pr.sems(
                "first_in", "firsti_ok", "rc_read", "dve_step", "ex_ok", "exp_ok", "run_ok")
            passed, fill_ok, fill_out = pr.sems("passed", "fill_ok", "fill_out")
            rc_in = [pr.sem(f"rc_in{k}") for k in range(2)]
            gt_in = [pr.sem(f"gt_in{k}") for k in range(2)]
            rn_out = [pr.sem(f"rn_out{k}") for k in range(2)]
            START, STEPS = 6, 12 + 3 * NH + HE
            with nc.Block() as block:
                @block.sync
                def _(sp):
                    pairs = sp.value_load(ctl[0:1, 1:2], min_val=1, max_val=LMAX // (2 * CK) - 1)
                    sp.dma_start(first[:], rv[:, 0, :]).then_inc(first_in, 16)
                    with sp.Fori(0, pairs) as i:
                        for b in range(2):
                            k = 2 * i + b
                            sp.wait_ge(gt_in[b], i * (16 * CK) + 16)
                            sp.sem_inc(passed, 1)
                            sp.wait_ge(rc_read, k + 1)
                            sp.sem_inc(passed, 1)
                            sp.dma_start(RC[b][:], rv[:, bass.ds(k * CK, CK), :]).then_inc(rc_in[b], 16)
                    rest = sp.value_load(ctl[0:1, 2:3], min_val=1, max_val=LMAX // (2 * CK))
                    filled = sp.snap(rest * 16)
                    sp.wait_ge(fill_ok, 1)
                    with sp.Fori(pairs, LMAX // (2 * CK)) as i:
                        sp.dma_start(nv[:, bass.ds(i * (2 * CK), 2 * CK), :], zeros[:]).then_inc(fill_out, 16)
                    sp.wait_ge(fill_out, filled)
                    sp.sem_inc(passed, 1)

                @block.gpsimd
                def _(pool):
                    pairs = pool.value_load(ctl[0:1, 1:2], min_val=1, max_val=LMAX // (2 * CK) - 1)
                    nc.gpsimd.memset(zeros[:], 0.0).then_inc(fill_ok, 1)
                    pool.wait_ge(firsti_ok, 1)
                    for b in range(2):
                        pool.indirect_dma_start(firstg[:, b, :], None, tab, bass.IndirectOffsetOnAxis(ap=firsti[:], axis=0)).then_inc(gt_in[b], 16)
                    with pool.Fori(0, pairs) as i:
                        for b in range(2):
                            k = 2 * i + b
                            pool.wait_ge(run_ok, k + 1)
                            pool.wait_ge(rc_in[b], i * 16 + 16)
                            pool.sem_inc(passed, 1)
                            for c in range(CK):
                                pool.indirect_dma_start(GT[b][:, c, :], None, tab,
                                                        bass.IndirectOffsetOnAxis(ap=RC[b][:, c, 1:2], axis=0)).then_inc(gt_in[b], 16)

                @block.vector
                def _(dve):
                    pairs = dve.value_load(ctl[0:1, 1:2], min_val=1, max_val=LMAX // (2 * CK) - 1)
                    step = LoopSteps(dve, dve_step)
                    dve.wait_ge(first_in, 16)
                    step.now(nc.vector.tensor_scalar(firsti[:], first[:, 0:1], float(N - 1), None, ALU.min))
                    nc.vector.memset(RN[1][:, CK, 0:NH], -LOW).then_inc(firsti_ok, 1)
                    step(nc.vector.memset(RN[1][:, CK, NH:W], 0.0))
                    step(nc.vector.tensor_copy(DF[1][:, CK:CK + 1], first[:, 0:1]))
                    step(nc.vector.memset(flag[:], 0.0))
                    dve.wait_ge(gt_in[0], 16)
                    step(nc.vector.tensor_copy(HOLD[1][:, CK, :], firstg[:, 0, HE + NH:TW]))
                    step.now(nc.vector.memset(own[:], 0.0))
                    nc.vector.memset(lg[:], 0.0).then_inc(rc_read, 2)
                    nc.vector.memset(ex[:], 0.0).then_inc(run_ok, 2)
                    for b in range(2):
                        dve.sem_inc(rn_out[b], 1)
                    assert step.n == START
                    with dve.Fori(0, pairs) as i:
                        step = LoopSteps(dve, dve_step, START + i * (2 * STEPS))
                        now = step.now
                        for b in range(2):
                            k = 2 * i + b
                            dve.wait_ge(rc_in[b], i * 16 + 16)
                            dve.wait_ge(rn_out[b], i * 16 + 1)
                            nc.vector.tensor_copy(DF[b][:, 1:CK + 1], RC[b][:, :, 0]).then_inc(rc_read, 1)
                            step(nc.vector.tensor_copy(DF[b][:, 0:1], DF[1 - b][:, CK:CK + 1]))
                            now(nc.vector.tensor_copy(RN[b][:, 0, :], RN[1 - b][:, CK, :]))
                            now(nc.vector.tensor_tensor(flag[:, 0, :], DF[b][:, 1:CK + 1], DF[b][:, 0:CK], ALU.not_equal))
                            step(nc.vector.tensor_scalar(flag[:, 1, :], flag[:, 0, :], -1.0, 1.0, ALU.mult, ALU.add))
                            step(nc.vector.tensor_scalar(flag[:, 2, :], flag[:, 0, :], -LOW, None, ALU.mult))
                            dve.wait_ge(gt_in[b], i * (16 * CK) + 16 * CK + 16)
                            now(nc.vector.tensor_tensor(own[:], GT[b][:, :, HE + NH:TW],
                                                        flag[:, 0, :].unsqueeze(2).to_broadcast([P, CK, NH]), ALU.mult))
                            for h in range(NH):
                                a = step(nc.vector.tensor_tensor_scan(HOLD[b][:, 1:CK + 1, h], flag[:, 1, :], own[:, :, h],
                                                                      HOLD[1 - b][:, CK, h:h + 1], ALU.mult, ALU.add))
                            dve.wait_ge(dve_step, a)
                            now(nc.vector.tensor_tensor(own[:], GT[b][:, :, HE:HE + NH], HOLD[b][:, 1:CK + 1, :], ALU.add))
                            now(nc.vector.scalar_tensor_tensor(out=lg[:], in0=own[:], scalar=0.2, in1=own[:], op0=ALU.mult, op1=ALU.max))
                            for h in range(NH):
                                a = step(nc.vector.tensor_tensor_scan(RN[b][:, 1:CK + 1, h], flag[:, 2, :], lg[:, :, h],
                                                                      RN[1 - b][:, CK, h:h + 1], ALU.add, ALU.max))
                            dve.wait_ge(dve_step, a)
                            step(nc.vector.tensor_tensor(ex[:, 0, :, :], lg[:], RN[b][:, 1:CK + 1, 0:NH], ALU.subtract))
                            now(nc.vector.tensor_tensor(ex[:, 1, :, :], RN[b][:, 0:CK, 0:NH],
                                                        flag[:, 2, :].unsqueeze(2).to_broadcast([P, CK, NH]), ALU.add))
                            now(nc.vector.tensor_tensor(ex[:, 1, :, :], ex[:, 1, :, :], RN[b][:, 1:CK + 1, 0:NH], ALU.subtract))
                            dve.sem_inc(ex_ok, 1)
                            dve.wait_ge(exp_ok, k + 1)
                            now(nc.vector.tensor_tensor(wt[:].rearrange("p c (h e) -> p c h e", h=NH),
                                                        GT[b][:, :, 0:HE].rearrange("p c (h e) -> p c h e", h=NH),
                                                        ex[:, 0, :, :].unsqueeze(3).to_broadcast([P, CK, NH, NE]), ALU.mult))
                            for c in range(S):
                                h = c if c < NH else (c - NH) // NE
                                new = ex[:, 0, :, h] if c < NH else wt[:, :, c - NH]
                                ins = nc.vector.tensor_tensor_scan(RN[b][:, 1:CK + 1, NH + c], ex[:, 1, :, h], new,
                                                                   RN[1 - b][:, CK, NH + c:NH + c + 1], ALU.mult, ALU.add)
                                a = step(ins)
                            dve.wait_ge(dve_step, a)
                            dve.sem_inc(run_ok, 1)
                        assert step.n == 2 * STEPS, step.n
                    nc.vector.tensor_copy(state[:], RN[1][:, CK, :])
                    nc.vector.tensor_copy(lastd[:], DF[1][:, CK:CK + 1])

                @block.scalar
                def _(act):
                    pairs = act.value_load(ctl[0:1, 1:2], min_val=1, max_val=LMAX // (2 * CK) - 1)
                    stored = act.snap(pairs * 16 + 1)
                    with act.Fori(0, pairs) as i:
                        for b in range(2):
                            k = 2 * i + b
                            act.wait_ge(ex_ok, k + 1)
                            nc.scalar.activation(ex[:], ex[:], ACT.Exp).then_inc(exp_ok, 1)
                            act.wait_ge(run_ok, k + 3)
                            act.dma_start(nv[:, bass.ds(k * CK, CK), :], RN[b][:, 1:CK + 1, :]).then_inc(rn_out[b], 16)
                    for b in range(2):
                        act.wait_ge(rn_out[b], stored)
                        act.sem_inc(passed, 1)

        RE = ph.sbuf("RE", [P, NF, W])
        CE = ph.sbuf("CE", [P, NF, 2 * S])
        with Phase(nc, "carry") as pc:
            ends = pc.sbuf("ends", [P, 3, S])
            turned = pc.sbuf("turned", [S, 3, P])
            pen = pc.sbuf("pen", [S, P])
            MC = pc.sbuf("MC", [S, P + 1])
            VC = pc.sbuf("VC", [S, P + 1])
            ex = pc.sbuf("ex", [S, 2, P])
            back = pc.sbuf("back", [P, 2 * S])
            PS = pc.psum("ps", [P, 2, BANK])
            dve_step, ends_ok, turned_ok, ex_ok, exp_ok, handed_ok, back_ok, back_sb, carry_out, run_in, carry_in = pc.sems(
                "dve_step", "ends_ok", "turned_ok", "ex_ok", "exp_ok", "handed_ok", "back_ok", "back_sb", "carry_out", "run_in", "carry_in")
            with nc.Block() as block:
                @block.vector
                def _(dve):
                    step = Chain(dve, dve_step)
                    step(nc.vector.tensor_copy(ends[:, 0, 0:NH], state[:, 0:NH]))
                    step(nc.vector.tensor_copy(ends[:, 0, NH:S].rearrange("p (h e) -> p h e", h=NH),
                                               state[:, 0:NH].unsqueeze(2).to_broadcast([P, NH, NE])))
                    step(nc.vector.tensor_copy(ends[:, 1, :], state[:, NH:W]))
                    step(nc.vector.tensor_copy(ends[:, 2, :], lastd[:].to_broadcast([P, S])))
                    nc.vector.memset(pen[:, 0:1], -LOW).then_inc(ends_ok, 1)
                    dve.wait_ge(turned_ok, 1)
                    step(nc.vector.tensor_copy(turned[:], PS[0:S, 0, 0:3 * P].rearrange("p (k m) -> p k m", k=3)))
                    m, v, d = turned[:, 0, :], turned[:, 1, :], turned[:, 2, :]
                    step(nc.vector.tensor_tensor(pen[:, 1:P], d[:, 1:P], d[:, 0:P - 1], ALU.not_equal))
                    step(nc.vector.tensor_scalar(pen[:, 1:P], pen[:, 1:P], -LOW, None, ALU.mult))
                    step(nc.vector.memset(MC[:, 0:1], -LOW))
                    step(nc.vector.memset(VC[:, 0:1], 0.0))
                    step(nc.vector.tensor_tensor_scan(MC[:, 1:P + 1], pen[:], m, MC[:, 0:1], ALU.add, ALU.max))
                    step(nc.vector.tensor_tensor(ex[:, 0, :], m, MC[:, 1:P + 1], ALU.subtract))
                    step(nc.vector.tensor_tensor(ex[:, 1, :], MC[:, 0:P], pen[:], ALU.add))
                    step(nc.vector.tensor_tensor(ex[:, 1, :], ex[:, 1, :], MC[:, 1:P + 1], ALU.subtract))
                    dve.sem_inc(ex_ok, 1)
                    dve.wait_ge(exp_ok, 1)
                    step(nc.vector.tensor_tensor(ex[:, 0, :], ex[:, 0, :], v, ALU.mult))
                    nc.vector.tensor_tensor_scan(VC[:, 1:P + 1], ex[:, 1, :], ex[:, 0, :], 0.0, ALU.mult, ALU.add).then_inc(handed_ok, 1)
                    dve.wait_ge(back_ok, 1)
                    nc.vector.tensor_copy(back[:], PS[:, 1, 0:2 * S]).then_inc(back_sb, 1)

                @block.scalar
                def _(act):
                    act.wait_ge(ex_ok, 1)
                    nc.scalar.activation(ex[:], ex[:], ACT.Exp).then_inc(exp_ok, 1)

                @block.tensor
                def _(pe):
                    pe.wait_ge(ends_ok, 1)
                    for k in range(3):
                        ins = nc.tensor.transpose(PS[0:S, 0, k * P:(k + 1) * P], ends[:, k, :], ident[:])
                    ins.then_inc(turned_ok, 1)
                    pe.wait_ge(handed_ok, 1)
                    nc.tensor.transpose(PS[:, 1, 0:S], MC[:, 0:P], ident[0:S, 0:S])
                    nc.tensor.transpose(PS[:, 1, S:2 * S], VC[:, 0:P], ident[0:S, 0:S]).then_inc(back_ok, 1)

                @block.sync
                def _(sp):
                    sp.wait_ge(back_sb, 1)
                    sp.dma_start(carry, back[:]).then_inc(carry_out, 16)
                    sp.wait_ge(carry_out, 16)

                @block.gpsimd
                def _(pool):
                    for f in range(NF):
                        pool.indirect_dma_start(RE[:, f, :], None, runs, bass.IndirectOffsetOnAxis(ap=endi[:, f:f + 1], axis=0)).then_inc(run_in, 16)
                    pool.wait_ge(carry_out, 16)
                    for f in range(NF):
                        pool.indirect_dma_start(CE[:, f, :], None, carry, bass.IndirectOffsetOnAxis(ap=endq[:, f:f + 1], axis=0)).then_inc(carry_in, 16)
                    pool.wait_ge(run_in, 16 * NF)
                    pool.wait_ge(carry_in, 16 * NF)

        with Phase(nc, "node") as pn:
            par = pn.sbuf("par", [P, 3, HE])
            cm = pn.sbuf("cm", [P, NF, NH])
            mm = pn.sbuf("mm", [P, NF, NH])
            ex = pn.sbuf("ex", [P, 2, NF, NH])
            sm = pn.sbuf("sm", [P, NF, NH])
            agg = pn.sbuf("agg", [P, NF, HE])
            tmp = pn.sbuf("tmp", [P, NF, HE])
            small = pn.sbuf("small", [P, 3, NF])
            sc = pn.sbuf("sc", [P, NF, NE])
            left = pn.sbuf("left", [P, NF, NE])
            sel = [pn.sbuf(f"sel{k}", [P, NF, NE]) for k in range(2)]
            best = pn.sbuf("best", [P, 2, NF])
            free = pn.sbuf("free", [P, NF])
            g2 = pn.sbuf("g2", [P, 2, NF])
            par_in, dve_step, ex_ok, exp_ok, var_ok, sqrt_ok, top_ok, top_exp, gates_ok, gates_out = pn.sems(
                "par_in", "dve_step", "ex_ok", "exp_ok", "var_ok", "sqrt_ok", "top_ok", "top_exp", "gates_ok", "gates_out")
            with nc.Block() as block:
                @block.sync
                def _(sp):
                    for k, v in enumerate((b_gat, ln_gamma, ln_beta)):
                        sp.dma_start(par[:, k, :], v.rearrange("(o c) -> o c", o=1).to_broadcast([P, HE])).then_inc(par_in, 16)
                    sp.wait_ge(gates_ok, 1)
                    sp.dma_start(gates.rearrange("(p f) e -> p f e", p=P), sc[:]).then_inc(gates_out, 16)
                    sp.wait_ge(gates_out, 16)

                @block.vector
                def _(dve):
                    step = Chain(dve, dve_step)

                    def heads(x):
                        return x.rearrange("p f (h e) -> p f h e", h=NH)

                    def over(x):
                        return x.unsqueeze(3).to_broadcast([P, NF, NH, NE])

                    def row(k):
                        return par[:, k, :].unsqueeze(1).to_broadcast([P, NF, HE])

                    step(nc.vector.tensor_scalar(free[:], cont[:], LOW, -LOW, ALU.mult, ALU.add))
                    step(nc.vector.tensor_tensor(cm[:], CE[:, :, 0:NH], free[:].unsqueeze(2).to_broadcast([P, NF, NH]), ALU.add))
                    step(nc.vector.tensor_tensor(mm[:], RE[:, :, 0:NH], cm[:], ALU.max))
                    step(nc.vector.tensor_tensor(ex[:, 0], RE[:, :, 0:NH], mm[:], ALU.subtract))
                    step(nc.vector.tensor_tensor(ex[:, 1], cm[:], mm[:], ALU.subtract))
                    dve.sem_inc(ex_ok, 1)
                    dve.wait_ge(exp_ok, 1)
                    step(nc.vector.tensor_tensor(sm[:], RE[:, :, NH:2 * NH], ex[:, 0], ALU.mult))
                    step(nc.vector.tensor_tensor(cm[:], CE[:, :, S:S + NH], ex[:, 1], ALU.mult))
                    step(nc.vector.tensor_tensor(sm[:], sm[:], cm[:], ALU.add))
                    step(nc.vector.tensor_scalar(sm[:], sm[:], 1e-16, None, ALU.add))
                    step(nc.vector.reciprocal(sm[:], sm[:]))
                    step(nc.vector.tensor_tensor(heads(agg[:]), heads(RE[:, :, 2 * NH:W]), over(ex[:, 0]), ALU.mult))
                    step(nc.vector.tensor_tensor(heads(tmp[:]), heads(CE[:, :, S + NH:2 * S]), over(ex[:, 1]), ALU.mult))
                    step(nc.vector.tensor_tensor(agg[:], agg[:], tmp[:], ALU.add))
                    step(nc.vector.tensor_tensor(heads(agg[:]), heads(agg[:]), over(sm[:]), ALU.mult))
                    dve.wait_ge(par_in, 48)
                    step(nc.vector.tensor_tensor(agg[:], agg[:], row(0), ALU.add))
                    norm_rows(nc, dve, step, agg, agg, tmp[:], small, var_ok, sqrt_ok, HE)
                    step(nc.vector.tensor_tensor(agg[:], agg[:], row(1), ALU.mult))
                    step(nc.vector.tensor_tensor(agg[:], agg[:], row(2), ALU.add))
                    step(nc.vector.tensor_reduce(sc[:], agg[:].rearrange("p f (h e) -> p f e h", h=NH), AX.X, ALU.add))
                    step(nc.vector.tensor_scalar(sc[:], sc[:], 1.0 / NH, None, ALU.mult))
                    top_two(nc, step, sc[:], left[:], [sel[0][:], sel[1][:]], best, free[:])
                    nc.vector.tensor_tensor(g2[:, 1, :], best[:, 1, :], best[:, 0, :], ALU.subtract).then_inc(top_ok, 1)
                    dve.wait_ge(top_exp, 1)
                    step(nc.vector.tensor_scalar(g2[:, 0, :], g2[:, 1, :], 1.0, None, ALU.add))
                    step(nc.vector.reciprocal(g2[:, 0, :], g2[:, 0, :]))
                    step(nc.vector.tensor_tensor(g2[:, 1, :], g2[:, 1, :], g2[:, 0, :], ALU.mult))
                    for k in range(2):
                        step(nc.vector.tensor_tensor(sel[k][:], sel[k][:], g2[:, k, :].unsqueeze(2).to_broadcast([P, NF, NE]), ALU.mult))
                    nc.vector.tensor_tensor(sc[:], sel[0][:], sel[1][:], ALU.add).then_inc(gates_ok, 1)

                @block.scalar
                def _(act):
                    act.wait_ge(ex_ok, 1)
                    nc.scalar.activation(ex[:], ex[:], ACT.Exp).then_inc(exp_ok, 1)
                    act.wait_ge(var_ok, 1)
                    nc.scalar.activation(small[:, 1, :], small[:, 2, :], ACT.Sqrt).then_inc(sqrt_ok, 1)
                    act.wait_ge(top_ok, 1)
                    nc.scalar.activation(g2[:, 1, :], g2[:, 1, :], ACT.Exp).then_inc(top_exp, 1)


MOST_LEVELS = 1 << 20


class LoopSteps:

    def __init__(self, eng, sem, base=0):
        self.eng, self.sem, self.base, self.n = eng, sem, base, 0

    def __call__(self, ins):
        self.n += 1
        ins.then_inc(self.sem, 1)
        return self.base + self.n

    def now(self, ins):
        self.eng.wait_ge(self.sem, self(ins))


def attend(nc, tag, ident, adj, maskrow, H, drow, d01, scol, out, anyrow=None, beside=None):
    first = d01 is not None
    N, D = out.shape
    T = N // P
    C = N // CW
    UPC = CW // UW
    U = N // UW
    BPU = UW // P
    ON_DVE = [u in DVE_UNITS[first] for u in range(U)]
    share = {True: sum(ON_DVE), False: U - sum(ON_DVE)}
    place = [sum(1 for v in range(u) if ON_DVE[v] == ON_DVE[u]) for u in range(U)]
    with Phase(nc, tag) as ph:
        AD = [ph.sbuf(f"adj{c}", [P, CW], I32) for c in range(C)] if first else None
        MB = [ph.sbuf(f"mask{c}", [P, CW], BF16) for c in range(C)]
        MD = [ph.sbuf(f"logit{c}", [P, CW]) for c in range(C)]
        PB = [ph.sbuf(f"prob{c}", [P, CW]) for c in range(2)]
        PT = [ph.sbuf(f"probT{c}", [P, UW]) for c in range(2)]
        mx = ph.sbuf("mx", [P, 2, C])
        sums = ph.sbuf("sums", [P, 2, C])
        passed = ph.sem("passed")
        st = ph.sbuf("st", [P, 2, 5])
        hp = ph.sbuf("hp", [P, 2, D])
        TP = [ph.psum(f"tp{c}", [P, UW]) for c in range(2)]
        OUT = ph.psum("out", [P, 2, BANK])
        in_c = [ph.sem(f"in{c}") for c in range(C)]
        store_c = [ph.sem(f"store{c}") for c in range(C)]
        conv, logit, bias_ok, expd, turned, unit_mm, hp_ok, dve_step = ph.sems(
            "conv", "logit", "bias_ok", "expd", "turned", "unit_mm", "hp_ok", "dve_step")
        moved = {True: ph.sem("moved_dve"), False: ph.sem("moved_act")}
        hp_out = [ph.sem("hp_out0"), ph.sem("hp_out1")]
        adj_t = adj.rearrange("(t p) (c w) -> t p c w", p=P, w=CW) if first else None
        mask_t = maskrow.rearrange("(t p) (c w) -> t p c w", p=P, w=CW)
        out_t = out.rearrange("(t p) d -> t p d", p=P)

        def wait_moved(eng, t, u):
            eng.wait_ge(moved[ON_DVE[u]], t * share[ON_DVE[u]] + place[u] + 1)

        def move(eng, copy, t, u):
            eng.wait_ge(turned, t * U + u + 1)
            if not (isinstance(t, int) and t * U + u < 2):
                eng.wait_ge(unit_mm, t * U + u - 1)
            copy(PT[u % 2][:], TP[u % 2][:]).then_inc(moved[ON_DVE[u]], 1)

        def move_share(eng, copy, on_dve, t, c):
            for u in range(c * UPC, (c + 1) * UPC):
                if ON_DVE[u] == on_dve:
                    move(eng, copy, t, u)

        with nc.Block() as block:
            @block.sync
            def _(sp):
                def load(t):
                    for c in range(C):
                        if not (isinstance(t, int) and t == 0):
                            sp.wait_ge(conv if first else logit, (t - 1) * C + c + 1)
                            sp.sem_inc(passed, 1)
                            sp.dma_start(mask_t[t - 1, :, c, :], MB[c][:]).then_inc(store_c[c], 16)
                        if first:
                            sp.dma_start(AD[c][:], adj_t[t, :, c, :]).then_inc(in_c[c], 16)
                        else:
                            sp.dma_start(MB[c][:], mask_t[t, :, c, :]).then_inc(in_c[c], 16)

                def store(t, h):
                    sp.wait_ge(hp_ok, t + 1)
                    sp.dma_start(out_t[t], hp[:, h, :]).then_inc(hp_out[h], 16)

                for t in range(4):
                    load(t)
                with sp.Fori(2, T // 2) as i:
                    for h in range(2):
                        load(2 * i + h)
                        store(2 * i + h - 4, h)
                for c in range(C):
                    sp.wait_ge(conv, (T - 1) * C + c + 1)
                    sp.dma_start(mask_t[T - 1, :, c, :], MB[c][:]).then_inc(store_c[c], 16)
                for t in range(T - 4, T):
                    store(t, t % 2)
                for c in range(C):
                    sp.wait_ge(store_c[c], 16 * T)
                for h in range(2):
                    sp.wait_ge(hp_out[h], 16 * (T // 2))

            @block.gpsimd
            def _(pool):
                beside(pool, ph)

            @block.vector
            def _(dve):
                def logits(step, t, h, c, has_exp, between):
                    if has_exp:
                        dve.wait_ge(expd, (t - 1) * C + c + 1)
                    if first:
                        z = step(nc.vector.scalar_tensor_tensor(
                            out=MD[c][:], in0=drow[:, CW * c:CW * c + CW], scalar=st[:, h, 0:1],
                            in1=d01[:, CW * c:CW * c + CW], op0=ALU.add, op1=ALU.max))
                        between()
                        dve.wait_ge(conv, t * C + c + 1)
                        dve.wait_ge(dve_step, z)
                        src = MD[c][:]
                    else:
                        between()
                        dve.wait_ge(in_c[c], t * 16 + 16)
                        src = drow[:, CW * c:CW * c + CW]
                    dve.sem_inc(passed, 1)
                    nc.vector.tensor_tensor_reduce(MD[c][:], src, MB[c][:], 1.0, -3e38, ALU.add, ALU.max,
                                                   mx[:, h, c:c + 1]).then_inc(logit, 1)

                def bias(step, t, h):
                    dve.wait_ge(logit, (t + 1) * C)
                    step.now(nc.vector.tensor_reduce(st[:, h, 1:2], mx[:, h, :], AX.X, ALU.max))
                    if first:
                        nc.vector.tensor_scalar(st[:, h, 4:5], st[:, h, 1:2], -1.0, None, ALU.mult).then_inc(bias_ok, 1)
                    else:
                        step(nc.vector.tensor_scalar(anyrow[:, bass.ds(t, 1)], st[:, h, 1:2], -0.5 * MASKED, None, ALU.is_gt))
                        step.now(nc.vector.tensor_tensor(st[:, h, 0:1], st[:, h, 1:2], scol[:, bass.ds(t, 1)], ALU.add))
                        nc.vector.scalar_tensor_tensor(out=st[:, h, 4:5], in0=st[:, h, 0:1], scalar=-1.0,
                                                       in1=scol[:, bass.ds(t, 1)], op0=ALU.mult, op1=ALU.add).then_inc(bias_ok, 1)

                def finish(step, t, h, waits_out):
                    dve.wait_ge(expd, (t + 1) * C)
                    step.now(nc.vector.tensor_reduce(st[:, h, 2:3], sums[:, h, :], AX.X, ALU.add))
                    step.now(nc.vector.reciprocal(st[:, h, 3:4], st[:, h, 2:3]))
                    dve.wait_ge(unit_mm, (t + 1) * U)
                    if waits_out is not None:
                        dve.wait_ge(hp_out[h], waits_out)
                    nc.vector.tensor_scalar(hp[:, h, :], OUT[:, h, 0:D], st[:, h, 3:4], None, ALU.mult).then_inc(hp_ok, 1)

                def tile_step(step, t, h, has_logits, out_wait):
                    known = isinstance(t, int)
                    for c in range(C):
                        def between():
                            if not known or t >= 2 or (t == 1 and c >= 1):
                                if c == 0:
                                    move_share(dve, nc.vector.tensor_copy, True, t - 2, C - 1)
                                else:
                                    move_share(dve, nc.vector.tensor_copy, True, t - 1, c - 1)
                        if c == 0 and first and has_logits:
                            step.now(nc.vector.tensor_scalar(st[:, h, 0:1], scol[:, bass.ds(t, 1)], 0.99, None, ALU.mult))
                        if has_logits:
                            logits(step, t, h, c, not known or t >= 1, between)
                        else:
                            between()
                        if c == 1 and (not known or t >= 2):
                            finish(step, t - 2, h, out_wait)
                    if has_logits:
                        bias(step, t, h)

                step = LoopSteps(dve, dve_step)
                for t in range(2):
                    tile_step(step, t, t, True, None)
                for t in range(2, 4):
                    tile_step(step, t, t % 2, True, None)
                n0 = step.n
                per = n0
                with dve.Fori(2, T // 2) as i:
                    per = LOOP_STEPS[first]
                    step = LoopSteps(dve, dve_step, n0 + (i - 2) * per)
                    for h in range(2):
                        tile_step(step, 2 * i + h, h, True, (i - 1) * 16)
                    assert step.n == per, step.n
                step = LoopSteps(dve, dve_step, n0 + (T // 2 - 2) * per)
                tile_step(step, T, 0, False, (T // 2 - 1) * 16)
                move_share(dve, nc.vector.tensor_copy, True, T - 1, C - 1)
                finish(step, T - 1, 1, (T // 2 - 1) * 16)

            @block.scalar
            def _(act):
                def convert(t, c, stored):
                    act.wait_ge(in_c[c], t * 16 + 16)
                    if stored:
                        act.wait_ge(logit, (t - 1) * C + c + 1)
                        act.wait_ge(store_c[c], t * 16)
                    nc.scalar.activation(MB[c][:], AD[c][:], ACT.Copy, scale=MASKED, bias=-MASKED).then_inc(conv, 1)

                def exponent(t, h, c, first_two):
                    if c == 0:
                        act.wait_ge(bias_ok, t + 1)
                    if not first_two:
                        act.wait_ge(turned, (t * C + c - 1) * UPC)
                    nc.scalar.activation(PB[c % 2][:], MD[c][:], ACT.Exp, bias=st[:, h, 4:5], scale=1.0,
                                         accum_out=sums[:, h, c:c + 1]).then_inc(expd, 1)

                def tile_step(t, h, has_logits):
                    known = isinstance(t, int)
                    for c in range(C):
                        if not known or t >= 1:
                            exponent(t - 1, 1 - h, c, known and t == 1 and c < 2)
                        if first and has_logits:
                            if c == 0:
                                convert(t, C - 1, not known or t >= 1)
                            elif not known or t + 1 < T:
                                convert(t + 1, c - 1, True)
                        if not known or t >= 2 or (t == 1 and c >= 1):
                            if c == 0:
                                move_share(act, nc.scalar.copy, False, t - 2, C - 1)
                            else:
                                move_share(act, nc.scalar.copy, False, t - 1, c - 1)

                if first:
                    for c in range(C - 1):
                        convert(0, c, False)
                for t in range(2):
                    tile_step(t, t, True)
                with act.Fori(1, T // 2 - 1) as i:
                    for h in range(2):
                        tile_step(2 * i + h, h, True)
                for t in range(T - 2, T + 1):
                    tile_step(t, t % 2, t < T)
                move_share(act, nc.scalar.copy, False, T - 1, C - 1)

            @block.tensor
            def _(pe):
                def turn(t, u):
                    if u % UPC == 0:
                        pe.wait_ge(expd, t * C + u // UPC + 1)
                    known = isinstance(t, int)
                    if not known or t * U + u >= 2:
                        wait_moved(pe, t if u >= 2 else t - 1, u - 2 if u >= 2 else U - 2 + u)
                    c, o = u // UPC, (u % UPC) * UW
                    for b in range(BPU):
                        ins = nc.tensor.transpose(TP[u % 2][:, b * P:(b + 1) * P], PB[c % 2][:, o + b * P:o + (b + 1) * P], ident[:])
                    ins.then_inc(turned, 1)

                def multiply(t, h, u, reused):
                    wait_moved(pe, t, u)
                    if u == 0 and reused:
                        pe.wait_ge(hp_ok, t - 1)
                    for b in range(BPU):
                        j = u * BPU + b
                        ins = nc.tensor.matmul(OUT[:, h, 0:D], PT[u % 2][:, b * P:(b + 1) * P], H[:, j, :],
                                               start=(j == 0), stop=(j == T - 1))
                    ins.then_inc(unit_mm, 1)

                def tile_step(t, h, reused):
                    for u in range(U):
                        turn(t, u)
                        if u:
                            multiply(t, h, u - 1, reused)
                        elif not isinstance(t, int) or t:
                            last_unit(t - 1, 1 - h)

                def last_unit(t, h):
                    multiply(t, h, U - 1, False)

                for t in range(2):
                    tile_step(t, t, False)
                with pe.Fori(1, T // 2) as i:
                    for h in range(2):
                        tile_step(2 * i + h, h, True)
                last_unit(T - 1, 1)


DVE_UNITS = {True: (), False: (1, 3, 5, 7)}
LOOP_STEPS = {True: 2 * (1 + CHUNKS + 1 + 2), False: 2 * (1 + 1 + 1 + 2)}


def project_l1(nc, X, H, work, row_w, dcol, low, levels, ident, W1, b1, W2, Ww, bw):
    T, D = X.shape[1], X.shape[2]
    G = T // 4
    HID = W1.shape[0]
    with Phase(nc, "pj2") as ph:
        FT = [ph.sbuf(f"FT{k}", [P, 4, D]) for k in range(2)]
        W = ph.sbuf("W", [HID, 2, D])
        wcol = ph.sbuf("wcol", [HID, 1])
        wrep = ph.sbuf("wrep", [HID, P])
        bias = ph.sbuf("bias", [P, 3])
        c12 = ph.sbuf("c12", [D, 2])
        small = ph.sbuf("small", [P, 3, T])
        scol = ph.sbuf("scol", [P, T])
        ext = ph.sbuf("ext", [P, 3])
        ext3 = ph.sbuf("ext3", [3, 1])
        diag = ph.sbuf("diag", [3, 3])
        ones = ph.sbuf("ones", [3, P])
        lev = ph.sbuf("lev", [1, 1])
        PS = ph.psum("ps", [P, 5, BANK])
        w_in, rep_ok, c_ok, c_out, var_ok, sqrt_ok, dve_step, h_ok, t_ok, t_out, d_ok = ph.sems(
            "w_in", "rep_ok", "c_ok", "c_out", "var_ok", "sqrt_ok", "dve_step", "h_ok", "t_ok", "t_out", "d_ok")
        ext_ok, turned_ok, diag_ok, all_ok, u_ok = ph.sems("ext_ok", "turned_ok", "diag_ok", "all_ok", "u_ok")
        with nc.Block() as block:
            @block.sync
            def _(sp):
                sp.dma_start(wcol[:], Ww.rearrange("o h -> h o")).then_inc(w_in, 16)
                sp.dma_start(W[:, 0, :], W1).then_inc(w_in, 16)
                sp.dma_start(W[:, 1, :], W2).then_inc(w_in, 16)
                sp.dma_start(bias[:, 0:1], b1.rearrange("(h o) -> h o", o=1)).then_inc(w_in, 16)
                sp.dma_start(bias[:, 1:2], bw.rearrange("(o c) -> o c", o=1).to_broadcast([P, 1])).then_inc(w_in, 16)

            @block.vector
            def _(dve):
                step = Chain(dve, dve_step)
                dve.wait_ge(w_in, 80)
                nc.vector.tensor_copy(wrep[:], wcol[:].to_broadcast([HID, P])).then_inc(rep_ok, 1)
                dve.wait_ge(c_ok, 1)
                nc.vector.tensor_tensor(bias[:, 2:3], PS[:, 3, 2:3], bias[:, 1:2], ALU.add)
                nc.vector.tensor_copy(c12[:], PS[:, 3, 0:2]).then_inc(c_out, 1)
                norm_rows(nc, dve, step, X, H, work, small, var_ok, sqrt_ok, D)
                dve.sem_inc(h_ok, 1)
                for g in range(G):
                    dve.wait_ge(t_ok, g + 1)
                    if g >= 2:
                        dve.wait_ge(d_ok, g - 1)
                    nc.vector.tensor_copy(FT[g % 2][:], PS[:, g % 2, :].rearrange("p (t d) -> p t d", d=D)).then_inc(t_out, 1)
                dve.wait_ge(d_ok, G)
                both = PS[:, 2, 0:2 * T].rearrange("p (t k) -> p t k", k=2)
                step(nc.vector.tensor_scalar(scol[:], both[:, :, 0], bias[:, 2:3], None, ALU.add))
                step(nc.vector.tensor_copy(dcol[:], both[:, :, 1]))
                step(nc.vector.tensor_reduce(ext[:, 0:1], dcol[:], AX.X, ALU.max))
                step(nc.vector.tensor_reduce(ext[:, 1:2], dcol[:], AX.X, ALU.min))
                step(nc.vector.tensor_scalar(ext[:, 1:2], ext[:, 1:2], -1.0, None, ALU.mult))
                step(nc.vector.tensor_reduce(ext[:, 2:3], scol[:], AX.X, ALU.max))
                step(nc.vector.memset(ones[:], 1.0))
                dve.sem_inc(ext_ok, 1)
                dve.wait_ge(turned_ok, 1)
                step(nc.vector.tensor_reduce(ext3[:], PS[0:3, 4, 0:P], AX.X, ALU.max))
                nc.vector.tensor_scalar(diag[:], ident[0:3, 0:3], ext3[:], None, ALU.mult).then_inc(diag_ok, 1)
                dve.wait_ge(all_ok, 1)
                step(nc.vector.tensor_copy(ext[:], PS[:, 3, 4:7]))
                step(nc.vector.tensor_scalar(low[:], ext[:, 0:1], -LEVEL, None, ALU.add))
                step(nc.vector.tensor_tensor(lev[:], ext[0:1, 0:1], ext[0:1, 1:2], ALU.add))
                step(nc.vector.tensor_scalar(lev[:], lev[:], 1.0, 1.0 / LEVEL, ALU.add, ALU.mult))
                step(nc.vector.tensor_scalar(lev[:], lev[:], 1.0, float(MOST_LEVELS), ALU.add, ALU.min))
                step(nc.vector.tensor_copy(levels[:], lev[:]))
                step(nc.vector.tensor_scalar(row_w[:], scol[:], ext[:, 2:3], -LEVEL, ALU.subtract, ALU.max))
                dve.sem_inc(u_ok, 1)

            @block.scalar
            def _(act):
                act.wait_ge(var_ok, 1)
                nc.scalar.activation(small[:, 1, :], small[:, 2, :], ACT.Sqrt).then_inc(sqrt_ok, 1)
                act.wait_ge(u_ok, 1)
                nc.scalar.activation(row_w[:], row_w[:], ACT.Exp)

            @block.tensor
            def _(pe):
                pe.wait_ge(rep_ok, 1)
                for k in range(2):
                    nc.tensor.matmul(PS[:, 3, k:k + 1], W[:, k, :], wcol[:], start=True, stop=True)
                nc.tensor.matmul(PS[:, 3, 2:3], wrep[:], bias[:, 0:1], start=True, stop=True).then_inc(c_ok, 1)
                pe.wait_ge(c_out, 1)
                pe.wait_ge(h_ok, 1)
                for g in range(G + 1):
                    if g < G:
                        if g >= 2:
                            pe.wait_ge(t_out, g - 1)
                        for k in range(4):
                            ins = nc.tensor.transpose(PS[:, g % 2, k * P:(k + 1) * P], H[:, 4 * g + k, :], ident[:])
                        ins.then_inc(t_ok, 1)
                    if g:
                        m = g - 1
                        pe.wait_ge(t_out, m + 1)
                        for t in range(4 * m, 4 * m + 4):
                            ins = nc.tensor.matmul(PS[:, 2, 2 * t:2 * t + 2], FT[m % 2][:, t % 4, :], c12[:], start=True, stop=True)
                        ins.then_inc(d_ok, 1)
                pe.wait_ge(ext_ok, 1)
                nc.tensor.transpose(PS[0:3, 4, 0:P], ext[:], ident[:]).then_inc(turned_ok, 1)
                pe.wait_ge(diag_ok, 1)
                nc.tensor.matmul(PS[:, 3, 4:7], ones[:], diag[:], start=True, stop=True).then_inc(all_ok, 1)


def attend_levels(nc, mask, F, row_w, dcol, low, levels, prop, anyrow, ident):
    T, D = F.shape[1], F.shape[2]
    N = T * P
    D1 = D + 1
    QT = 4
    UB = 8
    UPT = T // UB
    U = QT * UPT
    NQ = T // QT
    LAG = 3
    HQ = T // 4
    NTP, NAT = 4, 4
    with Phase(nc, "at1") as ph:
        MB = [ph.sbuf(f"mask{b}", [P, N], BF16) for b in range(2)]
        AT = [ph.sbuf(f"at{b}", [P, UB * P], BF16) for b in range(NAT)]
        parts = ph.sbuf("parts", [P, T, 3, D1], BF16)
        left = [ph.sbuf(f"left{b}", [P, HQ, D1]) for b in range(2)]
        ev = ph.sbuf("ev", [P, T])
        todo = ph.sbuf("todo", [P, T])
        res = ph.sbuf("res", [P, 2, D1])
        st = ph.sbuf("st", [P, 4])
        identB = ph.sbuf("identB", [P, P], BF16)
        TP = [ph.psum(f"tp{b}", [P, UB * P], BF16) for b in range(NTP)]
        OUT = ph.psum("out", [P, QT, BANK])
        id_ok, turned, mult, fin, dve_step, ev_ok, exp_ok, left_ok, part_ok, split_ok, passed = ph.sems(
            "id_ok", "turned", "mult", "fin", "dve_step", "ev_ok", "exp_ok", "left_ok", "part_ok", "split_ok", "passed")
        copied = [ph.sem("copied_act"), ph.sem("copied_dve")]
        in_b = [ph.sem(f"in{b}") for b in range(2)]
        mask_t = mask.rearrange("(t p) c -> t p c", p=P)
        START = 2
        AT_LEVEL, IN_BODY = 3 + 4 * 4, QT * 8

        def nested(eng, level_start, body):
            n = eng.value_load(levels[0:1, 0:1], min_val=1, max_val=MOST_LEVELS)
            with eng.Fori(0, n) as l:
                if level_start is not None:
                    level_start(l)
                with eng.Fori(0, NQ) as i:
                    body(l, i, l * NQ + i)

        with nc.Block() as block:
            @block.sync
            def _(sp):
                def body(l, i, q):
                    for x in range(QT):
                        sp.wait_ge(turned, q * U + UPT * (x + 1))
                        sp.sem_inc(passed, 1)
                        sp.dma_start(MB[x % 2][:], mask_t[QT * i + x]).then_inc(in_b[x % 2], 16)

                nested(sp, None, body)

            @block.tensor
            def _(pe):
                def turn(q, u):
                    x = u // UPT
                    if u % UPT == 0:
                        pe.wait_ge(in_b[x % 2], q * (16 * QT // 2) + 16 * (x // 2 + 1))
                    pe.wait_ge(copied[u % 2], q * (U // 2) + u // 2 + 1)
                    for b in range(UB):
                        o = ((u % UPT) * UB + b) * P
                        ins = nc.tensor.transpose(TP[u % NTP][:, b * P:(b + 1) * P], MB[x % 2][:, o:o + P], identB[:])
                    ins.then_inc(turned, 1)

                def multiply(q, u):
                    x = u // UPT
                    pe.wait_ge(copied[u % 2], q * (U // 2) + u // 2 + 3)
                    if u % UPT == 0:
                        pe.wait_ge(fin, q * QT + x + 1)
                    for b in range(UB):
                        k = (u % UPT) * UB + b
                        ins = nc.tensor.matmul(OUT[:, x, 0:3 * D1], AT[u % NAT][:, b * P:(b + 1) * P],
                                               parts[:, k].rearrange("p k d -> p (k d)"), start=(k == 0), stop=(k == T - 1))
                    ins.then_inc(mult, 1)

                def body(l, i, q):
                    for u in range(U + LAG):
                        if u < U:
                            turn(q, u)
                        if u >= LAG:
                            multiply(q, u - LAG)

                pe.wait_ge(id_ok, 1)
                pe.sem_inc(turned, 2 * UPT)
                pe.sem_inc(mult, NAT)
                nested(pe, lambda l: (pe.wait_ge(split_ok, l + 1), pe.sem_inc(passed, 1)), body)

            def copy_out(eng, q, u, copy):
                eng.wait_ge(turned, q * U + u + 1 + 2 * UPT)
                eng.wait_ge(mult, q * U + u + 1)
                copy(AT[u % NAT][:], TP[u % NTP][:]).then_inc(copied[u % 2], 1)

            @block.scalar
            def _(act):
                def level_start(l):
                    act.wait_ge(ev_ok, l + 1)
                    nc.scalar.activation(ev[:], ev[:], ACT.Exp).then_inc(exp_ok, 1)
                    for h in range(4):
                        for k in range(2):
                            act.wait_ge(left_ok, l * 8 + 2 * h + k + 1)
                            nc.scalar.activation(parts[:, h * HQ:(h + 1) * HQ, k, :], left[h % 2][:], ACT.Copy).then_inc(part_ok, 1)

                def body(l, i, q):
                    for u in range(0, U, 2):
                        copy_out(act, q, u, lambda o, x: nc.scalar.activation(o, x, ACT.Copy, scale=1.0 / MASKED, bias=1.0))

                act.sem_inc(copied[0], 2)
                nested(act, level_start, body)

            @block.vector
            def _(dve):
                def level_start(l):
                    step = LoopSteps(dve, dve_step, START + l * (AT_LEVEL + NQ * IN_BODY))
                    step.now(nc.vector.tensor_scalar(ev[:], dcol[:], low[:, 0:1], LEVEL, ALU.subtract, ALU.min))
                    step.now(nc.vector.tensor_scalar(low[:], low[:], -LEVEL, None, ALU.add))
                    dve.sem_inc(ev_ok, 1)
                    dve.wait_ge(exp_ok, l + 1)
                    step.now(nc.vector.tensor_copy(st[:, 0:1], ev[:, 0:1]))
                    for h in range(4):
                        ts = slice(h * HQ, (h + 1) * HQ)
                        e = ev[:, ts]
                        step(nc.vector.tensor_copy(left[h % 2][:, :, D], e))
                        step.now(nc.vector.tensor_tensor(left[h % 2][:, :, 0:D], F[:, ts, :], e.unsqueeze(2).to_broadcast([P, HQ, D]), ALU.mult))
                        for k in range(2):
                            dve.sem_inc(left_ok, 1)
                            dve.wait_ge(part_ok, l * 8 + 2 * h + k + 1)
                            step.now(nc.vector.tensor_tensor(left[h % 2][:], left[h % 2][:], parts[:, ts, k, :], ALU.subtract))
                        ins = nc.vector.tensor_copy(parts[:, ts, 2, :], left[h % 2][:])
                    ins.then_inc(split_ok, 1)

                def finish(step, l, i, q, x):
                    t = bass.ds(QT * i + x, 1)
                    dve.wait_ge(mult, q * U + UPT * (x + 1) + NAT)
                    step.now(nc.vector.tensor_copy(res[:, 0, :], OUT[:, x, 2 * D1:3 * D1]))
                    step.now(nc.vector.tensor_tensor(res[:, 0, :], res[:, 0, :], OUT[:, x, D1:2 * D1], ALU.add))
                    step.now(nc.vector.tensor_tensor(res[:, 1, :], res[:, 0, :], OUT[:, x, 0:D1], ALU.add))
                    dve.sem_inc(fin, 1)
                    total = res[:, 1, D:D1]
                    step(nc.vector.scalar_tensor_tensor(out=st[:, 0:1], in0=total, scalar=0.5, in1=todo[:, t], op0=ALU.is_gt, op1=ALU.mult))
                    step.now(nc.vector.tensor_scalar(st[:, 1:2], total, row_w[:, t], 1e-37, ALU.mult, ALU.max))
                    step.now(nc.vector.reciprocal(st[:, 2:3], st[:, 1:2]))
                    step.now(nc.vector.scalar_tensor_tensor(out=st[:, 3:4], in0=st[:, 2:3], scalar=row_w[:, t], in1=st[:, 0:1], op0=ALU.mult, op1=ALU.mult))
                    nc.vector.tensor_tensor(todo[:, t], todo[:, t], st[:, 0:1], ALU.subtract)
                    row = prop[:, t, :].rearrange("p a d -> p (a d)")
                    step.now(nc.vector.scalar_tensor_tensor(out=row, in0=res[:, 1, 0:D], scalar=st[:, 3:4], in1=row, op0=ALU.mult, op1=ALU.add))

                def body(l, i, q):
                    step = LoopSteps(dve, dve_step, START + AT_LEVEL + l * (AT_LEVEL + NQ * IN_BODY) + i * IN_BODY)
                    for u in range(1, U, 2):
                        copy_out(dve, q, u, lambda o, x: nc.vector.tensor_scalar(o, x, 1.0 / MASKED, 1.0, ALU.mult, ALU.add))
                        if u % UPT == LAG + 2 and u > UPT:
                            finish(step, l, i, q, u // UPT - 1)
                    finish(step, l, i, q, QT - 1)
                    assert step.n == IN_BODY, step.n

                nc.vector.tensor_copy(identB[:], ident[:]).then_inc(id_ok, 1)
                dve.sem_inc(copied[1], 2)
                dve.sem_inc(fin, QT)
                step = LoopSteps(dve, dve_step)
                step(nc.vector.memset(todo[:], 1.0))
                step.now(nc.vector.memset(prop[:], 0.0))
                nested(dve, level_start, body)
                nc.vector.tensor_scalar(anyrow[:], todo[:], -1.0, 1.0, ALU.mult, ALU.add)


def route_l1(nc, ident, X, F, anyrow, router_w, w1, w2, w3, XT, G, up, gate, down):
    T, D = X.shape[1], X.shape[2]
    GR = T // 4
    NE, HID = w1.shape[0], w1.shape[1]
    parts = hidden_parts(HID)
    K = len(parts)
    with Phase(nc, "rt") as ph:
        PR = XT
        W13 = [ph.sbuf(f"W13_{k}", [P, NE, K, D]) for k in range(2)]
        W2 = ph.sbuf("W2", [P, NE, HID])
        rw = ph.sbuf("rw", [NE, D])
        rwT = ph.sbuf("rwT", [D, NE])
        small = ph.sbuf("small", [P, 3, T])
        prob = ph.sbuf("prob", [P, T, NE])
        left = ph.sbuf("left", [P, T, NE])
        sel = [ph.sbuf(f"sel{k}", [P, T, NE]) for k in range(2)]
        best = ph.sbuf("best", [P, 2, T])
        free = ph.sbuf("free", [P, T])
        PS = ph.psum("ps", [P, 7, BANK])
        w_in, var_ok, sqrt_ok, dve_step, y_ok, t_ok, t_out, l_ok, ex_ok, exp_ok = ph.sems(
            "w_in", "var_ok", "sqrt_ok", "dve_step", "y_ok", "t_ok", "t_out", "l_ok", "ex_ok", "exp_ok")
        r_ok, r_out, turned, up_out, gate_out, down_out = ph.sems("r_ok", "r_out", "turned", "up_out", "gate_out", "down_out")
        n_w = 2 + 2 * K
        with nc.Block() as block:
            @block.sync
            def _(sp):
                sp.dma_start(rw[:], router_w).then_inc(w_in, 16)
                for dst, w in ((W13[0], w1), (W13[1], w3)):
                    for k, (o, n) in enumerate(parts):
                        sp.dma_start(dst[0:n, :, k, :], w[:, o:o + n, :].rearrange("e h c -> h e c")).then_inc(w_in, 16)
                sp.dma_start(W2[:], w2.rearrange("e c h -> c e h")).then_inc(w_in, 16)

            @block.tensor
            def _(pe):
                pe.wait_ge(w_in, 16 * n_w)
                nc.tensor.transpose(PS[:, 6, 0:NE], rw[:], ident[0:NE, 0:NE]).then_inc(r_ok, 1)
                for e in range(NE):
                    if e:
                        pe.wait_ge(up_out, e)
                        pe.wait_ge(gate_out, e)
                        pe.wait_ge(down_out, e)
                    for s in range(2):
                        for k, (o, n) in enumerate(parts):
                            nc.tensor.transpose(PS[:, 2 + s, o:o + n], W13[s][0:n, e, k, :], ident[0:n, 0:n])
                    for k, (o, n) in enumerate(parts):
                        ins = nc.tensor.transpose(PS[0:n, 4, k * D:(k + 1) * D], W2[:, e, o:o + n], ident[:])
                    ins.then_inc(turned, 1)
                pe.wait_ge(y_ok, 1)
                pe.wait_ge(r_out, 1)
                for g in range(GR + 1):
                    if g < GR:
                        if g >= 2:
                            pe.wait_ge(t_out, g - 1)
                        for k in range(4):
                            ins = nc.tensor.transpose(PS[:, g % 2, k * P:(k + 1) * P], F[:, 4 * g + k, :], ident[:])
                        ins.then_inc(t_ok, 1)
                    if g:
                        pe.wait_ge(t_out, g)
                        for t in range(4 * g - 4, 4 * g):
                            ins = nc.tensor.matmul(PS[:, 5, t * NE:(t + 1) * NE], XT[:, t, :], rwT[:], start=True, stop=True)
                ins.then_inc(l_ok, 1)

            @block.scalar
            def _(act):
                act.wait_ge(r_ok, 1)
                nc.scalar.copy(rwT[:], PS[:, 6, 0:NE]).then_inc(r_out, 1)
                for e in range(NE):
                    act.wait_ge(turned, e + 1)
                    nc.scalar.copy(up[:, e, :], PS[:, 2, 0:HID]).then_inc(up_out, 1)
                    nc.scalar.copy(gate[:, e, :], PS[:, 3, 0:HID]).then_inc(gate_out, 1)
                    for k, (o, n) in enumerate(parts):
                        ins = nc.scalar.copy(down[0:n, e, k, :], PS[0:n, 4, k * D:(k + 1) * D])
                    ins.then_inc(down_out, 1)
                act.wait_ge(var_ok, 1)
                nc.scalar.activation(small[:, 1, :], small[:, 2, :], ACT.Sqrt).then_inc(sqrt_ok, 1)
                for g in range(GR):
                    act.wait_ge(t_ok, g + 1)
                    nc.scalar.copy(XT[:, 4 * g:4 * g + 4, :], PS[:, g % 2, :].rearrange("p (t d) -> p t d", d=D)).then_inc(t_out, 1)
                act.wait_ge(ex_ok, 1)
                nc.scalar.activation(prob[:], prob[:], ACT.Exp).then_inc(exp_ok, 1)

            @block.vector
            def _(dve):
                step = Chain(dve, dve_step)

                def over(x, n):
                    return x.unsqueeze(2).to_broadcast([P, T, n])

                step(nc.vector.tensor_tensor(PR[:], PR[:], F[:], ALU.subtract))
                step(nc.vector.tensor_tensor(PR[:], PR[:], over(anyrow[:], D), ALU.mult))
                step(nc.vector.scalar_tensor_tensor(out=PR[:], in0=F[:], scalar=2.0, in1=PR[:], op0=ALU.mult, op1=ALU.add))
                step(nc.vector.scalar_tensor_tensor(out=X[:], in0=PR[:], scalar=0.5, in1=X[:], op0=ALU.mult, op1=ALU.add))
                norm_rows(nc, dve, step, X, F, PR[:], small, var_ok, sqrt_ok, D)
                dve.sem_inc(y_ok, 1)
                dve.wait_ge(l_ok, 1)
                logits = PS[:, 5, 0:T * NE].rearrange("p (t e) -> p t e", e=NE)
                step(nc.vector.tensor_reduce(free[:], logits, AX.X, ALU.max))
                step(nc.vector.tensor_tensor(prob[:], logits, over(free[:], NE), ALU.subtract))
                dve.sem_inc(ex_ok, 1)
                dve.wait_ge(exp_ok, 1)
                step(nc.vector.tensor_reduce(free[:], prob[:], AX.X, ALU.add))
                step(nc.vector.reciprocal(free[:], free[:]))
                step(nc.vector.tensor_tensor(prob[:], prob[:], over(free[:], NE), ALU.mult))
                top_two(nc, step, prob[:], left[:], [sel[0][:], sel[1][:]], best, free[:])
                step(nc.vector.tensor_tensor(free[:], best[:, 0, :], best[:, 1, :], ALU.add))
                step(nc.vector.tensor_scalar(free[:], free[:], 1e-9, None, ALU.add))
                step(nc.vector.reciprocal(free[:], free[:]))
                for k in range(2):
                    step(nc.vector.tensor_tensor(best[:, k, :], best[:, k, :], free[:], ALU.mult))
                    step(nc.vector.tensor_tensor(sel[k][:], sel[k][:], over(best[:, k, :], NE), ALU.mult))
                step(nc.vector.tensor_tensor(G[:], sel[0][:], sel[1][:], ALU.add))


def hidden_parts(hidden):
    return [(o, min(P, hidden - o)) for o in range(0, hidden, P)]


def experts(nc, tag, X, XT, G, hidden, up, down, gate=None, b1=None, b2=None, gates=None, out=None):
    T, D = X.shape[1], X.shape[2]
    GT = BANK // P
    NG = T // GT
    NE = G.shape[2]
    parts = hidden_parts(hidden)
    K = len(parts)
    U = NE * K
    assert NE % 2 == 0 and U % 2 == 0
    with Phase(nc, tag) as ph:
        HH = [[ph.sbuf(f"HH{b}_{k}", [P, BANK]) for k in range(K)] for b in range(2)]
        SL = [ph.sbuf(f"SL{b}", [P, BANK]) for b in range(2)] if gate is not None else None
        b2row = ph.sbuf("b2row", [1, NE, D]) if b2 is not None else None
        b1col = ph.sbuf("b1col", [P, NE, K]) if b1 is not None else None
        one = ph.sbuf("one", [1, P]) if b2 is not None else None
        HP = ph.psum("hp", [P, 2, 2, BANK])
        YP = ph.psum("yp", [P, 2, BANK])
        in_ok, one_ok, h_ok, silu_ok, hid_ok, y_ok, y_used, x_out = ph.sems(
            "in_ok", "one_ok", "h_ok", "silu_ok", "hid_ok", "y_ok", "y_used", "x_out")
        n_in = 0 if gate is not None else NE * K + 2
        with nc.Block() as block:
            @block.sync
            def _(sp):
                if gate is None:
                    sp.dma_start(G[:], gates.rearrange("(t p) e -> p t e", p=P)).then_inc(in_ok, 16)
                    sp.dma_start(b2row[:], b2.rearrange("(o e) d -> o e d", o=1)).then_inc(in_ok, 16)
                    for e in range(NE):
                        for k, (o, n) in enumerate(parts):
                            sp.dma_start(b1col[0:n, e, k:k + 1], b1[e, o:o + n].rearrange("(h o) -> h o", o=1)).then_inc(in_ok, 16)
                if out is not None:
                    ov = out.rearrange("(t p) d -> p t d", p=P)
                    for g in range(NG):
                        sp.wait_ge(y_used, (g + 1) * NE)
                        sp.dma_start(ov[:, g * GT:(g + 1) * GT, :], X[:, g * GT:(g + 1) * GT, :]).then_inc(x_out, 16)
                    sp.wait_ge(x_out, 16 * NG)

            @block.tensor
            def _(pe):
                def hidden_part(g, e, k):
                    u = e * K + k
                    o, n = parts[k]
                    if not isinstance(g, int) or u >= 2:
                        pe.wait_ge(hid_ok, g * U + u - 1)
                    for s, w in enumerate([up] if gate is None else [up, gate]):
                        ins = nc.tensor.matmul(HP[0:n, u % 2, s, :], w[:, e, o:o + n], XT[:, bass.ds(g * GT, GT), :], start=True, stop=True)
                    ins.then_inc(h_ok, 1)

                def output(g, e, peeled):
                    pe.wait_ge(hid_ok, (g * NE + e + 1) * K)
                    if not peeled or e >= 2:
                        pe.wait_ge(y_used, g * NE + e - 1)
                    for q in range(GT):
                        for k, (o, n) in enumerate(parts):
                            ins = nc.tensor.matmul(YP[:, e % 2, q * D:(q + 1) * D], HH[e % 2][k][0:n, q * P:(q + 1) * P],
                                                   down[0:n, e % NE, k, :], start=(k == 0), stop=(k == K - 1 and b2 is None))
                        if b2 is not None:
                            ins = nc.tensor.matmul(YP[:, e % 2, q * D:(q + 1) * D], one[:], b2row[:, e % NE, :], start=False, stop=True)
                    ins.then_inc(y_ok, 1)

                def group(g, peeled):
                    for e in range(NE):
                        for k in range(K):
                            hidden_part(g, e, k)
                        if e or not peeled:
                            output(g, e - 1, peeled)

                if gate is None:
                    pe.wait_ge(in_ok, 16 * n_in)
                    pe.wait_ge(one_ok, 1)
                group(0, True)
                with pe.Fori(1, NG) as g:
                    group(g, False)
                output(NG, -1, False)

            @block.scalar
            def _(act):
                if gate is None:
                    act.wait_ge(in_ok, 16 * n_in)
                with act.Fori(0, NG) as g:
                    for e in range(NE):
                        for k, (o, n) in enumerate(parts):
                            u = e * K + k
                            act.wait_ge(h_ok, g * U + u + 1)
                            if gate is None:
                                nc.scalar.activation(HH[e % 2][k][0:n, :], HP[0:n, u % 2, 0, :], ACT.Gelu,
                                                     bias=b1col[0:n, e, k:k + 1]).then_inc(hid_ok, 1)
                            else:
                                nc.scalar.activation(SL[u % 2][0:n, :], HP[0:n, u % 2, 0, :], ACT.Silu).then_inc(silu_ok, 1)

            @block.vector
            def _(dve):
                def gated(g, e, k):
                    u = e * K + k
                    o, n = parts[k]
                    dve.wait_ge(silu_ok, g * U + u + 1)
                    nc.vector.tensor_tensor(HH[e % 2][k][0:n, :], SL[u % 2][0:n, :], HP[0:n, u % 2, 1, :], ALU.mult).then_inc(hid_ok, 1)

                def add(g, e, gx, ex):
                    dve.wait_ge(y_ok, g * NE + e + 1)
                    if not isinstance(g, int) or e:
                        dve.wait_ge(y_used, g * NE + e)
                    for q in range(GT):
                        t = bass.ds(gx * GT + q, 1)
                        xt = X[:, t, :].rearrange("p a d -> p (a d)")
                        ins = nc.vector.scalar_tensor_tensor(out=xt, in0=YP[:, ex % 2, q * D:(q + 1) * D],
                                                             scalar=G[:, t, ex:ex + 1].rearrange("p a e -> p (a e)"), in1=xt, op0=ALU.mult, op1=ALU.add)
                    ins.then_inc(y_used, 1)

                def group(g, peeled):
                    for e in range(NE):
                        if gate is not None:
                            for k in range(K):
                                gated(g, e, k)
                        if e or not peeled:
                            add(g, e - 1, g - (e == 0), (e - 1) % NE)

                if gate is None:
                    dve.wait_ge(in_ok, 16 * n_in)
                    nc.vector.memset(one[:], 1.0).then_inc(one_ok, 1)
                group(0, True)
                with dve.Fori(1, NG) as g:
                    group(g, False)
                add(NG, -1, NG - 1, NE - 1)


def load_experts_l0(nc, W1, W2, up, down):
    with Phase(nc, "lw0") as ph:
        w_in = ph.sem("w_in")
        parts = hidden_parts(W1.shape[2])
        with nc.Block() as block:
            @block.sync
            def _(sp):
                sp.dma_start(up[:], W1.rearrange("e c h -> c e h")).then_inc(w_in, 16)
                for k, (o, n) in enumerate(parts):
                    sp.dma_start(down[0:n, :, k, :], W2[:, o:o + n, :].rearrange("e h c -> h e c")).then_inc(w_in, 16)
                sp.wait_ge(w_in, 16 * (1 + len(parts)))


def graph_network(nc, x, adj, L0_gnn_W, L0_gnn_a, L0_ffn_W_gat, L0_ffn_att_src, L0_ffn_att_dst, L0_ffn_b_gat,
                  L0_ffn_ln_gamma, L0_ffn_ln_beta, L0_ffn_W1, L0_ffn_b1, L0_ffn_W2, L0_ffn_b2, L0_ffn_edge_index,
                  L1_gnn_W1, L1_gnn_b1, L1_gnn_W2, L1_gnn_Ww, L1_gnn_bw, L1_ffn_router_w, L1_ffn_w1, L1_ffn_w2, L1_ffn_w3,
                  out):
    N, D = x.shape
    T = N // P
    NE0, NE1 = L0_ffn_W1.shape[0], L1_ffn_w1.shape[0]
    HID0, HID1 = L0_ffn_W1.shape[2], L1_ffn_w1.shape[1]
    NH, HE = L0_ffn_att_src.shape[0], L0_ffn_b_gat.shape[0]
    CHUNK = 128
    LMAX = (-(-(L0_ffn_edge_index.shape[1] + N) // (P * CHUNK)) + 1) * CHUNK

    def dram(name, shape, dtype=F32):
        return nc.dram_tensor(name, shape, dtype).ap()

    mask = dram("mask", (N, N), BF16)
    rec = dram("rec", (P * LMAX, 2), I32)
    plan = dram("plan", (P, L0_ffn_edge_index.shape[1] // P + 16, 3), I32)
    tab = dram("tab", (N, HE + 2 * NH))
    runs = dram("runs", (P * LMAX, 2 * NH + HE))
    carry = dram("carry", (P, 2 * (NH + HE)))
    gates0 = dram("gates0", (N, NE0))
    prop0 = dram("prop0", (N, D))
    with Phase(nc, "top") as top:
        ident = top.sbuf("ident", [P, P])
        ctl = top.sbuf("ctl", [1, 3], I32)
        endi = top.sbuf("endi", [P, T], I32)
        endq = top.sbuf("endq", [P, T], I32)
        cont = top.sbuf("cont", [P, T])
        make_identity(nc, ident)
        with Phase(nc, "g0") as ph:
            self_idx = ph.sbuf("self_idx", [P, T], I32)
            self_rec = ph.sbuf("self_rec", [P, T, 2], I32)
            sort_edges(nc, ident, L0_ffn_edge_index, N, rec, plan, self_idx, self_rec, ctl, endi, endq, cont)
            H = ph.sbuf("H", [P, T, D])
            drow = ph.sbuf("drow", [P, N])
            d01 = ph.sbuf("d01", [P, N])
            scol = ph.sbuf("scol", [P, T])
            project_l0(nc, ident, x, L0_gnn_W, L0_gnn_a, H, drow, d01, scol)
            attend(nc, "at0", ident, adj, mask, H, drow, d01, scol, prop0,
                   beside=lambda pool, at: scatter_records(nc, pool, at, rec, plan, self_idx, self_rec, ctl))

        X = top.sbuf("X", [P, T, D])
        with Phase(nc, "f0") as ph:
            XT = ph.sbuf("XT", [P, T, D])
            project_edges(nc, ident, x, prop0, X, L0_ffn_W_gat, L0_ffn_att_src, L0_ffn_att_dst, XT, tab)
            gate_nodes(nc, ident, rec, tab, runs, carry, ctl, endi, endq, cont, L0_ffn_b_gat, L0_ffn_ln_gamma,
                       L0_ffn_ln_beta, gates0)
            G = ph.sbuf("G", [P, T, NE0])
            up = ph.sbuf("up", [P, NE0, HID0])
            down = ph.sbuf("down", [P, NE0, len(hidden_parts(HID0)), D])
            load_experts_l0(nc, L0_ffn_W1, L0_ffn_W2, up, down)
            experts(nc, "ex0", X, XT, G, HID0, up, down, b1=L0_ffn_b1, b2=L0_ffn_b2, gates=gates0)

        F = top.sbuf("F", [P, T, D])
        anyrow = top.sbuf("anyrow", [P, T])
        XT = top.sbuf("XT", [P, T, D])
        with Phase(nc, "g1") as ph:
            row_w = ph.sbuf("row_w", [P, T])
            dcol = ph.sbuf("dcol", [P, T])
            low = ph.sbuf("low", [P, 1])
            levels = ph.sbuf("levels", [1, 1], I32)
            project_l1(nc, X, F, XT[:], row_w, dcol, low, levels, ident, L1_gnn_W1, L1_gnn_b1, L1_gnn_W2, L1_gnn_Ww, L1_gnn_bw)
            attend_levels(nc, mask, F, row_w, dcol, low, levels, XT, anyrow, ident)

        G = top.sbuf("G", [P, T, NE1])
        up = top.sbuf("up", [P, NE1, HID1])
        gate = top.sbuf("gate", [P, NE1, HID1])
        down = top.sbuf("down", [P, NE1, len(hidden_parts(HID1)), D])
        route_l1(nc, ident, X, F, anyrow, L1_ffn_router_w, L1_ffn_w1, L1_ffn_w2, L1_ffn_w3, XT, G, up, gate, down)
        experts(nc, "ex1", X, XT, G, HID1, up, down, gate=gate, out=out)


def kernel(**inputs):
    import numpy as np
    import concourse.bacc as _bacc
    from concourse import mybir as _mybir
    from concourse.bass_utils import run_bass_kernel_spmd as _run

    nc = _bacc.Bacc("TRN2", target_bir_lowering=False, num_devices=1)
    arrays, args = {}, {}
    for name, value in inputs.items():
        a = np.ascontiguousarray(np.asarray(value))
        arrays[f"in_{name}_dram"] = a
        args[name] = nc.dram_tensor(f"in_{name}_dram", a.shape, _mybir.dt.from_np(a.dtype), kind="ExternalInput").ap()
    out = nc.dram_tensor("out_0_dram", inputs["x"].shape, F32, kind="ExternalOutput").ap()
    graph_network(nc, out=out, **args)
    r = _run(nc, [arrays], core_ids=[0])
    return np.asarray(r.results[0]["out_0_dram"])
```

```python
import math
from contextlib import ExitStack

import concourse.bass as bass
from concourse import mybir

ALU = mybir.AluOpType
ACT = mybir.ActivationFunctionType
AX = mybir.AxisListType
F32 = mybir.dt.float32
BF16 = mybir.dt.bfloat16
I32 = mybir.dt.int32
U16 = mybir.dt.uint16

P = 128
BANK = 512
EPS = 1e-5
LOW = 1e30
CW = 1024
REACH = 20.0
STEEP = 50.0
FLAT = 5000.0
LEVEL = 60.0


class Chain:

    def __init__(self, eng, sem):
        self.eng, self.sem, self.n = eng, sem, 0

    def __call__(self, ins):
        self.n += 1
        ins.then_inc(self.sem, 1)
        self.eng.wait_ge(self.sem, self.n)


class Phase:

    def __init__(self, nc, tag):
        self.nc, self.tag, self.stack, self.taken = nc, tag, ExitStack(), []

    def __enter__(self):
        self.stack.__enter__()
        return self

    def __exit__(self, *e):
        if self.taken:
            self.nc.clear_and_free_semaphores(self.taken)
            self.nc.all_engine_barrier()
        return self.stack.__exit__(*e)

    def sbuf(self, name, shape, dtype=F32):
        return self.stack.enter_context(self.nc.sbuf_tensor(f"{self.tag}_{name}", shape, dtype))

    def psum(self, name, shape, dtype=F32):
        return self.stack.enter_context(self.nc.psum_tensor(f"{self.tag}_{name}", shape, dtype))

    def sem(self, name):
        sem = self.nc.alloc_semaphore(f"{self.tag}_{name}")
        self.taken.append(sem.num)
        return sem

    def sems(self, *names):
        return [self.sem(n) for n in names]


def norm_rows(nc, dve, step, X, Y, work, small, rsqrt_ready, sqrt_done, width):
    T = X.shape[1]
    mean, var, rstd = small[:, 0, :], small[:, 1, :], small[:, 2, :]
    step(nc.vector.tensor_reduce(mean, X[:], AX.X, ALU.add))
    step(nc.vector.tensor_scalar(mean, mean, 1.0 / width, None, ALU.mult))
    step(nc.vector.tensor_tensor(Y[:], X[:], mean.unsqueeze(2).to_broadcast([P, T, width]), ALU.subtract))
    step(nc.vector.tensor_tensor(work, Y[:], Y[:], ALU.mult))
    step(nc.vector.tensor_reduce(var, work, AX.X, ALU.add))
    step(nc.vector.tensor_scalar(var, var, 1.0 / width, EPS, ALU.mult, ALU.add))
    nc.vector.tensor_copy(rstd, var).then_inc(rsqrt_ready, 1)
    dve.wait_ge(sqrt_done, 1)
    step(nc.vector.reciprocal(rstd, var))
    step(nc.vector.tensor_tensor(Y[:], Y[:], rstd.unsqueeze(2).to_broadcast([P, T, width]), ALU.mult))


def make_identity(nc, ident):
    with Phase(nc, "id") as ph:
        zeroed, made = ph.sems("zeroed", "made")
        with nc.Block() as block:
            @block.gpsimd
            def _(pool):
                nc.gpsimd.memset(ident[:], 0.0).then_inc(zeroed, 1)
                pool.wait_ge(zeroed, 1)
                nc.gpsimd.affine_select(out=ident[:], in_=ident[:], compare_op=ALU.not_equal, fill=1.0, base=0,
                                        pattern=[[-1, P]], channel_multiplier=1).then_inc(made, 1)
                pool.wait_ge(made, 1)


def project_l0(nc, ident, x, W, a, H, work, srow, scol, dcol, low, levels):
    N, D = x.shape
    T = N // P
    G = T // 4
    with Phase(nc, "pj0") as ph:
        X = ph.sbuf("X", [P, T, D])
        XT = ph.sbuf("XT", [P, T, D])
        Wt = ph.sbuf("W", [P, D])
        WT = ph.sbuf("WT", [P, D])
        a2 = ph.sbuf("a2", [P, 2])
        wa = ph.sbuf("wa", [P, 2])
        wd = ph.sbuf("wd", [P, P])
        small = ph.sbuf("small", [P, 3, T])
        ext = ph.sbuf("ext", [P, 2])
        ext2 = ph.sbuf("ext2", [2, 1])
        diag = ph.sbuf("diag", [2, 2])
        ones = ph.sbuf("ones", [2, P])
        lev = ph.sbuf("lev", [1, 1])
        ext_ok, ext_turned, diag_ok, all_ok = ph.sems("ext_ok", "ext_turned", "diag_ok", "all_ok")
        PS = ph.psum("ps", [P, 8, BANK])
        x_in, w_in, var_ok, sqrt_ok, dve_step, xn_ok, wt_ok, wt_out, wa_ok, wa_out = ph.sems(
            "x_in", "w_in", "var_ok", "sqrt_ok", "dve_step", "xn_ok", "wt_ok", "wt_out", "wa_ok", "wa_out")
        xt_ok, xt_out, h_ok, h_out, d_ok, d_out = ph.sems(
            "xt_ok", "xt_out", "h_ok", "h_out", "d_ok", "d_out")
        with nc.Block() as block:
            @block.sync
            def _(sp):
                sp.dma_start(Wt[:], W).then_inc(w_in, 16)
                for s in range(2):
                    sp.dma_start(a2[:, s:s + 1], a[s * D:(s + 1) * D, :]).then_inc(w_in, 16)
                xv = x.rearrange("(t p) d -> p t d", p=P)
                for q in range(4):
                    sp.dma_start(X[:, q * T // 4:(q + 1) * T // 4, :], xv[:, q * T // 4:(q + 1) * T // 4, :]).then_inc(x_in, 16)

            @block.vector
            def _(dve):
                step = Chain(dve, dve_step)
                dve.wait_ge(x_in, 64)
                norm_rows(nc, dve, step, X, X, work, small, var_ok, sqrt_ok, D)
                nc.vector.tensor_copy(small[:, 2, 0:1], small[:, 1, 0:1]).then_inc(xn_ok, 1)
                dve.wait_ge(wt_ok, 1)
                nc.vector.tensor_copy(WT[:], PS[:, 7, 0:D]).then_inc(wt_out, 1)
                dve.wait_ge(wa_ok, 1)
                step(nc.vector.tensor_copy(wa[:], PS[:, 7, 128:130]))
                nc.vector.tensor_copy(wd[:], wa[:, 0:1].to_broadcast([P, P])).then_inc(wa_out, 1)
                for g in range(G):
                    dve.wait_ge(xt_ok, g + 1)
                    nc.vector.tensor_copy(XT[:, 4 * g:4 * g + 4, :], PS[:, g % 2, :].rearrange("p (t d) -> p t d", t=4)).then_inc(xt_out, 1)
                    dve.wait_ge(h_ok, g + 1)
                    nc.vector.tensor_copy(H[:, 4 * g:4 * g + 4, :], PS[:, 2 + g % 2, :].rearrange("p (t d) -> p t d", t=4)).then_inc(h_out, 1)
                both = PS[:, 6, 0:2 * T].rearrange("p (t k) -> p t k", k=2)
                step(nc.vector.tensor_copy(scol[:], both[:, :, 0]))
                step(nc.vector.tensor_copy(dcol[:], both[:, :, 1]))
                step(nc.vector.tensor_reduce(ext[:, 0:1], dcol[:], AX.X, ALU.max))
                step(nc.vector.tensor_reduce(ext[:, 1:2], dcol[:], AX.X, ALU.min))
                step(nc.vector.tensor_scalar(ext[:, 1:2], ext[:, 1:2], -1.0, None, ALU.mult))
                step(nc.vector.memset(ones[:], 1.0))
                dve.sem_inc(ext_ok, 1)
                dve.wait_ge(ext_turned, 1)
                step(nc.vector.tensor_reduce(ext2[:], PS[0:2, 7, 0:P], AX.X, ALU.max))
                nc.vector.tensor_scalar(diag[:], ident[0:2, 0:2], ext2[:], None, ALU.mult).then_inc(diag_ok, 1)
                dve.wait_ge(all_ok, 1)
                step(nc.vector.tensor_copy(ext[:], PS[:, 7, P:P + 2]))
                step(nc.vector.tensor_scalar(low[:], ext[:, 0:1], -REACH, None, ALU.add))
                step(nc.vector.tensor_tensor(lev[:], ext[0:1, 0:1], ext[0:1, 1:2], ALU.add))
                step(nc.vector.tensor_scalar(lev[:], lev[:], 1.0, 1.0 / REACH, ALU.add, ALU.mult))
                step(nc.vector.tensor_scalar(lev[:], lev[:], 1.0, float(MOST_LEVELS), ALU.add, ALU.min))
                step(nc.vector.tensor_copy(levels[:], lev[:]))

            @block.scalar
            def _(act):
                act.wait_ge(var_ok, 1)
                nc.scalar.activation(small[:, 1, :], small[:, 2, :], ACT.Sqrt).then_inc(sqrt_ok, 1)
                for g in range(G):
                    act.wait_ge(d_ok, g + 1)
                    nc.scalar.copy(srow[:, BANK * g:BANK * g + BANK], PS[:, 4 + g % 2, :]).then_inc(d_out, 1)

            @block.tensor
            def _(pe):
                pe.wait_ge(w_in, 48)
                nc.tensor.transpose(PS[:, 7, 0:D], Wt[:], ident[:]).then_inc(wt_ok, 1)
                pe.wait_ge(wt_out, 1)
                nc.tensor.matmul(PS[:, 7, 128:130], WT[:], a2[:], start=True, stop=True).then_inc(wa_ok, 1)
                pe.wait_ge(xn_ok, 1)
                pe.wait_ge(wa_out, 1)
                for g in range(G):
                    if g >= 2:
                        pe.wait_ge(xt_out, g - 1)
                    for k in range(4):
                        ins = nc.tensor.transpose(PS[:, g % 2, k * P:(k + 1) * P], X[:, 4 * g + k, :], ident[:])
                    ins.then_inc(xt_ok, 1)
                    if g >= 2:
                        pe.wait_ge(h_out, g - 1)
                        pe.wait_ge(d_out, g - 1)
                    pe.wait_ge(xt_out, g + 1)
                    for k in range(4):
                        nc.tensor.matmul(PS[:, 6, 2 * (4 * g + k):2 * (4 * g + k) + 2], XT[:, 4 * g + k, :], wa[:], start=True, stop=True)
                        ins = nc.tensor.matmul(PS[:, 2 + g % 2, k * P:(k + 1) * P], XT[:, 4 * g + k, :], Wt[:], start=True, stop=True)
                    ins.then_inc(h_ok, 1)
                    ins = nc.tensor.matmul(PS[:, 4 + g % 2, :], wd[:], XT[:, 4 * g:4 * g + 4, :], start=True, stop=True)
                    ins.then_inc(d_ok, 1)
                pe.wait_ge(ext_ok, 1)
                nc.tensor.transpose(PS[0:2, 7, 0:P], ext[:], ident[:]).then_inc(ext_turned, 1)
                pe.wait_ge(diag_ok, 1)
                nc.tensor.matmul(PS[:, 7, P:P + 2], ones[:], diag[:], start=True, stop=True).then_inc(all_ok, 1)


def project_edges(nc, ident, x, X, W_gat, att_src, att_dst, XT, tab):
    N, D = x.shape
    T = N // P
    G = T // 4
    HE = W_gat.shape[1]
    NH, NE = att_src.shape
    with Phase(nc, "pj1") as ph:
        Y = ph.sbuf("Y", [P, T, D])
        E = ph.sbuf("E", [P, T, D])
        Wg = ph.sbuf("Wg", [P, HE])
        att = ph.sbuf("att", [P, 2, HE])
        rows = ph.sbuf("rows", [P, T, HE + 2 * NH])
        prod = ph.sbuf("prod", [P, T, HE])
        small = ph.sbuf("small", [P, 3, T])
        PS = ph.psum("ps", [P, 4, BANK])
        x_in, w_in, neg_ok, exp_ok, var_ok, sqrt_ok, dve_step, y_ok = ph.sems(
            "x_in", "w_in", "neg_ok", "exp_ok", "var_ok", "sqrt_ok", "dve_step", "y_ok")
        xt_ok, xt_out, h_ok, tab_ok, tab_out = ph.sems("xt_ok", "xt_out", "h_ok", "tab_ok", "tab_out")
        with nc.Block() as block:
            @block.sync
            def _(sp):
                sp.dma_start(Y[:], x.rearrange("(t p) d -> p t d", p=P)).then_inc(x_in, 16)
                sp.dma_start(Wg[:], W_gat).then_inc(w_in, 16)
                for k, v in enumerate((att_src, att_dst)):
                    sp.dma_start(att[:, k, :], v.rearrange("(o h) e -> o (h e)", o=1).to_broadcast([P, HE])).then_inc(w_in, 16)
                sp.wait_ge(tab_ok, 1)
                sp.dma_start(tab.rearrange("(t p) c -> p t c", p=P), rows[:]).then_inc(tab_out, 16)
                sp.wait_ge(tab_out, 16)

            @block.vector
            def _(dve):
                step = Chain(dve, dve_step)
                nc.vector.tensor_scalar(E[:], X[:], 0.0, None, ALU.min).then_inc(neg_ok, 1)
                dve.wait_ge(x_in, 16)
                step(nc.vector.scalar_tensor_tensor(out=X[:], in0=X[:], scalar=0.0, in1=Y[:], op0=ALU.max, op1=ALU.add))
                dve.wait_ge(exp_ok, 1)
                step(nc.vector.scalar_tensor_tensor(out=X[:], in0=E[:], scalar=-1.0, in1=X[:], op0=ALU.add, op1=ALU.add))
                norm_rows(nc, dve, step, X, Y, E[:], small, var_ok, sqrt_ok, D)
                dve.sem_inc(y_ok, 1)
                for g in range(G):
                    if g % 2:
                        dve.wait_ge(xt_ok, g + 1)
                        nc.vector.tensor_copy(XT[:, 4 * g:4 * g + 4, :], PS[:, g % 2, :].rearrange("p (t d) -> p t d", t=4)).then_inc(xt_out, 1)
                dve.wait_ge(h_ok, 1)
                hrow = PS[:, 2:4, :].rearrange("p b c -> p (b c)")
                nc.vector.tensor_copy(rows[:, :, 0:HE], hrow.rearrange("p (t c) -> p t c", t=T))
                dve.wait_ge(w_in, 48)
                for k in range(2):
                    step(nc.vector.tensor_tensor(prod[:], hrow.rearrange("p (t c) -> p t c", t=T),
                                                 att[:, k, :].unsqueeze(1).to_broadcast([P, T, HE]), ALU.mult))
                    step(nc.vector.tensor_reduce(rows[:, :, HE + k * NH:HE + (k + 1) * NH],
                                                 prod[:].rearrange("p t (h e) -> p t h e", h=NH), AX.X, ALU.add))
                dve.sem_inc(tab_ok, 1)

            @block.scalar
            def _(act):
                act.wait_ge(neg_ok, 1)
                nc.scalar.activation(E[:], E[:], ACT.Exp).then_inc(exp_ok, 1)
                act.wait_ge(var_ok, 1)
                nc.scalar.activation(small[:, 1, :], small[:, 2, :], ACT.Sqrt).then_inc(sqrt_ok, 1)
                for g in range(0, G, 2):
                    act.wait_ge(xt_ok, g + 1)
                    nc.scalar.copy(XT[:, 4 * g:4 * g + 4, :], PS[:, g % 2, :].rearrange("p (t d) -> p t d", t=4)).then_inc(exp_ok, 1)

            @block.tensor
            def _(pe):
                pe.wait_ge(y_ok, 1)
                pe.wait_ge(w_in, 48)

                def turned(g):
                    if g % 2:
                        pe.wait_ge(xt_out, g // 2 + 1)
                    else:
                        pe.wait_ge(exp_ok, g // 2 + 2)

                def project(g):
                    for t in range(4 * g, 4 * g + 4):
                        o = t * HE
                        ins = nc.tensor.matmul(PS[:, 2 + o // BANK, o % BANK:o % BANK + HE], XT[:, t, :], Wg[:], start=True, stop=True)
                    return ins

                for g in range(G):
                    if g >= 2:
                        turned(g - 2)
                    for k in range(4):
                        ins = nc.tensor.transpose(PS[:, g % 2, k * P:(k + 1) * P], Y[:, 4 * g + k, :], ident[:])
                    ins.then_inc(xt_ok, 1)
                    if g:
                        turned(g - 1)
                        project(g - 1)
                turned(G - 1)
                project(G - 1).then_inc(h_ok, 1)


def split_rows(nc, step, pos, rows_per, inv_rows, neg_rows, gap, q_int, rest, flip, q_out, idx_out):
    step(nc.vector.tensor_scalar(q_int, pos, inv_rows, None, ALU.mult))
    step(nc.vector.scalar_tensor_tensor(out=rest, in0=q_int, scalar=neg_rows, in1=pos, op0=ALU.mult, op1=ALU.add))
    step(nc.vector.scalar_tensor_tensor(out=flip, in0=rest, scalar=0.0, in1=q_int, op0=ALU.is_lt, op1=ALU.subtract))
    step(nc.vector.scalar_tensor_tensor(out=q_out, in0=rest, scalar=rows_per, in1=flip, op0=ALU.is_ge, op1=ALU.subtract))
    return nc.vector.scalar_tensor_tensor(out=idx_out, in0=q_out, scalar=gap, in1=pos, op0=ALU.mult, op1=ALU.add)


def sort_edges(nc, ident, edge_index, N, rec, plan, self_idx, self_rec, ctl, endi, endq, cont):
    E = edge_index.shape[1]
    CE = E // P
    NF = N // P
    GC = 8
    LMAX = rec.shape[0] // P
    CHUNK = 128
    TRASH = 2 * N
    FAR = float(1 << 22)
    LOGF = NF.bit_length() - 1
    assert 1 << LOGF == NF and N % (P * NF) == 0
    with Phase(nc, "sort") as ph:
        dstF = ph.sbuf("dstF", [P, CE + GC])
        partB = ph.sbuf("partB", [P, CE + GC], BF16)
        offB = ph.sbuf("offB", [P, CE + GC], BF16)
        recs = ph.sbuf("recs", [P, CE + 2 * GC, 3], I32)
        iotaF = ph.sbuf("iotaF", [P, P], BF16)
        tri = ph.sbuf("tri", [P, P])
        before = ph.sbuf("before", [P, P])
        ones = ph.sbuf("ones", [P, P])
        Lc = ph.sbuf("Lc", [P, 4])
        cnt = ph.sbuf("cnt", [P, 1])
        start1 = ph.sbuf("start1", [P, NF])

        with Phase(nc, "pack") as pk:
            src = pk.sbuf("src", [P, CE], I32)
            V = [pk.sbuf(f"V{k}", [P, CE]) for k in range(2)]
            S = [pk.sbuf(f"S{k}", [P, CE], I32) for k in range(2)]
            M = pk.sbuf("M", [P, CE], I32)
            iota = pk.sbuf("iota", [P, CE])
            scr = pk.sbuf("scr", [P, 6])
            scri = pk.sbuf("scri", [P, 4], I32)
            PS = pk.psum("ps", [P, 2, BANK])
            e_in, made, z_ok, step_p, dve_step, cnt_ok, tot_ok, fill_ok, fill_out = pk.sems(
                "e_in", "made", "z_ok", "step_p", "dve_step", "cnt_ok", "tot_ok", "fill_ok", "fill_out")
            dst = M
            t1 = iota
            with nc.Block() as block:
                @block.sync
                def _(sp):
                    ev = edge_index.rearrange("k (p c) -> k p c", p=P)
                    sp.dma_start(src[:], ev[0]).then_inc(e_in, 16)
                    sp.dma_start(dst[:], ev[1]).then_inc(e_in, 16)
                    sp.wait_ge(fill_ok, 1)
                    rv = rec.rearrange("(p a t) c -> a p (t c)", p=P, a=4)
                    for q in range(4):
                        sp.dma_start(rv[q], S[1][:, 0:LMAX // 2]).then_inc(fill_out, 16)
                    sp.wait_ge(fill_out, 64)

                @block.gpsimd
                def _(pool):
                    c = [0]

                    def link(ins):
                        c[0] += 1
                        ins.then_inc(step_p, 1)
                        pool.wait_ge(step_p, c[0])

                    link(nc.gpsimd.iota(iotaF[:], pattern=[[1, P]], base=0, channel_multiplier=0,
                                        allow_small_or_imprecise_dtypes=True))
                    link(nc.gpsimd.memset(ones[:], 1.0))
                    for m, mult in ((tri, 1), (before, -1)):
                        link(nc.gpsimd.affine_select(out=m[:], in_=ones[:], compare_op=ALU.is_gt, fill=0.0, base=0,
                                                     pattern=[[mult, P]], channel_multiplier=-mult))
                    link(nc.gpsimd.iota(self_rec[:], pattern=[[1, NF], [0, 2]], base=0, channel_multiplier=NF))
                    nc.gpsimd.memset(ones[:], 1.0).then_inc(made, 1)
                    pool.wait_ge(z_ok, 1)
                    nc.gpsimd.iota(iota[:], pattern=[[1, CE]], base=0, channel_multiplier=0,
                                   allow_small_or_imprecise_dtypes=True).then_inc(made, 1)

                @block.vector
                def _(dve):
                    step = Chain(dve, dve_step)
                    half = [v[:].bitcast(U16).rearrange("p (c k) -> p c k", k=2) for v in V]
                    fill = S[1][:, 0:LMAX // 2].rearrange("p (t c) -> p t c", c=2)
                    step(nc.vector.memset(fill[:, :, 0], N))
                    step(nc.vector.memset(fill[:, :, 1], 0))
                    dve.sem_inc(fill_ok, 1)
                    dve.wait_ge(e_in, 32)
                    step(nc.vector.tensor_scalar(t1[:], src[:], 0.0, float(N), ALU.is_lt, ALU.mult))
                    step(nc.vector.tensor_tensor(t1[:], t1[:], src[:], ALU.add))
                    step(nc.vector.tensor_scalar(half[0][:, :, 0], t1[:], 0.0, float(N - 1), ALU.max, ALU.min))
                    step(nc.vector.tensor_scalar(t1[:], dst[:], 0.0, float(N), ALU.is_lt, ALU.mult))
                    step(nc.vector.tensor_tensor(t1[:], t1[:], dst[:], ALU.add))
                    inv, run = V[1], dstF[:, 0:CE]
                    step(nc.vector.tensor_scalar(inv[:], t1[:], 0.0, None, ALU.is_ge))
                    step(nc.vector.scalar_tensor_tensor(out=inv[:], in0=t1[:], scalar=float(N - 1), in1=inv[:], op0=ALU.is_le, op1=ALU.mult))
                    step(nc.vector.tensor_scalar(t1[:], t1[:], 0.0, float(N - 1), ALU.max, ALU.min))
                    step(nc.vector.tensor_scalar(half[0][:, :, 1], t1[:], 16384.0, None, ALU.add))
                    step(nc.vector.tensor_scalar(t1[:], inv[:], -1.0, 1.0, ALU.mult, ALU.add))
                    step(nc.vector.tensor_tensor_scan(run, t1[:], t1[:], 0.0, ALU.add, ALU.max))
                    step(nc.vector.tensor_scalar(cnt[:], dstF[:, CE - 1:CE], -1.0, float(CE), ALU.mult, ALU.add))
                    dve.sem_inc(cnt_ok, 1)
                    step(nc.vector.tensor_tensor(S[0][:], run, inv[:], ALU.mult))
                    dve.wait_ge(fill_out, 64)
                    a = 0
                    for k in range(CE.bit_length() - 1):
                        far, b = 1 << k, 1 - a
                        step(nc.vector.tensor_scalar(M[:], S[a][:], far, None, ALU.bitwise_and))
                        step(nc.vector.scalar_tensor_tensor(out=S[b][:], in0=M[:], scalar=0.0, in1=S[a][:], op0=ALU.is_equal, op1=ALU.mult))
                        step(nc.vector.copy_predicated(S[b][:, 0:CE - far], M[:, far:CE], S[a][:, far:CE]))
                        step(nc.vector.tensor_copy(V[b][:], V[a][:]))
                        step(nc.vector.copy_predicated(V[b][:, 0:CE - far], M[:, far:CE], V[a][:, far:CE]))
                        a = b
                    dve.sem_inc(z_ok, 1)
                    dve.wait_ge(made, 2)
                    step(nc.vector.tensor_scalar(iota[:], iota[:], cnt[:], float(TRASH), ALU.is_ge, ALU.mult))
                    step(nc.vector.tensor_scalar(V[1 - a][:], half[a][:, :, 1], -16384.0, None, ALU.add))
                    step(nc.vector.tensor_tensor(dstF[:, 0:CE], V[1 - a][:], iota[:], ALU.max))
                    step(nc.vector.memset(dstF[:, CE:CE + GC], float(TRASH)))
                    step(nc.vector.tensor_copy(S[0][:], dstF[:, 0:CE]))
                    step(nc.vector.memset(recs[:, CE:CE + 2 * GC, :], 0))
                    step(nc.vector.tensor_copy(recs[:, 0:CE, 0], dstF[:, 0:CE]))
                    step(nc.vector.tensor_copy(recs[:, 0:CE, 1], half[a][:, :, 0]))
                    step(nc.vector.tensor_scalar(M[:], S[0][:], LOGF, None, ALU.arith_shift_right))
                    step(nc.vector.tensor_copy(partB[:, 0:CE], M[:]))
                    step(nc.vector.memset(partB[:, CE:CE + GC], float(TRASH // NF)))
                    step(nc.vector.tensor_scalar(M[:], S[0][:], NF - 1, None, ALU.bitwise_and))
                    step(nc.vector.tensor_copy(offB[:, 0:CE], M[:]))
                    step(nc.vector.memset(offB[:, CE:CE + GC], 0.0))
                    dve.wait_ge(tot_ok, 1)
                    step(nc.vector.tensor_scalar(scr[:, 1:2], PS[:, 0, 0:1], float(N + P * CHUNK - 1), None, ALU.add))
                    step(nc.vector.tensor_copy(scri[:, 0:1], scr[:, 1:2]))
                    step(nc.vector.tensor_scalar(scri[:, 1:2], scri[:, 0:1], (P * CHUNK).bit_length() - 1, None, ALU.arith_shift_right))
                    step(nc.vector.tensor_scalar(Lc[:, 0:1], scri[:, 1:2], float(CHUNK), None, ALU.mult))
                    step(nc.vector.reciprocal(Lc[:, 1:2], Lc[:, 0:1]))
                    step(nc.vector.tensor_scalar(Lc[:, 2:3], Lc[:, 0:1], -1.0, None, ALU.mult))
                    step(nc.vector.tensor_scalar(Lc[:, 3:4], Lc[:, 0:1], -1.0, float(LMAX), ALU.mult, ALU.add))
                    step(nc.vector.tensor_copy(ctl[0:1, 1:2], scri[0:1, 1:2]))
                    step(nc.vector.tensor_scalar(ctl[0:1, 2:3], scri[0:1, 1:2], -1.0, float(LMAX // CHUNK), ALU.mult, ALU.add))
                    step(nc.vector.tensor_reduce(scr[0:1, 2:3], PS[0:1, 1, 0:P], AX.X, ALU.max))
                    step(nc.vector.tensor_scalar(scr[0:1, 3:4], scr[0:1, 2:3], 1.0, float(2 * GC - 1), ALU.max, ALU.add))
                    step(nc.vector.tensor_copy(scri[0:1, 2:3], scr[0:1, 3:4]))
                    step(nc.vector.tensor_scalar(ctl[0:1, 0:1], scri[0:1, 2:3], (2 * GC).bit_length() - 1, None, ALU.arith_shift_right))

                @block.tensor
                def _(pe):
                    pe.wait_ge(cnt_ok, 1)
                    pe.wait_ge(made, 1)
                    nc.tensor.matmul(PS[:, 0, 0:1], ones[:], cnt[:], start=True, stop=True)
                    nc.tensor.transpose(PS[0:1, 1, 0:P], cnt[:], ident[:]).then_inc(tot_ok, 1)

        with Phase(nc, "count") as pc:
            OF = [pc.sbuf(f"OF{k}", [P, GC, NF], BF16) for k in range(2)]
            OP = [pc.sbuf(f"OP{k}", [P, GC, P], BF16) for k in range(2)]
            w = pc.sbuf("w", [P, 8, NF])
            wi = pc.sbuf("wi", [P, NF], I32)
            tot = pc.sbuf("tot", [P, 2])
            zero = pc.sbuf("zero", [P, P], BF16)
            HIST = pc.psum("hist", [P, BANK])
            BASE = pc.psum("base", [P, BANK])
            hot, counted, hist_ok, tot_ok, base_ok, dve_step, zero_ok = pc.sems(
                "hot", "counted", "hist_ok", "tot_ok", "base_ok", "dve_step", "zero_ok")
            with nc.Block() as block:
                @block.vector
                def _(dve):
                    groups = dve.value_load(ctl[0:1, 0:1], min_val=1, max_val=CE // (2 * GC))
                    nc.vector.memset(zero[:], 0.0).then_inc(zero_ok, 1)
                    with dve.Fori(0, groups) as i:
                        for b in range(2):
                            dve.wait_ge(counted, 2 * i + b + 1)
                            cols = bass.ds((2 * i + b) * GC, GC)
                            one_hots(nc, OF[b], OP[b], iotaF, offB[:, cols], partB[:, cols], NF, GC)[1].then_inc(hot, 1)
                    dve.wait_ge(hist_ok, 1)
                    step = Chain(dve, dve_step)
                    c1, incl, start, last = w[:, 0, :], w[:, 1, :], w[:, 2, :], w[:, 3, :]
                    step(nc.vector.tensor_scalar(c1, HIST[:, 0:NF], 1.0, None, ALU.add))
                    step(nc.vector.tensor_reduce(tot[:, 0:1], c1, AX.X, ALU.add))
                    dve.sem_inc(tot_ok, 1)
                    dve.wait_ge(base_ok, 1)
                    step(nc.vector.tensor_copy(tot[:, 1:2], BASE[:, 0:1]))
                    step(nc.vector.tensor_tensor_scan(incl, c1, c1, tot[:, 1:2], ALU.add, ALU.max))
                    step(nc.vector.tensor_tensor(start, incl, c1, ALU.subtract))
                    step(nc.vector.tensor_scalar(start1[:], start, 1.0, None, ALU.add))
                    step(nc.vector.tensor_scalar(last, incl, -1.0, None, ALU.add))
                    step(split_rows(nc, step, start, Lc[:, 0:1], Lc[:, 1:2], Lc[:, 2:3], Lc[:, 3:4], wi[:], w[:, 4, :], w[:, 5, :], w[:, 6, :], self_idx[:]))
                    step(split_rows(nc, step, last, Lc[:, 0:1], Lc[:, 1:2], Lc[:, 2:3], Lc[:, 3:4], wi[:], w[:, 4, :], w[:, 5, :], w[:, 6, :], endi[:]))
                    step(nc.vector.tensor_copy(endq[:], w[:, 6, :]))
                    step(nc.vector.scalar_tensor_tensor(out=w[:, 7, :], in0=w[:, 6, :], scalar=Lc[:, 2:3], in1=start, op0=ALU.mult, op1=ALU.add))
                    step(nc.vector.tensor_scalar(cont[:], w[:, 7, :], 0.0, None, ALU.is_lt))

                @block.tensor
                def _(pe):
                    groups = pe.value_load(ctl[0:1, 0:1], min_val=1, max_val=CE // (2 * GC))
                    pe.wait_ge(zero_ok, 1)
                    nc.tensor.matmul(HIST[:, 0:NF], zero[:], zero[:, 0:NF], start=True, stop=False, skip_group_check=True).then_inc(counted, 2)
                    with pe.Fori(0, groups) as i:
                        for b in range(2):
                            pe.wait_ge(hot, 2 * i + b + 1)
                            for c in range(GC):
                                ins = nc.tensor.matmul(HIST[:, 0:NF], OP[b][:, c, :], OF[b][:, c, :], start=False, stop=False, skip_group_check=True)
                            ins.then_inc(counted, 1)
                    nc.tensor.matmul(HIST[:, 0:NF], zero[:], zero[:, 0:NF], start=False, stop=True, skip_group_check=True).then_inc(hist_ok, 1)
                    pe.wait_ge(tot_ok, 1)
                    nc.tensor.matmul(BASE[:, 0:1], tri[:], tot[:, 0:1], start=True, stop=True).then_inc(base_ok, 1)

        with Phase(nc, "place") as pp:
            OF = [pp.sbuf(f"OF{k}", [P, GC, NF], BF16) for k in range(2)]
            OP = [pp.sbuf(f"OP{k}", [P, GC, P], BF16) for k in range(2)]
            OPT = [pp.sbuf(f"OPT{k}", [P, GC, P]) for k in range(2)]
            HS = [pp.sbuf(f"HS{k}", [P, NF]) for k in range(2)]
            dcol = [pp.sbuf(f"dcol{k}", [P, GC]) for k in range(2)]
            hit = pp.sbuf("hit", [P, GC, P])
            pick = pp.sbuf("pick", [P, GC, NF])
            rank = pp.sbuf("rank", [P, 2, GC])
            sel = pp.sbuf("sel", [P, 2, GC])
            pos = pp.sbuf("pos", [P, CE])
            m = pp.sbuf("m", [P, 3, CE])
            mi = pp.sbuf("mi", [P, CE], I32)
            identB = pp.sbuf("identB", [P, P], BF16)
            TB = pp.psum("tb", [P, GC * P], BF16)
            DD = [pp.psum(f"dd{k}", [P, GC * P]) for k in range(2)]
            LK = [pp.psum(f"lk{k}", [P, GC, NF]) for k in range(2)]
            HR = pp.psum("hr", [P, BANK])
            hot, ttd, optd, ddd, hcopy, hupd, looked, placed, dve_step, id_ok = pp.sems(
                "hot", "ttd", "optd", "ddd", "hcopy", "hupd", "looked", "placed", "dve_step", "id_ok")
            passed, end_step, plan_ok, plan_out = pp.sems("passed", "end_step", "plan_ok", "plan_out")
            STEPS = GC + GC
            self_out = pp.sem("self_out")
            with nc.Block() as block:
                @block.gpsimd
                def _(pool):
                    for f in range(2, NF):
                        pool.indirect_dma_start(rec, bass.IndirectOffsetOnAxis(ap=self_idx[:, f:f + 1], axis=0),
                                                self_rec[:, f, :], None).then_inc(self_out, 16)
                    pool.wait_ge(self_out, 16 * (NF - 2))

                @block.sync
                def _(sp):
                    sp.wait_ge(plan_ok, 1)
                    sp.dma_start(plan, recs[:]).then_inc(plan_out, 16)
                    sp.wait_ge(plan_out, 16)

                @block.vector
                def _(dve):
                    groups = dve.value_load(ctl[0:1, 0:1], min_val=1, max_val=CE // (2 * GC))
                    nc.vector.tensor_copy(identB[:], ident[:]).then_inc(id_ok, 1)
                    dve.sem_inc(dve_step, 1)
                    nc.vector.memset(pos[:], 0.0).then_inc(end_step, 1)
                    dve.wait_ge(end_step, 1)
                    placed_all = dve.snap(groups * 2)
                    def build(g, b):
                        cols = bass.ds(g * GC, GC)
                        one_hots(nc, OF[b], OP[b], iotaF, offB[:, cols], partB[:, cols], NF, GC)
                        nc.vector.tensor_copy(dcol[b][:], dstF[:, cols]).then_inc(hot, 1)

                    def consume(step, g, i, b):
                        cols = bass.ds(g * GC, GC)
                        dve.wait_ge(ddd, g + 1)
                        for c in range(GC):
                            a = step(nc.vector.scalar_tensor_tensor(
                                out=hit[:, c, :], in0=DD[b][:, c * P:(c + 1) * P], scalar=dcol[b][:, c:c + 1], in1=before[:],
                                op0=ALU.is_equal, op1=ALU.mult, accum_out=rank[:, b, c:c + 1]))
                        dve.wait_ge(looked, (g + 1) * GC)
                        for c in range(GC):
                            a = step(nc.vector.tensor_tensor_reduce(pick[:, c, :], LK[b][:, c, :], OF[b][:, c, :], 1.0, 0.0,
                                                                    ALU.mult, ALU.add, sel[:, b, c:c + 1]))
                        step.eng.wait_ge(dve_step, a)
                        nc.vector.tensor_tensor(pos[:, cols], sel[:, b, :], rank[:, b, :], ALU.add).then_inc(placed, 1)

                    build(0, 0)
                    with dve.Fori(0, groups) as i:
                        step = LoopSteps(dve, dve_step, i * (2 * STEPS) + 1)
                        for b in range(2):
                            g = 2 * i + b
                            dve.wait_ge(hupd, g * GC + 1)
                            dve.wait_ge(dve_step, g * STEPS + 1)
                            build(g + 1, 1 - b)
                            consume(step, g, i, b)
                        assert step.n == 2 * STEPS, step.n
                    dve.wait_ge(placed, placed_all)
                    dve.sem_inc(passed, 1)
                    end = Chain(dve, end_step)
                    end.n = 1
                    end(nc.vector.tensor_scalar(m[:, 0, :], dstF[:, 0:CE], float(N), FAR, ALU.is_ge, ALU.mult))
                    end(nc.vector.tensor_tensor(pos[:], pos[:], m[:, 0, :], ALU.add))
                    end(split_rows(nc, end, pos[:], Lc[:, 0:1], Lc[:, 1:2], Lc[:, 2:3], Lc[:, 3:4], mi[:],
                                   m[:, 0, :], m[:, 1, :], m[:, 2, :], recs[:, 0:CE, 2]))
                    dve.sem_inc(plan_ok, 1)

                @block.scalar
                def _(act):
                    groups = act.value_load(ctl[0:1, 0:1], min_val=1, max_val=CE // (2 * GC))
                    act.sem_inc(optd, 1)
                    with act.Fori(0, groups) as i:
                        for b in range(2):
                            g = 2 * i + b
                            act.wait_ge(ttd, g + 1)
                            nc.scalar.copy(OPT[b][:].rearrange("p c e -> p (c e)"), TB[:]).then_inc(optd, 1)
                            for c in range(GC):
                                act.wait_ge(hupd, g * GC + c + 1)
                                nc.scalar.copy(HS[c % 2][:], HR[:, 0:NF]).then_inc(hcopy, 1)

                @block.tensor
                def _(pe):
                    groups = pe.value_load(ctl[0:1, 0:1], min_val=1, max_val=CE // (2 * GC))
                    pe.wait_ge(id_ok, 1)
                    nc.tensor.matmul(HR[:, 0:NF], ident[:], start1[:], start=True, stop=False, skip_group_check=True).then_inc(hupd, 1)
                    with pe.Fori(0, groups) as i:
                        for b in range(2):
                            g = 2 * i + b
                            pe.wait_ge(hot, g + 1)
                            pe.wait_ge(optd, g + 1)
                            for c in range(GC):
                                ins = nc.tensor.transpose(TB[:, c * P:(c + 1) * P], OP[b][:, c, :], identB[:])
                            ins.then_inc(ttd, 1)
                            for c in range(GC):
                                ins = nc.tensor.matmul(DD[b][:, c * P:(c + 1) * P], dcol[b][:, c:c + 1].to_broadcast([P, P]),
                                                       ident[:], start=True, stop=True)
                            ins.then_inc(ddd, 1)
                            pe.wait_ge(optd, g + 2)
                            for c in range(GC):
                                pe.wait_ge(hcopy, g * GC + c + 1)
                                nc.tensor.matmul(HR[:, 0:NF], OP[b][:, c, :], OF[b][:, c, :], start=False, stop=False,
                                                 skip_group_check=True).then_inc(hupd, 1)
                                nc.tensor.matmul(LK[b][:, c, :], OPT[b][:, c, :], HS[c % 2][:], start=True, stop=True).then_inc(looked, 1)


def scatter_records(nc, pool, ph, rec, plan, self_idx, self_rec, ctl):
    HC = 8
    GROUP = 2 * HC
    LAST = rec.shape[0] - 1
    SELF = 16
    ahead = ph.sbuf("ahead", [P, GROUP, 3], I32)
    part = [ph.sbuf(f"part{h}", [P, HC, 3], I32) for h in range(2)]
    ahead_in, copied, passed = ph.sem("ahead_in"), ph.sem("part_copied"), ph.sem("scat_passed")
    scat = [ph.sem(f"scat{h}") for h in range(2)]
    groups = pool.value_load(ctl[0:1, 0:1], min_val=1, max_val=(plan.shape[1] - GROUP) // GROUP)
    pool.dma_start(ahead[:], plan[:, 0:GROUP, :]).then_inc(ahead_in, 16)
    for f in range(2):
        pool.indirect_dma_start(rec, bass.IndirectOffsetOnAxis(ap=self_idx[:, f:f + 1], axis=0),
                                self_rec[:, f, :], None).then_inc(scat[f], 16)
    with pool.Fori(0, groups) as i:
        pool.wait_ge(ahead_in, i * 16 + 16)
        pool.sem_inc(passed, 1)
        for h in range(2):
            pool.wait_ge(scat[h], i * (16 * HC) + SELF)
            pool.sem_inc(passed, 1)
            nc.gpsimd.tensor_copy(part[h][:], ahead[:, h * HC:(h + 1) * HC, :]).then_inc(copied, 1)
            pool.wait_ge(copied, 2 * i + h + 1)
            pool.sem_inc(passed, 1)
            if h:
                pool.dma_start(ahead[:], plan[:, bass.ds((i + 1) * GROUP, GROUP), :]).then_inc(ahead_in, 16)
            for c in range(HC):
                pool.indirect_dma_start(rec, bass.IndirectOffsetOnAxis(ap=part[h][:, c, 2:3], axis=0),
                                        part[h][:, c, 0:2], None, bounds_check=LAST, oob_is_err=False).then_inc(scat[h], 16)
    scattered = pool.snap(groups * (16 * HC) + SELF)
    loaded = pool.snap(groups * 16 + 16)
    for h in range(2):
        pool.wait_ge(scat[h], scattered)
        pool.sem_inc(passed, 1)
    pool.wait_ge(ahead_in, loaded)
    pool.sem_inc(passed, 1)


def one_hots(nc, off_hot, part_hot, iota, off, part, NF, GC):
    return (nc.vector.tensor_tensor(off_hot[:], iota[:, 0:NF].unsqueeze(1).to_broadcast([P, GC, NF]),
                                    off.unsqueeze(2).to_broadcast([P, GC, NF]), ALU.is_equal),
            nc.vector.tensor_tensor(part_hot[:], iota[:].unsqueeze(1).to_broadcast([P, GC, P]),
                                    part.unsqueeze(2).to_broadcast([P, GC, P]), ALU.is_equal))


def top_two(nc, step, score, left, sel, best, free):
    NE = score.shape[2]
    T = score.shape[1]
    src = score
    for k in range(2):
        step(nc.vector.tensor_reduce(best[:, k, :], src, AX.X, ALU.max))
        step(nc.vector.tensor_tensor(sel[k], src, best[:, k, :].unsqueeze(2).to_broadcast([P, T, NE]), ALU.is_equal))
        step(nc.vector.memset(free, 1.0))
        for e in range(NE):
            step(nc.vector.tensor_tensor(sel[k][:, :, e], sel[k][:, :, e], free, ALU.mult))
            if e < NE - 1:
                step(nc.vector.tensor_tensor(free, free, sel[k][:, :, e], ALU.subtract))
        if k == 0:
            step(nc.vector.scalar_tensor_tensor(out=left, in0=sel[0], scalar=-LOW, in1=score, op0=ALU.mult, op1=ALU.add))
            src = left


def gate_nodes(nc, ident, rec, tab, runs, carry, ctl, endi, endq, cont, b_gat, ln_gamma, ln_beta, gates):
    N, TW = tab.shape
    NE = gates.shape[1]
    HE = b_gat.shape[0]
    NH = HE // NE
    NF = N // P
    S = NH + HE
    W = NH + S
    LMAX = rec.shape[0] // P
    CK = 64
    rv = rec.rearrange("(p t) c -> p t c", p=P)
    nv = runs.rearrange("(p t) c -> p t c", p=P)
    with Phase(nc, "gat") as ph:
        state = ph.sbuf("state", [P, W])
        lastd = ph.sbuf("lastd", [P, 1])
        with Phase(nc, "runs") as pr:
            RC = [pr.sbuf(f"RC{k}", [P, CK, 2], I32) for k in range(2)]
            GT = [pr.sbuf(f"GT{k}", [P, CK, TW]) for k in range(2)]
            RN = [pr.sbuf(f"RN{k}", [P, CK + 1, W]) for k in range(2)]
            HOLD = [pr.sbuf(f"HOLD{k}", [P, CK + 1, NH]) for k in range(2)]
            DF = [pr.sbuf(f"DF{k}", [P, CK + 1]) for k in range(2)]
            flag = pr.sbuf("flag", [P, 3, CK])
            own = pr.sbuf("own", [P, CK, NH])
            lg = pr.sbuf("lg", [P, CK, NH])
            ex = pr.sbuf("ex", [P, 2, CK, NH])
            wt = pr.sbuf("wt", [P, CK, HE])
            first = pr.sbuf("first", [P, 2], I32)
            firsti = pr.sbuf("firsti", [P, 1], I32)
            firstg = pr.sbuf("firstg", [P, 2, TW])
            zeros = pr.sbuf("zeros", [P, 2 * CK, W])
            first_in, firsti_ok, rc_read, dve_step, ex_ok, exp_ok, run_ok = pr.sems(
                "first_in", "firsti_ok", "rc_read", "dve_step", "ex_ok", "exp_ok", "run_ok")
            passed, fill_ok, fill_out = pr.sems("passed", "fill_ok", "fill_out")
            rc_in = [pr.sem(f"rc_in{k}") for k in range(2)]
            gt_in = [pr.sem(f"gt_in{k}") for k in range(2)]
            rn_out = [pr.sem(f"rn_out{k}") for k in range(2)]
            START, STEPS = 6, 12 + 3 * NH + HE
            with nc.Block() as block:
                @block.sync
                def _(sp):
                    pairs = sp.value_load(ctl[0:1, 1:2], min_val=1, max_val=LMAX // (2 * CK) - 1)
                    sp.dma_start(first[:], rv[:, 0, :]).then_inc(first_in, 16)
                    with sp.Fori(0, pairs) as i:
                        for b in range(2):
                            k = 2 * i + b
                            sp.wait_ge(gt_in[b], i * (16 * CK) + 16)
                            sp.sem_inc(passed, 1)
                            sp.wait_ge(rc_read, k + 1)
                            sp.sem_inc(passed, 1)
                            sp.dma_start(RC[b][:], rv[:, bass.ds(k * CK, CK), :]).then_inc(rc_in[b], 16)
                    rest = sp.value_load(ctl[0:1, 2:3], min_val=1, max_val=LMAX // (2 * CK))
                    filled = sp.snap(rest * 16)
                    sp.wait_ge(fill_ok, 1)
                    with sp.Fori(pairs, LMAX // (2 * CK)) as i:
                        sp.dma_start(nv[:, bass.ds(i * (2 * CK), 2 * CK), :], zeros[:]).then_inc(fill_out, 16)
                    sp.wait_ge(fill_out, filled)
                    sp.sem_inc(passed, 1)

                @block.gpsimd
                def _(pool):
                    pairs = pool.value_load(ctl[0:1, 1:2], min_val=1, max_val=LMAX // (2 * CK) - 1)
                    nc.gpsimd.memset(zeros[:], 0.0).then_inc(fill_ok, 1)
                    pool.wait_ge(firsti_ok, 1)
                    for b in range(2):
                        pool.indirect_dma_start(firstg[:, b, :], None, tab, bass.IndirectOffsetOnAxis(ap=firsti[:], axis=0)).then_inc(gt_in[b], 16)
                    with pool.Fori(0, pairs) as i:
                        for b in range(2):
                            k = 2 * i + b
                            pool.wait_ge(run_ok, k + 1)
                            pool.wait_ge(rc_in[b], i * 16 + 16)
                            pool.sem_inc(passed, 1)
                            for c in range(CK):
                                pool.indirect_dma_start(GT[b][:, c, :], None, tab,
                                                        bass.IndirectOffsetOnAxis(ap=RC[b][:, c, 1:2], axis=0)).then_inc(gt_in[b], 16)

                @block.vector
                def _(dve):
                    pairs = dve.value_load(ctl[0:1, 1:2], min_val=1, max_val=LMAX // (2 * CK) - 1)
                    step = LoopSteps(dve, dve_step)
                    dve.wait_ge(first_in, 16)
                    step.now(nc.vector.tensor_scalar(firsti[:], first[:, 0:1], float(N - 1), None, ALU.min))
                    nc.vector.memset(RN[1][:, CK, 0:NH], -LOW).then_inc(firsti_ok, 1)
                    step(nc.vector.memset(RN[1][:, CK, NH:W], 0.0))
                    step(nc.vector.tensor_copy(DF[1][:, CK:CK + 1], first[:, 0:1]))
                    step(nc.vector.memset(flag[:], 0.0))
                    dve.wait_ge(gt_in[0], 16)
                    step(nc.vector.tensor_copy(HOLD[1][:, CK, :], firstg[:, 0, HE + NH:TW]))
                    step.now(nc.vector.memset(own[:], 0.0))
                    nc.vector.memset(lg[:], 0.0).then_inc(rc_read, 2)
                    nc.vector.memset(ex[:], 0.0).then_inc(run_ok, 2)
                    for b in range(2):
                        dve.sem_inc(rn_out[b], 1)
                    assert step.n == START
                    with dve.Fori(0, pairs) as i:
                        step = LoopSteps(dve, dve_step, START + i * (2 * STEPS))
                        now = step.now
                        for b in range(2):
                            k = 2 * i + b
                            dve.wait_ge(rc_in[b], i * 16 + 16)
                            dve.wait_ge(rn_out[b], i * 16 + 1)
                            nc.vector.tensor_copy(DF[b][:, 1:CK + 1], RC[b][:, :, 0]).then_inc(rc_read, 1)
                            step(nc.vector.tensor_copy(DF[b][:, 0:1], DF[1 - b][:, CK:CK + 1]))
                            now(nc.vector.tensor_copy(RN[b][:, 0, :], RN[1 - b][:, CK, :]))
                            now(nc.vector.tensor_tensor(flag[:, 0, :], DF[b][:, 1:CK + 1], DF[b][:, 0:CK], ALU.not_equal))
                            step(nc.vector.tensor_scalar(flag[:, 1, :], flag[:, 0, :], -1.0, 1.0, ALU.mult, ALU.add))
                            step(nc.vector.tensor_scalar(flag[:, 2, :], flag[:, 0, :], -LOW, None, ALU.mult))
                            dve.wait_ge(gt_in[b], i * (16 * CK) + 16 * CK + 16)
                            now(nc.vector.tensor_tensor(own[:], GT[b][:, :, HE + NH:TW],
                                                        flag[:, 0, :].unsqueeze(2).to_broadcast([P, CK, NH]), ALU.mult))
                            for h in range(NH):
                                a = step(nc.vector.tensor_tensor_scan(HOLD[b][:, 1:CK + 1, h], flag[:, 1, :], own[:, :, h],
                                                                      HOLD[1 - b][:, CK, h:h + 1], ALU.mult, ALU.add))
                            dve.wait_ge(dve_step, a)
                            now(nc.vector.tensor_tensor(own[:], GT[b][:, :, HE:HE + NH], HOLD[b][:, 1:CK + 1, :], ALU.add))
                            now(nc.vector.scalar_tensor_tensor(out=lg[:], in0=own[:], scalar=0.2, in1=own[:], op0=ALU.mult, op1=ALU.max))
                            for h in range(NH):
                                a = step(nc.vector.tensor_tensor_scan(RN[b][:, 1:CK + 1, h], flag[:, 2, :], lg[:, :, h],
                                                                      RN[1 - b][:, CK, h:h + 1], ALU.add, ALU.max))
                            dve.wait_ge(dve_step, a)
                            step(nc.vector.tensor_tensor(ex[:, 0, :, :], lg[:], RN[b][:, 1:CK + 1, 0:NH], ALU.subtract))
                            now(nc.vector.tensor_tensor(ex[:, 1, :, :], RN[b][:, 0:CK, 0:NH],
                                                        flag[:, 2, :].unsqueeze(2).to_broadcast([P, CK, NH]), ALU.add))
                            now(nc.vector.tensor_tensor(ex[:, 1, :, :], ex[:, 1, :, :], RN[b][:, 1:CK + 1, 0:NH], ALU.subtract))
                            dve.sem_inc(ex_ok, 1)
                            dve.wait_ge(exp_ok, k + 1)
                            now(nc.vector.tensor_tensor(wt[:].rearrange("p c (h e) -> p c h e", h=NH),
                                                        GT[b][:, :, 0:HE].rearrange("p c (h e) -> p c h e", h=NH),
                                                        ex[:, 0, :, :].unsqueeze(3).to_broadcast([P, CK, NH, NE]), ALU.mult))
                            for c in range(S):
                                h = c if c < NH else (c - NH) // NE
                                new = ex[:, 0, :, h] if c < NH else wt[:, :, c - NH]
                                ins = nc.vector.tensor_tensor_scan(RN[b][:, 1:CK + 1, NH + c], ex[:, 1, :, h], new,
                                                                   RN[1 - b][:, CK, NH + c:NH + c + 1], ALU.mult, ALU.add)
                                a = step(ins)
                            dve.wait_ge(dve_step, a)
                            dve.sem_inc(run_ok, 1)
                        assert step.n == 2 * STEPS, step.n
                    nc.vector.tensor_copy(state[:], RN[1][:, CK, :])
                    nc.vector.tensor_copy(lastd[:], DF[1][:, CK:CK + 1])

                @block.scalar
                def _(act):
                    pairs = act.value_load(ctl[0:1, 1:2], min_val=1, max_val=LMAX // (2 * CK) - 1)
                    stored = act.snap(pairs * 16 + 1)
                    with act.Fori(0, pairs) as i:
                        for b in range(2):
                            k = 2 * i + b
                            act.wait_ge(ex_ok, k + 1)
                            nc.scalar.activation(ex[:], ex[:], ACT.Exp).then_inc(exp_ok, 1)
                            act.wait_ge(run_ok, k + 3)
                            act.dma_start(nv[:, bass.ds(k * CK, CK), :], RN[b][:, 1:CK + 1, :]).then_inc(rn_out[b], 16)
                    for b in range(2):
                        act.wait_ge(rn_out[b], stored)
                        act.sem_inc(passed, 1)

        RE = ph.sbuf("RE", [P, NF, W])
        CE = ph.sbuf("CE", [P, NF, 2 * S])
        with Phase(nc, "carry") as pc:
            ends = pc.sbuf("ends", [P, 3, S])
            turned = pc.sbuf("turned", [S, 3, P])
            pen = pc.sbuf("pen", [S, P])
            MC = pc.sbuf("MC", [S, P + 1])
            VC = pc.sbuf("VC", [S, P + 1])
            ex = pc.sbuf("ex", [S, 2, P])
            back = pc.sbuf("back", [P, 2 * S])
            PS = pc.psum("ps", [P, 2, BANK])
            dve_step, ends_ok, turned_ok, ex_ok, exp_ok, handed_ok, back_ok, back_sb, carry_out, run_in, carry_in = pc.sems(
                "dve_step", "ends_ok", "turned_ok", "ex_ok", "exp_ok", "handed_ok", "back_ok", "back_sb", "carry_out", "run_in", "carry_in")
            with nc.Block() as block:
                @block.vector
                def _(dve):
                    step = Chain(dve, dve_step)
                    step(nc.vector.tensor_copy(ends[:, 0, 0:NH], state[:, 0:NH]))
                    step(nc.vector.tensor_copy(ends[:, 0, NH:S].rearrange("p (h e) -> p h e", h=NH),
                                               state[:, 0:NH].unsqueeze(2).to_broadcast([P, NH, NE])))
                    step(nc.vector.tensor_copy(ends[:, 1, :], state[:, NH:W]))
                    step(nc.vector.tensor_copy(ends[:, 2, :], lastd[:].to_broadcast([P, S])))
                    nc.vector.memset(pen[:, 0:1], -LOW).then_inc(ends_ok, 1)
                    dve.wait_ge(turned_ok, 1)
                    step(nc.vector.tensor_copy(turned[:], PS[0:S, 0, 0:3 * P].rearrange("p (k m) -> p k m", k=3)))
                    m, v, d = turned[:, 0, :], turned[:, 1, :], turned[:, 2, :]
                    step(nc.vector.tensor_tensor(pen[:, 1:P], d[:, 1:P], d[:, 0:P - 1], ALU.not_equal))
                    step(nc.vector.tensor_scalar(pen[:, 1:P], pen[:, 1:P], -LOW, None, ALU.mult))
                    step(nc.vector.memset(MC[:, 0:1], -LOW))
                    step(nc.vector.memset(VC[:, 0:1], 0.0))
                    step(nc.vector.tensor_tensor_scan(MC[:, 1:P + 1], pen[:], m, MC[:, 0:1], ALU.add, ALU.max))
                    step(nc.vector.tensor_tensor(ex[:, 0, :], m, MC[:, 1:P + 1], ALU.subtract))
                    step(nc.vector.tensor_tensor(ex[:, 1, :], MC[:, 0:P], pen[:], ALU.add))
                    step(nc.vector.tensor_tensor(ex[:, 1, :], ex[:, 1, :], MC[:, 1:P + 1], ALU.subtract))
                    dve.sem_inc(ex_ok, 1)
                    dve.wait_ge(exp_ok, 1)
                    step(nc.vector.tensor_tensor(ex[:, 0, :], ex[:, 0, :], v, ALU.mult))
                    nc.vector.tensor_tensor_scan(VC[:, 1:P + 1], ex[:, 1, :], ex[:, 0, :], 0.0, ALU.mult, ALU.add).then_inc(handed_ok, 1)
                    dve.wait_ge(back_ok, 1)
                    nc.vector.tensor_copy(back[:], PS[:, 1, 0:2 * S]).then_inc(back_sb, 1)

                @block.scalar
                def _(act):
                    act.wait_ge(ex_ok, 1)
                    nc.scalar.activation(ex[:], ex[:], ACT.Exp).then_inc(exp_ok, 1)

                @block.tensor
                def _(pe):
                    pe.wait_ge(ends_ok, 1)
                    for k in range(3):
                        ins = nc.tensor.transpose(PS[0:S, 0, k * P:(k + 1) * P], ends[:, k, :], ident[:])
                    ins.then_inc(turned_ok, 1)
                    pe.wait_ge(handed_ok, 1)
                    nc.tensor.transpose(PS[:, 1, 0:S], MC[:, 0:P], ident[0:S, 0:S])
                    nc.tensor.transpose(PS[:, 1, S:2 * S], VC[:, 0:P], ident[0:S, 0:S]).then_inc(back_ok, 1)

                @block.sync
                def _(sp):
                    sp.wait_ge(back_sb, 1)
                    sp.dma_start(carry, back[:]).then_inc(carry_out, 16)
                    sp.wait_ge(carry_out, 16)

                @block.gpsimd
                def _(pool):
                    for f in range(NF):
                        pool.indirect_dma_start(RE[:, f, :], None, runs, bass.IndirectOffsetOnAxis(ap=endi[:, f:f + 1], axis=0)).then_inc(run_in, 16)
                    pool.wait_ge(carry_out, 16)
                    for f in range(NF):
                        pool.indirect_dma_start(CE[:, f, :], None, carry, bass.IndirectOffsetOnAxis(ap=endq[:, f:f + 1], axis=0)).then_inc(carry_in, 16)
                    pool.wait_ge(run_in, 16 * NF)
                    pool.wait_ge(carry_in, 16 * NF)

        with Phase(nc, "node") as pn:
            par = pn.sbuf("par", [P, 3, HE])
            cm = pn.sbuf("cm", [P, NF, NH])
            mm = pn.sbuf("mm", [P, NF, NH])
            ex = pn.sbuf("ex", [P, 2, NF, NH])
            sm = pn.sbuf("sm", [P, NF, NH])
            agg = pn.sbuf("agg", [P, NF, HE])
            tmp = pn.sbuf("tmp", [P, NF, HE])
            small = pn.sbuf("small", [P, 3, NF])
            sc = pn.sbuf("sc", [P, NF, NE])
            left = pn.sbuf("left", [P, NF, NE])
            sel = [pn.sbuf(f"sel{k}", [P, NF, NE]) for k in range(2)]
            best = pn.sbuf("best", [P, 2, NF])
            free = pn.sbuf("free", [P, NF])
            g2 = pn.sbuf("g2", [P, 2, NF])
            par_in, dve_step, ex_ok, exp_ok, var_ok, sqrt_ok, top_ok, top_exp, gates_ok, gates_out = pn.sems(
                "par_in", "dve_step", "ex_ok", "exp_ok", "var_ok", "sqrt_ok", "top_ok", "top_exp", "gates_ok", "gates_out")
            with nc.Block() as block:
                @block.sync
                def _(sp):
                    for k, v in enumerate((b_gat, ln_gamma, ln_beta)):
                        sp.dma_start(par[:, k, :], v.rearrange("(o c) -> o c", o=1).to_broadcast([P, HE])).then_inc(par_in, 16)
                    sp.wait_ge(gates_ok, 1)
                    sp.dma_start(gates.rearrange("(p f) e -> p f e", p=P), sc[:]).then_inc(gates_out, 16)
                    sp.wait_ge(gates_out, 16)

                @block.vector
                def _(dve):
                    step = Chain(dve, dve_step)

                    def heads(x):
                        return x.rearrange("p f (h e) -> p f h e", h=NH)

                    def over(x):
                        return x.unsqueeze(3).to_broadcast([P, NF, NH, NE])

                    def row(k):
                        return par[:, k, :].unsqueeze(1).to_broadcast([P, NF, HE])

                    step(nc.vector.tensor_scalar(free[:], cont[:], LOW, -LOW, ALU.mult, ALU.add))
                    step(nc.vector.tensor_tensor(cm[:], CE[:, :, 0:NH], free[:].unsqueeze(2).to_broadcast([P, NF, NH]), ALU.add))
                    step(nc.vector.tensor_tensor(mm[:], RE[:, :, 0:NH], cm[:], ALU.max))
                    step(nc.vector.tensor_tensor(ex[:, 0], RE[:, :, 0:NH], mm[:], ALU.subtract))
                    step(nc.vector.tensor_tensor(ex[:, 1], cm[:], mm[:], ALU.subtract))
                    dve.sem_inc(ex_ok, 1)
                    dve.wait_ge(exp_ok, 1)
                    step(nc.vector.tensor_tensor(sm[:], RE[:, :, NH:2 * NH], ex[:, 0], ALU.mult))
                    step(nc.vector.tensor_tensor(cm[:], CE[:, :, S:S + NH], ex[:, 1], ALU.mult))
                    step(nc.vector.tensor_tensor(sm[:], sm[:], cm[:], ALU.add))
                    step(nc.vector.tensor_scalar(sm[:], sm[:], 1e-16, None, ALU.add))
                    step(nc.vector.reciprocal(sm[:], sm[:]))
                    step(nc.vector.tensor_tensor(heads(agg[:]), heads(RE[:, :, 2 * NH:W]), over(ex[:, 0]), ALU.mult))
                    step(nc.vector.tensor_tensor(heads(tmp[:]), heads(CE[:, :, S + NH:2 * S]), over(ex[:, 1]), ALU.mult))
                    step(nc.vector.tensor_tensor(agg[:], agg[:], tmp[:], ALU.add))
                    step(nc.vector.tensor_tensor(heads(agg[:]), heads(agg[:]), over(sm[:]), ALU.mult))
                    dve.wait_ge(par_in, 48)
                    step(nc.vector.tensor_tensor(agg[:], agg[:], row(0), ALU.add))
                    norm_rows(nc, dve, step, agg, agg, tmp[:], small, var_ok, sqrt_ok, HE)
                    step(nc.vector.tensor_tensor(agg[:], agg[:], row(1), ALU.mult))
                    step(nc.vector.tensor_tensor(agg[:], agg[:], row(2), ALU.add))
                    step(nc.vector.tensor_reduce(sc[:], agg[:].rearrange("p f (h e) -> p f e h", h=NH), AX.X, ALU.add))
                    step(nc.vector.tensor_scalar(sc[:], sc[:], 1.0 / NH, None, ALU.mult))
                    top_two(nc, step, sc[:], left[:], [sel[0][:], sel[1][:]], best, free[:])
                    nc.vector.tensor_tensor(g2[:, 1, :], best[:, 1, :], best[:, 0, :], ALU.subtract).then_inc(top_ok, 1)
                    dve.wait_ge(top_exp, 1)
                    step(nc.vector.tensor_scalar(g2[:, 0, :], g2[:, 1, :], 1.0, None, ALU.add))
                    step(nc.vector.reciprocal(g2[:, 0, :], g2[:, 0, :]))
                    step(nc.vector.tensor_tensor(g2[:, 1, :], g2[:, 1, :], g2[:, 0, :], ALU.mult))
                    for k in range(2):
                        step(nc.vector.tensor_tensor(sel[k][:], sel[k][:], g2[:, k, :].unsqueeze(2).to_broadcast([P, NF, NE]), ALU.mult))
                    nc.vector.tensor_tensor(sc[:], sel[0][:], sel[1][:], ALU.add).then_inc(gates_ok, 1)

                @block.scalar
                def _(act):
                    act.wait_ge(ex_ok, 1)
                    nc.scalar.activation(ex[:], ex[:], ACT.Exp).then_inc(exp_ok, 1)
                    act.wait_ge(var_ok, 1)
                    nc.scalar.activation(small[:, 1, :], small[:, 2, :], ACT.Sqrt).then_inc(sqrt_ok, 1)
                    act.wait_ge(top_ok, 1)
                    nc.scalar.activation(g2[:, 1, :], g2[:, 1, :], ACT.Exp).then_inc(top_exp, 1)


MOST_LEVELS = 1 << 18


class LoopSteps:

    def __init__(self, eng, sem, base=0):
        self.eng, self.sem, self.base, self.n = eng, sem, base, 0

    def __call__(self, ins):
        self.n += 1
        ins.then_inc(self.sem, 1)
        return self.base + self.n

    def now(self, ins):
        self.eng.wait_ge(self.sem, self(ins))


def attend_leaky(nc, adj, adj01, H1, srow, scol, dcol, low, levels, prop, ident, beside):
    D = prop.shape[2]
    T = prop.shape[1]
    N = T * P
    D1 = D + 1
    RT = 2
    R = RT * P
    GB = 2
    JB = 4
    UPG = T // JB
    U = GB * UPG
    NB = T // (RT * GB)
    LAG = 3
    NBUF = 4
    C = N // CW
    M = RT * C
    UPC = UPG // C
    with Phase(nc, "at0") as ph:
        AD = [ph.sbuf(f"adj{b}", [P, CW], I32) for b in range(NBUF)]
        AB = [ph.sbuf(f"a{b}", [P, RT, N], BF16) for b in range(GB)]
        PT = [ph.sbuf(f"pt{b}", [P, JB, R]) for b in range(NBUF)]
        flat = ph.sbuf("flat", [P, T])
        fe = ph.sbuf("fe", [P, 2, T])
        steep = ph.sbuf("steep", [P, T])
        ev = ph.sbuf("ev", [P, T])
        qrow = ph.sbuf("qrow", [P, GB * R])
        enough = ph.sbuf("enough", [P, T])
        todo = ph.sbuf("todo", [P, T])
        res = ph.sbuf("res", [P, RT, D1])
        st = ph.sbuf("st", [P, 3, RT])
        mean = ph.sbuf("mean", [P, D])
        identB = ph.sbuf("identB", [P, P], BF16)
        TP = [ph.psum(f"tp{b}", [P, JB * R], BF16) for b in range(NBUF)]
        OUT = ph.psum("out", [P, GB, RT, BANK])
        start_ok, sum_ok, mean_ok, conv, turned, made, mult, fin, dve_step, ev_ok, exp_ok, q_ok, qexp_ok, low_ok, passed = ph.sems(
            "start_ok", "sum_ok", "mean_ok", "conv", "turned", "made", "mult", "fin", "dve_step", "ev_ok", "exp_ok", "q_ok",
            "qexp_ok", "low_ok", "passed")
        in_b = [ph.sem(f"in{b}") for b in range(NBUF)]
        stored = [ph.sem(f"stored{b}") for b in range(GB)]
        adj_t = adj.rearrange("(t p) (c w) -> t p c w", p=P, w=CW)
        a_g = adj01.rearrange("(g t p) c -> g p t c", p=P, t=RT)
        START, AT_LEVEL, IN_BODY = 2, 7, 1 + U + GB * 9

        def nested(eng, level_start, body):
            n = eng.value_load(levels[0:1, 0:1], min_val=1, max_val=MOST_LEVELS)
            with eng.Fori(0, n) as l:
                if level_start is not None:
                    level_start(l)
                with eng.Fori(0, NB) as i:
                    body(l, i, l * NB + i)
            return n

        with nc.Block() as block:
            @block.gpsimd
            def _(pool):
                beside(pool, ph)

            @block.sync
            def _(sp):
                def body(l, i, q):
                    for x in range(GB):
                        for m in range(M):
                            k = x * M + m
                            sp.wait_ge(conv, q * (GB * M) + k + 1)
                            sp.sem_inc(passed, 1)
                            sp.dma_start(AD[k % NBUF][:], adj_t[i * (GB * RT) + (x * RT + m % RT), :, m // RT, :]).then_inc(in_b[k % NBUF], 16)
                            if m == NBUF and x:
                                store(i, q, x - 1)
                    store(i, q, GB - 1)

                def store(i, q, x):
                    sp.wait_ge(conv, q * (GB * M) + (x + 1) * M + NBUF)
                    sp.sem_inc(passed, 1)
                    sp.dma_start(a_g[i * GB + x], AB[x][:]).then_inc(stored[x], 16)

                n = nested(sp, None, body)
                all_stored = sp.snap(n * (16 * NB) + 16)
                for x in range(GB):
                    sp.wait_ge(stored[x], all_stored)
                    sp.sem_inc(passed, 1)

            @block.scalar
            def _(act):
                def level_start(l):
                    act.wait_ge(ev_ok, l + 1)
                    nc.scalar.activation(flat[:], flat[:], ACT.Exp, scale=0.01)
                    nc.scalar.activation(steep[:], ev[:], ACT.Exp, scale=0.99).then_inc(exp_ok, 1)

                def convert(q, x):
                    act.wait_ge(turned, q * U + (x + 1) * UPG)
                    act.wait_ge(stored[x], q * 16 + 16)
                    for m in range(M):
                        k = x * M + m
                        act.wait_ge(in_b[k % NBUF], q * (16 * GB * M // NBUF) + 16 * (k // NBUF + 1))
                        nc.scalar.copy(AB[x][:, m % RT, (m // RT) * CW:(m // RT + 1) * CW], AD[k % NBUF][:]).then_inc(conv, 1)

                def body(l, i, q):
                    convert(q, 0)
                    act.wait_ge(q_ok, q + 1)
                    nc.scalar.activation(qrow[:], qrow[:], ACT.Exp, scale=0.99).then_inc(qexp_ok, 1)
                    for x in range(1, GB):
                        convert(q, x)

                act.sem_inc(conv, NBUF)
                for x in range(GB):
                    act.sem_inc(stored[x], 16)
                nested(act, level_start, body)

            @block.vector
            def _(dve):
                def level_start(l):
                    step = LoopSteps(dve, dve_step, START + l * (AT_LEVEL + NB * IN_BODY))
                    step.now(nc.vector.tensor_scalar(ev[:], dcol[:], low[:, 0:1], REACH, ALU.subtract, ALU.min))
                    step.now(nc.vector.tensor_scalar(fe[:, 0, :], ev[:], -FLAT, None, ALU.max))
                    step.now(nc.vector.tensor_tensor(flat[:], fe[:, 0, :], fe[:, 1, :], ALU.subtract))
                    step(nc.vector.tensor_copy(fe[:, 1, :], fe[:, 0, :]))
                    dve.sem_inc(ev_ok, 1)
                    step.now(nc.vector.tensor_scalar(enough[:], scol[:], low[:, 0:1], STEEP, ALU.add, ALU.is_ge))
                    step(nc.vector.tensor_scalar(enough[:], enough[:], 0.5 * math.exp(0.99 * STEEP), 5e-7, ALU.mult, ALU.max))
                    dve.wait_ge(exp_ok, l + 1)
                    step.now(nc.vector.tensor_tensor(H1[:], H1[:], flat[:].unsqueeze(2).to_broadcast([P, T, D1]), ALU.mult))
                    dve.sem_inc(passed, 1)

                def larger(step, q, u):
                    x, w = u // UPG, u % UPG
                    dve.wait_ge(mult, q * U + u + 1)
                    for j in range(JB):
                        k = w * JB + j
                        ins = nc.vector.tensor_scalar(PT[u % NBUF][:, j, :], qrow[:, x * R:(x + 1) * R], steep[:, k:k + 1],
                                                      1.0, ALU.mult, ALU.max)
                    return step(ins)

                def times_a(q, u, z):
                    dve.wait_ge(turned, q * U + u + 1 + U)
                    dve.wait_ge(dve_step, z)
                    buf = PT[u % NBUF][:].rearrange("p j r -> p (j r)")
                    nc.vector.tensor_tensor(buf, buf, TP[u % NBUF][:], ALU.mult).then_inc(made, 1)

                def finish(step, i, q, x):
                    rows = bass.ds(i * (GB * RT) + x * RT, RT)
                    dve.wait_ge(mult, q * U + (x + 1) * UPG + NBUF)
                    step.now(nc.vector.tensor_copy(res[:], OUT[:, x, :, 0:D1]))
                    dve.sem_inc(fin, 1)
                    step(nc.vector.tensor_scalar(st[:, 1, :], res[:, :, D], 1e-30, None, ALU.max))
                    step.now(nc.vector.tensor_tensor(st[:, 0, :], res[:, :, D], enough[:, rows], ALU.is_gt))
                    step.now(nc.vector.tensor_tensor(st[:, 0, :], st[:, 0, :], todo[:, rows], ALU.mult))
                    step(nc.vector.tensor_tensor(todo[:, rows], todo[:, rows], st[:, 0, :], ALU.subtract))
                    step.now(nc.vector.reciprocal(st[:, 2, :], st[:, 1, :]))
                    step.now(nc.vector.tensor_tensor(st[:, 2, :], st[:, 2, :], st[:, 0, :], ALU.mult))
                    step.now(nc.vector.tensor_tensor(res[:, :, 0:D], res[:, :, 0:D], st[:, 2, :].unsqueeze(2).to_broadcast([P, RT, D]), ALU.mult))
                    step.now(nc.vector.tensor_tensor(prop[:, rows, :], prop[:, rows, :], res[:, :, 0:D], ALU.add))

                def body(l, i, q):
                    step = LoopSteps(dve, dve_step, START + AT_LEVEL + l * (AT_LEVEL + NB * IN_BODY) + i * IN_BODY)
                    step.now(nc.vector.tensor_scalar(qrow[:], srow[:, bass.ds(i * (GB * R), GB * R)], low[:, 0:1], STEEP, ALU.add, ALU.min))
                    dve.sem_inc(q_ok, 1)
                    dve.wait_ge(qexp_ok, q + 1)
                    z = larger(step, q, 0)
                    for u in range(U):
                        nxt = larger(step, q, u + 1) if u + 1 < U else None
                        times_a(q, u, z)
                        z = nxt
                        if u % UPG == LAG + 2 and u > UPG:
                            finish(step, i, q, u // UPG - 1)
                    finish(step, i, q, GB - 1)
                    assert step.n == IN_BODY, step.n

                step = LoopSteps(dve, dve_step)
                nc.vector.memset(PT[0][:, 0, :], 1.0)
                nc.vector.tensor_copy(identB[:], ident[:]).then_inc(start_ok, 1)
                dve.sem_inc(made, NBUF)
                dve.sem_inc(fin, GB)
                nc.vector.memset(fe[:], 0.0)
                step(nc.vector.memset(todo[:], 1.0))
                step.now(nc.vector.memset(prop[:], 0.0))
                dve.wait_ge(sum_ok, 1)
                nc.vector.tensor_scalar(mean[:], OUT[:, 0, 0, 0:D], 1.0 / N, None, ALU.mult).then_inc(mean_ok, 1)

                n = dve.value_load(levels[0:1, 0:1], min_val=1, max_val=MOST_LEVELS)
                with dve.Fori(0, n) as l:
                    level_start(l)
                    with dve.Fori(0, NB) as i:
                        body(l, i, l * NB + i)
                    nc.vector.tensor_scalar(low[:], low[:], -REACH, None, ALU.add).then_inc(low_ok, 1)
                    dve.wait_ge(low_ok, l + 1)
                with dve.Fori(0, T) as t:
                    row = prop[:, bass.ds(t, 1), :].rearrange("p a d -> p (a d)")
                    nc.vector.scalar_tensor_tensor(out=row, in0=mean[:], scalar=todo[:, bass.ds(t, 1)], in1=row, op0=ALU.mult, op1=ALU.add)

            @block.tensor
            def _(pe):
                def turn(q, u):
                    x, w = u // UPG, u % UPG
                    if w % UPC == 0:
                        pe.wait_ge(conv, q * (GB * M) + x * M + (w // UPC + 1) * RT + NBUF)
                    pe.wait_ge(made, q * U + u + 1)
                    for j in range(JB):
                        for t in range(RT):
                            o = (w * JB + j) * P
                            ins = nc.tensor.transpose(TP[u % NBUF][:, (j * RT + t) * P:(j * RT + t + 1) * P], AB[x][:, t, o:o + P], identB[:])
                    ins.then_inc(turned, 1)

                def multiply(q, u):
                    x, w = u // UPG, u % UPG
                    pe.wait_ge(made, q * U + u + 1 + NBUF)
                    if w == 0:
                        pe.wait_ge(fin, q * GB + x + 1)
                    for j in range(JB):
                        for t in range(RT):
                            k = w * JB + j
                            ins = nc.tensor.matmul(OUT[:, x, t, 0:D1], PT[u % NBUF][:, j, t * P:(t + 1) * P], H1[:, k, :],
                                                   start=(k == 0), stop=(k == T - 1))
                    ins.then_inc(mult, 1)

                def body(l, i, q):
                    for u in range(U + LAG):
                        if u < U:
                            turn(q, u)
                        if u >= LAG:
                            multiply(q, u - LAG)

                pe.wait_ge(start_ok, 1)
                for k in range(T):
                    ins = nc.tensor.matmul(OUT[:, 0, 0, 0:D], PT[0][:, 0, 0:P], H1[:, k, 0:D], start=(k == 0), stop=(k == T - 1))
                ins.then_inc(sum_ok, 1)
                pe.wait_ge(mean_ok, 1)
                pe.sem_inc(turned, U)
                pe.sem_inc(mult, NBUF)
                nested(pe, None, body)


def project_l1(nc, X, H, work, row_w, dcol, low, levels, ident, W1, b1, W2, Ww, bw):
    T, D = X.shape[1], X.shape[2]
    G = T // 4
    HID = W1.shape[0]
    with Phase(nc, "pj2") as ph:
        FT = [ph.sbuf(f"FT{k}", [P, 4, D]) for k in range(2)]
        W = ph.sbuf("W", [HID, 2, D])
        wcol = ph.sbuf("wcol", [HID, 1])
        wrep = ph.sbuf("wrep", [HID, P])
        bias = ph.sbuf("bias", [P, 3])
        c12 = ph.sbuf("c12", [D, 2])
        small = ph.sbuf("small", [P, 3, T])
        scol = ph.sbuf("scol", [P, T])
        ext = ph.sbuf("ext", [P, 3])
        ext3 = ph.sbuf("ext3", [3, 1])
        diag = ph.sbuf("diag", [3, 3])
        ones = ph.sbuf("ones", [3, P])
        lev = ph.sbuf("lev", [1, 1])
        PS = ph.psum("ps", [P, 5, BANK])
        w_in, rep_ok, c_ok, c_out, var_ok, sqrt_ok, dve_step, h_ok, t_ok, t_out, d_ok = ph.sems(
            "w_in", "rep_ok", "c_ok", "c_out", "var_ok", "sqrt_ok", "dve_step", "h_ok", "t_ok", "t_out", "d_ok")
        ext_ok, turned_ok, diag_ok, all_ok, u_ok = ph.sems("ext_ok", "turned_ok", "diag_ok", "all_ok", "u_ok")
        with nc.Block() as block:
            @block.sync
            def _(sp):
                sp.dma_start(wcol[:], Ww.rearrange("o h -> h o")).then_inc(w_in, 16)
                sp.dma_start(W[:, 0, :], W1).then_inc(w_in, 16)
                sp.dma_start(W[:, 1, :], W2).then_inc(w_in, 16)
                sp.dma_start(bias[:, 0:1], b1.rearrange("(h o) -> h o", o=1)).then_inc(w_in, 16)
                sp.dma_start(bias[:, 1:2], bw.rearrange("(o c) -> o c", o=1).to_broadcast([P, 1])).then_inc(w_in, 16)

            @block.vector
            def _(dve):
                step = Chain(dve, dve_step)
                dve.wait_ge(w_in, 80)
                nc.vector.tensor_copy(wrep[:], wcol[:].to_broadcast([HID, P])).then_inc(rep_ok, 1)
                dve.wait_ge(c_ok, 1)
                nc.vector.tensor_tensor(bias[:, 2:3], PS[:, 3, 2:3], bias[:, 1:2], ALU.add)
                nc.vector.tensor_copy(c12[:], PS[:, 3, 0:2]).then_inc(c_out, 1)
                norm_rows(nc, dve, step, X, H, work, small, var_ok, sqrt_ok, D)
                dve.sem_inc(h_ok, 1)
                for g in range(G):
                    dve.wait_ge(t_ok, g + 1)
                    if g >= 2:
                        dve.wait_ge(d_ok, g - 1)
                    nc.vector.tensor_copy(FT[g % 2][:], PS[:, g % 2, :].rearrange("p (t d) -> p t d", d=D)).then_inc(t_out, 1)
                dve.wait_ge(d_ok, G)
                both = PS[:, 2, 0:2 * T].rearrange("p (t k) -> p t k", k=2)
                step(nc.vector.tensor_scalar(scol[:], both[:, :, 0], bias[:, 2:3], None, ALU.add))
                step(nc.vector.tensor_copy(dcol[:], both[:, :, 1]))
                step(nc.vector.tensor_reduce(ext[:, 0:1], dcol[:], AX.X, ALU.max))
                step(nc.vector.tensor_reduce(ext[:, 1:2], dcol[:], AX.X, ALU.min))
                step(nc.vector.tensor_scalar(ext[:, 1:2], ext[:, 1:2], -1.0, None, ALU.mult))
                step(nc.vector.tensor_reduce(ext[:, 2:3], scol[:], AX.X, ALU.max))
                step(nc.vector.memset(ones[:], 1.0))
                dve.sem_inc(ext_ok, 1)
                dve.wait_ge(turned_ok, 1)
                step(nc.vector.tensor_reduce(ext3[:], PS[0:3, 4, 0:P], AX.X, ALU.max))
                nc.vector.tensor_scalar(diag[:], ident[0:3, 0:3], ext3[:], None, ALU.mult).then_inc(diag_ok, 1)
                dve.wait_ge(all_ok, 1)
                step(nc.vector.tensor_copy(ext[:], PS[:, 3, 4:7]))
                step(nc.vector.tensor_scalar(low[:], ext[:, 0:1], -LEVEL, None, ALU.add))
                step(nc.vector.tensor_tensor(lev[:], ext[0:1, 0:1], ext[0:1, 1:2], ALU.add))
                step(nc.vector.tensor_scalar(lev[:], lev[:], 1.0, 1.0 / LEVEL, ALU.add, ALU.mult))
                step(nc.vector.tensor_scalar(lev[:], lev[:], 1.0, float(MOST_LEVELS), ALU.add, ALU.min))
                step(nc.vector.tensor_copy(levels[:], lev[:]))
                step(nc.vector.tensor_scalar(row_w[:], scol[:], ext[:, 2:3], -LEVEL, ALU.subtract, ALU.max))
                dve.sem_inc(u_ok, 1)

            @block.scalar
            def _(act):
                act.wait_ge(var_ok, 1)
                nc.scalar.activation(small[:, 1, :], small[:, 2, :], ACT.Sqrt).then_inc(sqrt_ok, 1)
                act.wait_ge(u_ok, 1)
                nc.scalar.activation(row_w[:], row_w[:], ACT.Exp)

            @block.tensor
            def _(pe):
                pe.wait_ge(rep_ok, 1)
                for k in range(2):
                    nc.tensor.matmul(PS[:, 3, k:k + 1], W[:, k, :], wcol[:], start=True, stop=True)
                nc.tensor.matmul(PS[:, 3, 2:3], wrep[:], bias[:, 0:1], start=True, stop=True).then_inc(c_ok, 1)
                pe.wait_ge(c_out, 1)
                pe.wait_ge(h_ok, 1)
                for g in range(G + 1):
                    if g < G:
                        if g >= 2:
                            pe.wait_ge(t_out, g - 1)
                        for k in range(4):
                            ins = nc.tensor.transpose(PS[:, g % 2, k * P:(k + 1) * P], H[:, 4 * g + k, :], ident[:])
                        ins.then_inc(t_ok, 1)
                    if g:
                        m = g - 1
                        pe.wait_ge(t_out, m + 1)
                        for t in range(4 * m, 4 * m + 4):
                            ins = nc.tensor.matmul(PS[:, 2, 2 * t:2 * t + 2], FT[m % 2][:, t % 4, :], c12[:], start=True, stop=True)
                        ins.then_inc(d_ok, 1)
                pe.wait_ge(ext_ok, 1)
                nc.tensor.transpose(PS[0:3, 4, 0:P], ext[:], ident[:]).then_inc(turned_ok, 1)
                pe.wait_ge(diag_ok, 1)
                nc.tensor.matmul(PS[:, 3, 4:7], ones[:], diag[:], start=True, stop=True).then_inc(all_ok, 1)


def attend_levels(nc, adj01, F, row_w, dcol, low, levels, prop, anyrow, ident):
    T, D = F.shape[1], F.shape[2]
    N = T * P
    D1 = D + 1
    QT = 4
    UB = 8
    UPT = T // UB
    U = QT * UPT
    NQ = T // QT
    LAG = 3
    HQ = T // 4
    NTP, NAT = 4, 4
    with Phase(nc, "at1") as ph:
        MB = [ph.sbuf(f"a{b}", [P, N], BF16) for b in range(2)]
        AT = [ph.sbuf(f"at{b}", [P, UB * P], BF16) for b in range(NAT)]
        parts = ph.sbuf("parts", [P, T, 3, D1], BF16)
        left = [ph.sbuf(f"left{b}", [P, HQ, D1]) for b in range(2)]
        ev = ph.sbuf("ev", [P, T])
        todo = ph.sbuf("todo", [P, T])
        res = ph.sbuf("res", [P, 2, D1])
        st = ph.sbuf("st", [P, 4])
        identB = ph.sbuf("identB", [P, P], BF16)
        TP = [ph.psum(f"tp{b}", [P, UB * P], BF16) for b in range(NTP)]
        OUT = ph.psum("out", [P, QT, BANK])
        id_ok, turned, mult, fin, dve_step, ev_ok, exp_ok, left_ok, part_ok, split_ok, passed = ph.sems(
            "id_ok", "turned", "mult", "fin", "dve_step", "ev_ok", "exp_ok", "left_ok", "part_ok", "split_ok", "passed")
        copied = [ph.sem("copied_act"), ph.sem("copied_dve")]
        in_b = [ph.sem(f"in{b}") for b in range(2)]
        adj_t = adj01.rearrange("(t p) c -> t p c", p=P)
        START = 2
        AT_LEVEL, IN_BODY = 2 + 4 * 4, QT * 8

        def nested(eng, level_start, body):
            n = eng.value_load(levels[0:1, 0:1], min_val=1, max_val=MOST_LEVELS)
            with eng.Fori(0, n) as l:
                if level_start is not None:
                    level_start(l)
                with eng.Fori(0, NQ) as i:
                    body(l, i, l * NQ + i)

        with nc.Block() as block:
            @block.sync
            def _(sp):
                def body(l, i, q):
                    for x in range(QT):
                        sp.wait_ge(turned, q * U + UPT * (x + 1))
                        sp.sem_inc(passed, 1)
                        sp.dma_start(MB[x % 2][:], adj_t[QT * i + x]).then_inc(in_b[x % 2], 16)

                nested(sp, None, body)

            @block.tensor
            def _(pe):
                def turn(q, u):
                    x = u // UPT
                    if u % UPT == 0:
                        pe.wait_ge(in_b[x % 2], q * (16 * QT // 2) + 16 * (x // 2 + 1))
                    pe.wait_ge(copied[u % 2], q * (U // 2) + u // 2 + 1)
                    for b in range(UB):
                        o = ((u % UPT) * UB + b) * P
                        ins = nc.tensor.transpose(TP[u % NTP][:, b * P:(b + 1) * P], MB[x % 2][:, o:o + P], identB[:])
                    ins.then_inc(turned, 1)

                def multiply(q, u):
                    x = u // UPT
                    pe.wait_ge(copied[u % 2], q * (U // 2) + u // 2 + 3)
                    if u % UPT == 0:
                        pe.wait_ge(fin, q * QT + x + 1)
                    for b in range(UB):
                        k = (u % UPT) * UB + b
                        ins = nc.tensor.matmul(OUT[:, x, 0:3 * D1], AT[u % NAT][:, b * P:(b + 1) * P],
                                               parts[:, k].rearrange("p k d -> p (k d)"), start=(k == 0), stop=(k == T - 1))
                    ins.then_inc(mult, 1)

                def body(l, i, q):
                    for u in range(U + LAG):
                        if u < U:
                            turn(q, u)
                        if u >= LAG:
                            multiply(q, u - LAG)

                pe.wait_ge(id_ok, 1)
                pe.sem_inc(turned, 2 * UPT)
                pe.sem_inc(mult, NAT)
                nested(pe, lambda l: (pe.wait_ge(split_ok, l + 1), pe.sem_inc(passed, 1)), body)

            def copy_out(eng, q, u, copy):
                eng.wait_ge(turned, q * U + u + 1 + 2 * UPT)
                eng.wait_ge(mult, q * U + u + 1)
                copy(AT[u % NAT][:], TP[u % NTP][:]).then_inc(copied[u % 2], 1)

            @block.scalar
            def _(act):
                def level_start(l):
                    act.wait_ge(ev_ok, l + 1)
                    nc.scalar.activation(ev[:], ev[:], ACT.Exp).then_inc(exp_ok, 1)
                    for h in range(4):
                        for k in range(2):
                            act.wait_ge(left_ok, l * 8 + 2 * h + k + 1)
                            nc.scalar.activation(parts[:, h * HQ:(h + 1) * HQ, k, :], left[h % 2][:], ACT.Copy).then_inc(part_ok, 1)

                def body(l, i, q):
                    for u in range(0, U, 2):
                        copy_out(act, q, u, nc.scalar.copy)

                act.sem_inc(copied[0], 2)
                nested(act, level_start, body)

            @block.vector
            def _(dve):
                def level_start(l):
                    step = LoopSteps(dve, dve_step, START + l * (AT_LEVEL + NQ * IN_BODY))
                    step.now(nc.vector.tensor_scalar(ev[:], dcol[:], low[:, 0:1], LEVEL, ALU.subtract, ALU.min))
                    step.now(nc.vector.tensor_scalar(low[:], low[:], -LEVEL, None, ALU.add))
                    dve.sem_inc(ev_ok, 1)
                    dve.wait_ge(exp_ok, l + 1)
                    for h in range(4):
                        ts = slice(h * HQ, (h + 1) * HQ)
                        e = ev[:, ts]
                        step(nc.vector.tensor_copy(left[h % 2][:, :, D], e))
                        step.now(nc.vector.tensor_tensor(left[h % 2][:, :, 0:D], F[:, ts, :], e.unsqueeze(2).to_broadcast([P, HQ, D]), ALU.mult))
                        for k in range(2):
                            dve.sem_inc(left_ok, 1)
                            dve.wait_ge(part_ok, l * 8 + 2 * h + k + 1)
                            step.now(nc.vector.tensor_tensor(left[h % 2][:], left[h % 2][:], parts[:, ts, k, :], ALU.subtract))
                        ins = nc.vector.tensor_copy(parts[:, ts, 2, :], left[h % 2][:])
                    ins.then_inc(split_ok, 1)

                def finish(step, l, i, q, x):
                    t = bass.ds(QT * i + x, 1)
                    dve.wait_ge(mult, q * U + UPT * (x + 1) + NAT)
                    step.now(nc.vector.tensor_copy(res[:, 0, :], OUT[:, x, 2 * D1:3 * D1]))
                    step.now(nc.vector.tensor_tensor(res[:, 0, :], res[:, 0, :], OUT[:, x, D1:2 * D1], ALU.add))
                    step.now(nc.vector.tensor_tensor(res[:, 1, :], res[:, 0, :], OUT[:, x, 0:D1], ALU.add))
                    dve.sem_inc(fin, 1)
                    total = res[:, 1, D:D1]
                    step(nc.vector.scalar_tensor_tensor(out=st[:, 0:1], in0=total, scalar=0.5, in1=todo[:, t], op0=ALU.is_gt, op1=ALU.mult))
                    step.now(nc.vector.tensor_scalar(st[:, 1:2], total, row_w[:, t], 1e-37, ALU.mult, ALU.max))
                    step.now(nc.vector.reciprocal(st[:, 2:3], st[:, 1:2]))
                    step.now(nc.vector.scalar_tensor_tensor(out=st[:, 3:4], in0=st[:, 2:3], scalar=row_w[:, t], in1=st[:, 0:1], op0=ALU.mult, op1=ALU.mult))
                    nc.vector.tensor_tensor(todo[:, t], todo[:, t], st[:, 0:1], ALU.subtract)
                    row = prop[:, t, :].rearrange("p a d -> p (a d)")
                    step.now(nc.vector.scalar_tensor_tensor(out=row, in0=res[:, 1, 0:D], scalar=st[:, 3:4], in1=row, op0=ALU.mult, op1=ALU.add))

                def body(l, i, q):
                    step = LoopSteps(dve, dve_step, START + AT_LEVEL + l * (AT_LEVEL + NQ * IN_BODY) + i * IN_BODY)
                    for u in range(1, U, 2):
                        copy_out(dve, q, u, nc.vector.tensor_copy)
                        if u % UPT == LAG + 2 and u > UPT:
                            finish(step, l, i, q, u // UPT - 1)
                    finish(step, l, i, q, QT - 1)
                    assert step.n == IN_BODY, step.n

                nc.vector.tensor_copy(identB[:], ident[:]).then_inc(id_ok, 1)
                dve.sem_inc(copied[1], 2)
                dve.sem_inc(fin, QT)
                step = LoopSteps(dve, dve_step)
                step(nc.vector.memset(todo[:], 1.0))
                step.now(nc.vector.memset(prop[:], 0.0))
                nested(dve, level_start, body)
                nc.vector.tensor_scalar(anyrow[:], todo[:], -1.0, 1.0, ALU.mult, ALU.add)


def route_l1(nc, ident, X, F, anyrow, router_w, w1, w2, w3, XT, G, up, gate, down):
    T, D = X.shape[1], X.shape[2]
    GR = T // 4
    NE, HID = w1.shape[0], w1.shape[1]
    parts = hidden_parts(HID)
    K = len(parts)
    with Phase(nc, "rt") as ph:
        PR = XT
        W13 = [ph.sbuf(f"W13_{k}", [P, NE, K, D]) for k in range(2)]
        W2 = ph.sbuf("W2", [P, NE, HID])
        rw = ph.sbuf("rw", [NE, D])
        rwT = ph.sbuf("rwT", [D, NE])
        small = ph.sbuf("small", [P, 3, T])
        prob = ph.sbuf("prob", [P, T, NE])
        left = ph.sbuf("left", [P, T, NE])
        sel = [ph.sbuf(f"sel{k}", [P, T, NE]) for k in range(2)]
        best = ph.sbuf("best", [P, 2, T])
        free = ph.sbuf("free", [P, T])
        PS = ph.psum("ps", [P, 7, BANK])
        w_in, var_ok, sqrt_ok, dve_step, y_ok, t_ok, t_out, l_ok, ex_ok, exp_ok = ph.sems(
            "w_in", "var_ok", "sqrt_ok", "dve_step", "y_ok", "t_ok", "t_out", "l_ok", "ex_ok", "exp_ok")
        r_ok, r_out, turned, up_out, gate_out, down_out = ph.sems("r_ok", "r_out", "turned", "up_out", "gate_out", "down_out")
        n_w = 2 + 2 * K
        with nc.Block() as block:
            @block.sync
            def _(sp):
                sp.dma_start(rw[:], router_w).then_inc(w_in, 16)
                for dst, w in ((W13[0], w1), (W13[1], w3)):
                    for k, (o, n) in enumerate(parts):
                        sp.dma_start(dst[0:n, :, k, :], w[:, o:o + n, :].rearrange("e h c -> h e c")).then_inc(w_in, 16)
                sp.dma_start(W2[:], w2.rearrange("e c h -> c e h")).then_inc(w_in, 16)

            @block.tensor
            def _(pe):
                pe.wait_ge(w_in, 16 * n_w)
                nc.tensor.transpose(PS[:, 6, 0:NE], rw[:], ident[0:NE, 0:NE]).then_inc(r_ok, 1)
                for e in range(NE):
                    if e:
                        pe.wait_ge(up_out, e)
                        pe.wait_ge(gate_out, e)
                        pe.wait_ge(down_out, e)
                    for s in range(2):
                        for k, (o, n) in enumerate(parts):
                            nc.tensor.transpose(PS[:, 2 + s, o:o + n], W13[s][0:n, e, k, :], ident[0:n, 0:n])
                    for k, (o, n) in enumerate(parts):
                        ins = nc.tensor.transpose(PS[0:n, 4, k * D:(k + 1) * D], W2[:, e, o:o + n], ident[:])
                    ins.then_inc(turned, 1)
                pe.wait_ge(y_ok, 1)
                pe.wait_ge(r_out, 1)
                for g in range(GR + 1):
                    if g < GR:
                        if g >= 2:
                            pe.wait_ge(t_out, g - 1)
                        for k in range(4):
                            ins = nc.tensor.transpose(PS[:, g % 2, k * P:(k + 1) * P], F[:, 4 * g + k, :], ident[:])
                        ins.then_inc(t_ok, 1)
                    if g:
                        pe.wait_ge(t_out, g)
                        for t in range(4 * g - 4, 4 * g):
                            ins = nc.tensor.matmul(PS[:, 5, t * NE:(t + 1) * NE], XT[:, t, :], rwT[:], start=True, stop=True)
                ins.then_inc(l_ok, 1)

            @block.scalar
            def _(act):
                act.wait_ge(r_ok, 1)
                nc.scalar.copy(rwT[:], PS[:, 6, 0:NE]).then_inc(r_out, 1)
                for e in range(NE):
                    act.wait_ge(turned, e + 1)
                    nc.scalar.copy(up[:, e, :], PS[:, 2, 0:HID]).then_inc(up_out, 1)
                    nc.scalar.copy(gate[:, e, :], PS[:, 3, 0:HID]).then_inc(gate_out, 1)
                    for k, (o, n) in enumerate(parts):
                        ins = nc.scalar.copy(down[0:n, e, k, :], PS[0:n, 4, k * D:(k + 1) * D])
                    ins.then_inc(down_out, 1)
                act.wait_ge(var_ok, 1)
                nc.scalar.activation(small[:, 1, :], small[:, 2, :], ACT.Sqrt).then_inc(sqrt_ok, 1)
                for g in range(GR):
                    act.wait_ge(t_ok, g + 1)
                    nc.scalar.copy(XT[:, 4 * g:4 * g + 4, :], PS[:, g % 2, :].rearrange("p (t d) -> p t d", d=D)).then_inc(t_out, 1)
                act.wait_ge(ex_ok, 1)
                nc.scalar.activation(prob[:], prob[:], ACT.Exp).then_inc(exp_ok, 1)

            @block.vector
            def _(dve):
                step = Chain(dve, dve_step)

                def over(x, n):
                    return x.unsqueeze(2).to_broadcast([P, T, n])

                step(nc.vector.tensor_tensor(PR[:], PR[:], F[:], ALU.subtract))
                step(nc.vector.tensor_tensor(PR[:], PR[:], over(anyrow[:], D), ALU.mult))
                step(nc.vector.scalar_tensor_tensor(out=PR[:], in0=F[:], scalar=2.0, in1=PR[:], op0=ALU.mult, op1=ALU.add))
                step(nc.vector.scalar_tensor_tensor(out=X[:], in0=PR[:], scalar=0.5, in1=X[:], op0=ALU.mult, op1=ALU.add))
                norm_rows(nc, dve, step, X, F, PR[:], small, var_ok, sqrt_ok, D)
                dve.sem_inc(y_ok, 1)
                dve.wait_ge(l_ok, 1)
                logits = PS[:, 5, 0:T * NE].rearrange("p (t e) -> p t e", e=NE)
                step(nc.vector.tensor_reduce(free[:], logits, AX.X, ALU.max))
                step(nc.vector.tensor_tensor(prob[:], logits, over(free[:], NE), ALU.subtract))
                dve.sem_inc(ex_ok, 1)
                dve.wait_ge(exp_ok, 1)
                step(nc.vector.tensor_reduce(free[:], prob[:], AX.X, ALU.add))
                step(nc.vector.reciprocal(free[:], free[:]))
                step(nc.vector.tensor_tensor(prob[:], prob[:], over(free[:], NE), ALU.mult))
                top_two(nc, step, prob[:], left[:], [sel[0][:], sel[1][:]], best, free[:])
                step(nc.vector.tensor_tensor(free[:], best[:, 0, :], best[:, 1, :], ALU.add))
                step(nc.vector.tensor_scalar(free[:], free[:], 1e-9, None, ALU.add))
                step(nc.vector.reciprocal(free[:], free[:]))
                for k in range(2):
                    step(nc.vector.tensor_tensor(best[:, k, :], best[:, k, :], free[:], ALU.mult))
                    step(nc.vector.tensor_tensor(sel[k][:], sel[k][:], over(best[:, k, :], NE), ALU.mult))
                step(nc.vector.tensor_tensor(G[:], sel[0][:], sel[1][:], ALU.add))


def hidden_parts(hidden):
    return [(o, min(P, hidden - o)) for o in range(0, hidden, P)]


def experts(nc, tag, X, XT, G, hidden, up, down, gate=None, b1=None, b2=None, gates=None, out=None):
    T, D = X.shape[1], X.shape[2]
    GT = BANK // P
    NG = T // GT
    NE = G.shape[2]
    parts = hidden_parts(hidden)
    K = len(parts)
    U = NE * K
    assert NE % 2 == 0 and U % 2 == 0
    with Phase(nc, tag) as ph:
        HH = [[ph.sbuf(f"HH{b}_{k}", [P, BANK]) for k in range(K)] for b in range(2)]
        SL = [ph.sbuf(f"SL{b}", [P, BANK]) for b in range(2)] if gate is not None else None
        b2row = ph.sbuf("b2row", [1, NE, D]) if b2 is not None else None
        b1col = ph.sbuf("b1col", [P, NE, K]) if b1 is not None else None
        one = ph.sbuf("one", [1, P]) if b2 is not None else None
        HP = ph.psum("hp", [P, 2, 2, BANK])
        YP = ph.psum("yp", [P, 2, BANK])
        in_ok, one_ok, h_ok, silu_ok, hid_ok, y_ok, y_used, x_out = ph.sems(
            "in_ok", "one_ok", "h_ok", "silu_ok", "hid_ok", "y_ok", "y_used", "x_out")
        gates_in = ph.sem("gates_in")
        n_in = 0 if gate is not None else NE * K + 1
        with nc.Block() as block:
            @block.sync
            def _(sp):
                if gate is None:
                    sp.dma_start(b2row[:], b2.rearrange("(o e) d -> o e d", o=1)).then_inc(in_ok, 16)
                    for e in range(NE):
                        for k, (o, n) in enumerate(parts):
                            sp.dma_start(b1col[0:n, e, k:k + 1], b1[e, o:o + n].rearrange("(h o) -> h o", o=1)).then_inc(in_ok, 16)
                if out is not None:
                    ov = out.rearrange("(t p) d -> p t d", p=P)
                    for g in range(NG):
                        sp.wait_ge(y_used, (g + 1) * NE)
                        sp.dma_start(ov[:, g * GT:(g + 1) * GT, :], X[:, g * GT:(g + 1) * GT, :]).then_inc(x_out, 16)
                    sp.wait_ge(x_out, 16 * NG)

            @block.tensor
            def _(pe):
                def hidden_part(g, e, k):
                    u = e * K + k
                    o, n = parts[k]
                    if not isinstance(g, int) or u >= 2:
                        pe.wait_ge(hid_ok, g * U + u - 1)
                    for s, w in enumerate([up] if gate is None else [up, gate]):
                        ins = nc.tensor.matmul(HP[0:n, u % 2, s, :], w[:, e, o:o + n], XT[:, bass.ds(g * GT, GT), :], start=True, stop=True)
                    ins.then_inc(h_ok, 1)

                def output(g, e, peeled):
                    pe.wait_ge(hid_ok, (g * NE + e + 1) * K)
                    if not peeled or e >= 2:
                        pe.wait_ge(y_used, g * NE + e - 1)
                    for q in range(GT):
                        for k, (o, n) in enumerate(parts):
                            ins = nc.tensor.matmul(YP[:, e % 2, q * D:(q + 1) * D], HH[e % 2][k][0:n, q * P:(q + 1) * P],
                                                   down[0:n, e % NE, k, :], start=(k == 0), stop=(k == K - 1 and b2 is None))
                        if b2 is not None:
                            ins = nc.tensor.matmul(YP[:, e % 2, q * D:(q + 1) * D], one[:], b2row[:, e % NE, :], start=False, stop=True)
                    ins.then_inc(y_ok, 1)

                def group(g, peeled):
                    for e in range(NE):
                        for k in range(K):
                            hidden_part(g, e, k)
                        if e or not peeled:
                            output(g, e - 1, peeled)

                if gate is None:
                    pe.wait_ge(in_ok, 16 * n_in)
                    pe.wait_ge(one_ok, 1)
                group(0, True)
                with pe.Fori(1, NG) as g:
                    group(g, False)
                output(NG, -1, False)

            @block.scalar
            def _(act):
                if gate is None:
                    act.dma_start(G[:], gates.rearrange("(t p) e -> p t e", p=P)).then_inc(gates_in, 16)
                    act.wait_ge(in_ok, 16 * n_in)
                with act.Fori(0, NG) as g:
                    for e in range(NE):
                        for k, (o, n) in enumerate(parts):
                            u = e * K + k
                            act.wait_ge(h_ok, g * U + u + 1)
                            if gate is None:
                                nc.scalar.activation(HH[e % 2][k][0:n, :], HP[0:n, u % 2, 0, :], ACT.Gelu,
                                                     bias=b1col[0:n, e, k:k + 1]).then_inc(hid_ok, 1)
                            else:
                                nc.scalar.activation(SL[u % 2][0:n, :], HP[0:n, u % 2, 0, :], ACT.Silu).then_inc(silu_ok, 1)

            @block.vector
            def _(dve):
                def gated(g, e, k):
                    u = e * K + k
                    o, n = parts[k]
                    dve.wait_ge(silu_ok, g * U + u + 1)
                    nc.vector.tensor_tensor(HH[e % 2][k][0:n, :], SL[u % 2][0:n, :], HP[0:n, u % 2, 1, :], ALU.mult).then_inc(hid_ok, 1)

                def add(g, e, gx, ex):
                    dve.wait_ge(y_ok, g * NE + e + 1)
                    if not isinstance(g, int) or e:
                        dve.wait_ge(y_used, g * NE + e)
                    for q in range(GT):
                        t = bass.ds(gx * GT + q, 1)
                        xt = X[:, t, :].rearrange("p a d -> p (a d)")
                        ins = nc.vector.scalar_tensor_tensor(out=xt, in0=YP[:, ex % 2, q * D:(q + 1) * D],
                                                             scalar=G[:, t, ex:ex + 1].rearrange("p a e -> p (a e)"), in1=xt, op0=ALU.mult, op1=ALU.add)
                    ins.then_inc(y_used, 1)

                def group(g, peeled):
                    for e in range(NE):
                        if gate is not None:
                            for k in range(K):
                                gated(g, e, k)
                        if e or not peeled:
                            add(g, e - 1, g - (e == 0), (e - 1) % NE)

                if gate is None:
                    nc.vector.memset(one[:], 1.0).then_inc(one_ok, 1)
                    dve.wait_ge(gates_in, 16)
                group(0, True)
                with dve.Fori(1, NG) as g:
                    group(g, False)
                add(NG, -1, NG - 1, NE - 1)


def set_ones(nc, where):
    with Phase(nc, "ones") as ph:
        done = ph.sem("done")
        with nc.Block() as block:
            @block.vector
            def _(dve):
                nc.vector.memset(where, 1.0).then_inc(done, 1)
                dve.wait_ge(done, 1)


def load_experts_l0(nc, W1, W2, up, down):
    with Phase(nc, "lw0") as ph:
        w_in = ph.sem("w_in")
        parts = hidden_parts(W1.shape[2])
        with nc.Block() as block:
            @block.sync
            def _(sp):
                sp.dma_start(up[:], W1.rearrange("e c h -> c e h")).then_inc(w_in, 16)
                for k, (o, n) in enumerate(parts):
                    sp.dma_start(down[0:n, :, k, :], W2[:, o:o + n, :].rearrange("e h c -> h e c")).then_inc(w_in, 16)
                sp.wait_ge(w_in, 16 * (1 + len(parts)))


def graph_network(nc, x, adj, L0_gnn_W, L0_gnn_a, L0_ffn_W_gat, L0_ffn_att_src, L0_ffn_att_dst, L0_ffn_b_gat,
                  L0_ffn_ln_gamma, L0_ffn_ln_beta, L0_ffn_W1, L0_ffn_b1, L0_ffn_W2, L0_ffn_b2, L0_ffn_edge_index,
                  L1_gnn_W1, L1_gnn_b1, L1_gnn_W2, L1_gnn_Ww, L1_gnn_bw, L1_ffn_router_w, L1_ffn_w1, L1_ffn_w2, L1_ffn_w3,
                  out):
    N, D = x.shape
    T = N // P
    NE0, NE1 = L0_ffn_W1.shape[0], L1_ffn_w1.shape[0]
    HID0, HID1 = L0_ffn_W1.shape[2], L1_ffn_w1.shape[1]
    NH, HE = L0_ffn_att_src.shape[0], L0_ffn_b_gat.shape[0]
    CHUNK = 128
    LMAX = (-(-(L0_ffn_edge_index.shape[1] + N) // (P * CHUNK)) + 1) * CHUNK

    def dram(name, shape, dtype=F32):
        return nc.dram_tensor(name, shape, dtype).ap()

    adj01 = dram("adj01", (N, N), BF16)
    rec = dram("rec", (P * LMAX, 2), I32)
    plan = dram("plan", (P, L0_ffn_edge_index.shape[1] // P + 16, 3), I32)
    tab = dram("tab", (N, HE + 2 * NH))
    runs = dram("runs", (P * LMAX, 2 * NH + HE))
    carry = dram("carry", (P, 2 * (NH + HE)))
    gates0 = dram("gates0", (N, NE0))
    with Phase(nc, "top") as top:
        ident = top.sbuf("ident", [P, P])
        ctl = top.sbuf("ctl", [1, 3], I32)
        endi = top.sbuf("endi", [P, T], I32)
        endq = top.sbuf("endq", [P, T], I32)
        cont = top.sbuf("cont", [P, T])
        make_identity(nc, ident)
        self_idx = top.sbuf("self_idx", [P, T], I32)
        self_rec = top.sbuf("self_rec", [P, T, 2], I32)
        sort_edges(nc, ident, L0_ffn_edge_index, N, rec, plan, self_idx, self_rec, ctl, endi, endq, cont)
        X = top.sbuf("X", [P, T, D])
        with Phase(nc, "g0") as ph:
            H1 = ph.sbuf("H", [P, T, D + 1])
            srow = ph.sbuf("srow", [P, N])
            scol = ph.sbuf("scol", [P, T])
            dcol = ph.sbuf("dcol", [P, T])
            low = ph.sbuf("low", [P, 1])
            levels = ph.sbuf("levels", [1, 1], I32)
            project_l0(nc, ident, x, L0_gnn_W, L0_gnn_a, H1[:, :, 0:D], X[:], srow, scol, dcol, low, levels)
            set_ones(nc, H1[:, :, D])
            attend_leaky(nc, adj, adj01, H1, srow, scol, dcol, low, levels, X, ident,
                         beside=lambda pool, at: scatter_records(nc, pool, at, rec, plan, self_idx, self_rec, ctl))

        with Phase(nc, "f0") as ph:
            XT = ph.sbuf("XT", [P, T, D])
            project_edges(nc, ident, x, X, L0_ffn_W_gat, L0_ffn_att_src, L0_ffn_att_dst, XT, tab)
            gate_nodes(nc, ident, rec, tab, runs, carry, ctl, endi, endq, cont, L0_ffn_b_gat, L0_ffn_ln_gamma,
                       L0_ffn_ln_beta, gates0)
            G = ph.sbuf("G", [P, T, NE0])
            up = ph.sbuf("up", [P, NE0, HID0])
            down = ph.sbuf("down", [P, NE0, len(hidden_parts(HID0)), D])
            load_experts_l0(nc, L0_ffn_W1, L0_ffn_W2, up, down)
            experts(nc, "ex0", X, XT, G, HID0, up, down, b1=L0_ffn_b1, b2=L0_ffn_b2, gates=gates0)

        F = top.sbuf("F", [P, T, D])
        anyrow = top.sbuf("anyrow", [P, T])
        XT = top.sbuf("XT", [P, T, D])
        with Phase(nc, "g1") as ph:
            row_w = ph.sbuf("row_w", [P, T])
            dcol = ph.sbuf("dcol", [P, T])
            low = ph.sbuf("low", [P, 1])
            levels = ph.sbuf("levels", [1, 1], I32)
            project_l1(nc, X, F, XT[:], row_w, dcol, low, levels, ident, L1_gnn_W1, L1_gnn_b1, L1_gnn_W2, L1_gnn_Ww, L1_gnn_bw)
            attend_levels(nc, adj01, F, row_w, dcol, low, levels, XT, anyrow, ident)

        G = top.sbuf("G", [P, T, NE1])
        up = top.sbuf("up", [P, NE1, HID1])
        gate = top.sbuf("gate", [P, NE1, HID1])
        down = top.sbuf("down", [P, NE1, len(hidden_parts(HID1)), D])
        route_l1(nc, ident, X, F, anyrow, L1_ffn_router_w, L1_ffn_w1, L1_ffn_w2, L1_ffn_w3, XT, G, up, gate, down)
        experts(nc, "ex1", X, XT, G, HID1, up, down, gate=gate, out=out)


def kernel(**inputs):
    import numpy as np
    import concourse.bacc as _bacc
    from concourse import mybir as _mybir
    from concourse.bass_utils import run_bass_kernel_spmd as _run

    nc = _bacc.Bacc("TRN2", target_bir_lowering=False, num_devices=1)
    arrays, args = {}, {}
    for name, value in inputs.items():
        a = np.ascontiguousarray(np.asarray(value))
        arrays[f"in_{name}_dram"] = a
        args[name] = nc.dram_tensor(f"in_{name}_dram", a.shape, _mybir.dt.from_np(a.dtype), kind="ExternalInput").ap()
    out = nc.dram_tensor("out_0_dram", inputs["x"].shape, F32, kind="ExternalOutput").ap()
    graph_network(nc, out=out, **args)
    r = _run(nc, [arrays], core_ids=[0])
    return np.asarray(r.results[0]["out_0_dram"])
```
